# Optimizing a Trainium2 kernel written in Bass

```python
import numpy as np
import jax
import jax.numpy as jnp

def _softmax(x, axis=-1):
    return jax.nn.softmax(x, axis=axis)

def _gelu(x):
    return jax.nn.gelu(x, approximate=True)

def _silu(x):
    return jax.nn.silu(x)

def _sigmoid(x):
    return jax.nn.sigmoid(x)

def _layernorm(x, axis=-1, eps=1e-05):
    m = jnp.mean(x, axis=axis, keepdims=True)
    v = jnp.var(x, axis=axis, keepdims=True)
    return (x - m) / jnp.sqrt(v + eps)

def _scatter_add(tgt, idx, src, axis=0):
    return tgt.at[idx].add(src)

def _segment_sum(src, seg, n):
    return jax.ops.segment_sum(src, seg, n)
kernel_name = 'mk_adj_preln_d4_adj_r2_51854b'

def setup_inputs(seed: int=0):
    np.random.seed(seed)
    _w = jnp.asarray

    def _rec_inputs():
        import jax
        import jax.numpy as jnp
        _gk = jax.random.key(seed)
        x = -0.0005207 + 1.001 * jax.random.normal(jax.random.fold_in(_gk, 1), (8, 1024, 128), jnp.float32)
        _w = (1.0 + jnp.arange(1024, dtype=jnp.float32)) ** (-0.5)
        _w = _w / _w.mean()
        _pij = jnp.clip(0.0078125 * _w[:, None] * _w[None, :], 0.0, 1.0)
        _a = jax.random.uniform(jax.random.fold_in(_gk, 2), (8, 1024, 1024)) < _pij
        _a = jnp.logical_or(_a, jnp.swapaxes(_a, -1, -2))
        _a = jnp.logical_or(_a, jnp.eye(1024, dtype=bool))
        _af = _a.astype(jnp.float32)
        _af = _af * jax.random.uniform(jax.random.fold_in(_gk, 3), (8, 1024, 1024), jnp.float32, 0.05, 1)
        adj = _af
        _nm = jnp.ones((8, 1024), dtype=bool)
        nodemask = jnp.where(_nm, 1.0, 0.0).astype(jnp.int32)
        return (x, adj, nodemask)
    x, adj, nodemask = _rec_inputs()

    def _L0_gnn_setup():
        import jax, jax.numpy as jnp
        import numpy as np
        C = 128
        key = jax.random.key(seed)
        k_h, k_A, k_Ww, k_Wb, k_aw, k_ab = jax.random.split(key, 6)
        B, N = (8, 1024)
        h = jax.random.normal(k_h, (B, N, C), dtype=jnp.float32)
        A = jax.random.uniform(k_A, (B, N, N), dtype=jnp.float32)
        lim_W = 1.0 / np.sqrt(C)
        W_w = jax.random.uniform(k_Ww, (C, C), minval=-lim_W, maxval=lim_W, dtype=jnp.float32)
        W_b = jax.random.uniform(k_Wb, (C,), minval=-lim_W, maxval=lim_W, dtype=jnp.float32)
        lim_a = 1.0 / np.sqrt(2 * C)
        a_w = jax.random.uniform(k_aw, (2 * C,), minval=-lim_a, maxval=lim_a, dtype=jnp.float32)
        a_b = jax.random.uniform(k_ab, (), minval=-lim_a, maxval=lim_a, dtype=jnp.float32)
        return {'h': h, 'A': A, 'W_w': W_w, 'W_b': W_b, 'a_w': a_w, 'a_b': a_b}
    _L0_gnn_all = _L0_gnn_setup()
    _L0_gnn_in = {k: v for k, v in _L0_gnn_all.items() if k in ('W_w', 'W_b', 'a_w', 'a_b')}
    del _L0_gnn_all

    def _L1_gnn_setup():
        import jax, jax.numpy as jnp
        import numpy as np
        T_DIL = 10
        K_DIL = 2
        BN_EPS = 1e-05
        NORM_EPS = 1e-12

        def _dilate_pattern(adj_bool, mask_b):
            N = adj_bool.shape[0]

            def step(carry, n):
                row = jnp.take(carry, n, axis=0)
                nbi = row.astype(jnp.int32)
                num = jnp.sum(nbi)
                sf = jnp.where(num > T_DIL, (num + K_DIL - 1) // K_DIL, 1)
                rank = jnp.cumsum(nbi)
                rm = row & (rank % sf == 0)
                valid = (mask_b[n] != 0) & (num > 1)
                rm = jnp.where(valid, rm, False)
                keep = ~rm
                carry = carry.at[n].set(row & keep)
                carry = carry.at[:, n].set(carry[:, n] & keep)
                return (carry, None)
            out, _ = jax.lax.scan(step, adj_bool, jnp.arange(N))
            return out

        def _dilate(adj, mask):
            keep = jax.vmap(_dilate_pattern)(adj > 0, mask)
            return adj * keep.astype(adj.dtype)

        def _sage(x, adj, Wr, Wx, b, mf):
            deg = jnp.clip(jnp.sum(adj, axis=-1, keepdims=True), 1.0, None)
            agg = jnp.einsum('bij,bjd->bid', adj, x) / deg
            out = agg @ Wr + x @ Wx + b
            nrm = jnp.maximum(jnp.linalg.norm(out, axis=-1, keepdims=True), NORM_EPS)
            return out / nrm * mf[..., None]

        def _bn(x, g, b):
            m = jnp.mean(x, axis=(0, 1))
            v = jnp.var(x, axis=(0, 1))
            return (x - m) * jax.lax.rsqrt(v + BN_EPS) * g + b

        def _forward(x, adj, mask, Wr1, Wx1, b1, g1, be1, Wr2, Wx2, b2, g2, be2, Wr3, Wx3, b3, g3, be3, Wl, bl):
            mf = mask.astype(x.dtype)
            adj_d = _dilate(adj, mask)
            h1 = _bn(jax.nn.relu(_sage(x, adj_d, Wr1, Wx1, b1, mf)), g1, be1)
            h2 = _bn(jax.nn.relu(_sage(h1, adj_d, Wr2, Wx2, b2, mf)), g2, be2)
            h3 = _bn(jax.nn.relu(_sage(h2, adj_d, Wr3, Wx3, b3, mf)), g3, be3)
            xc = jnp.concatenate([h1, h2, h3], axis=-1) * mf[..., None]
            return (xc @ Wl + bl) * mf[..., None]
        B, N, D, H, E = (8, 1024, 128, 128, 128)
        key = jax.random.key(seed)
        ks = jax.random.split(key, 24)
        x = jax.random.normal(ks[0], (B, N, D), dtype=jnp.float32)
        a = jax.random.bernoulli(ks[1], 0.01, (B, N, N))
        a = a | jnp.swapaxes(a, 1, 2)
        a = a & ~jnp.eye(N, dtype=bool)[None]
        adj = a.astype(jnp.float32)
        mask = jnp.ones((B, N), dtype=jnp.int32)
        s = 0.05
        p = {}
        dims = [(D, H), (H, H), (H, E)]
        for i, (di, do) in enumerate(dims, 1):
            p[f'Wr{i}'] = s * jax.random.normal(ks[2 * i], (di, do), dtype=jnp.float32)
            p[f'Wx{i}'] = s * jax.random.normal(ks[2 * i + 1], (di, do), dtype=jnp.float32)
            p[f'b{i}'] = jnp.zeros((do,), dtype=jnp.float32)
            p[f'g{i}'] = jnp.ones((do,), dtype=jnp.float32)
            p[f'be{i}'] = jnp.zeros((do,), dtype=jnp.float32)
        p['Wl'] = s * jax.random.normal(ks[10], (2 * H + E, E), dtype=jnp.float32)
        p['bl'] = jnp.zeros((E,), dtype=jnp.float32)
        return {'x': x, 'adj': adj, 'mask': mask, **p}
    _L1_gnn_all = _L1_gnn_setup()
    _L1_gnn_in = {k: v for k, v in _L1_gnn_all.items() if k in ('Wr1', 'Wx1', 'b1', 'g1', 'be1', 'Wr2', 'Wx2', 'b2', 'g2', 'be2', 'Wr3', 'Wx3', 'b3', 'g3', 'be3', 'Wl', 'bl')}
    del _L1_gnn_all

    def _L2_gnn_setup():
        import jax, jax.numpy as jnp
        import numpy as np

        def _normalize_adjacency(adj):
            N = adj.shape[-1]
            adj_self = adj + jnp.eye(N, dtype=adj.dtype)
            rowsum = adj_self.sum(axis=2)
            d_inv_sqrt = rowsum ** (-0.5)
            d_inv_sqrt = jnp.where(jnp.isinf(d_inv_sqrt), 0.0, d_inv_sqrt)
            return adj_self * d_inv_sqrt[:, :, None] * d_inv_sqrt[:, None, :]
        key = jax.random.key(seed)
        k1, k2, k3 = jax.random.split(key, 3)
        B, N, Fin, Fout = (32, 512, 128, 128)
        x = jax.random.normal(k1, (B, N, Fin), dtype=jnp.float32)
        adj = jax.random.uniform(k2, (B, N, N), dtype=jnp.float32)
        limit = float(np.sqrt(6.0 / (Fin + Fout)))
        weight = jax.random.uniform(k3, (Fin, Fout), dtype=jnp.float32, minval=-limit, maxval=limit)
        bias = jnp.zeros((Fout,), dtype=jnp.float32)
        return {'x': x, 'adj': adj, 'weight': weight, 'bias': bias}
    _L2_gnn_all = _L2_gnn_setup()
    _L2_gnn_in = {k: v for k, v in _L2_gnn_all.items() if k in ('weight', 'bias')}
    del _L2_gnn_all

    def _L3_gnn_setup():
        import jax, jax.numpy as jnp
        import numpy as np
        B, N, D = (4, 2048, 128)
        key = jax.random.key(seed)
        k1, k2, k3 = jax.random.split(key, 3)
        x = jax.random.normal(k1, (B, N, D), dtype=jnp.float32)
        adj_mat = jax.random.randint(k2, (B, N, N), 0, 2).astype(jnp.float32)
        U = jax.random.normal(k3, (D, D), dtype=jnp.float32) * np.sqrt(2.0 / (D + D))
        return {'x': x, 'adj_mat': adj_mat, 'U': U}
    _L3_gnn_all = _L3_gnn_setup()
    _L3_gnn_in = {k: v for k, v in _L3_gnn_all.items() if k in ('U',)}
    del _L3_gnn_all
    return {'x': x, 'adj': adj, 'nodemask': nodemask, 'L0_gnn_W_w': _L0_gnn_in['W_w'], 'L0_gnn_W_b': _L0_gnn_in['W_b'], 'L0_gnn_a_w': _L0_gnn_in['a_w'], 'L0_gnn_a_b': _L0_gnn_in['a_b'], 'L1_gnn_Wr1': _L1_gnn_in['Wr1'], 'L1_gnn_Wx1': _L1_gnn_in['Wx1'], 'L1_gnn_b1': _L1_gnn_in['b1'], 'L1_gnn_g1': _L1_gnn_in['g1'], 'L1_gnn_be1': _L1_gnn_in['be1'], 'L1_gnn_Wr2': _L1_gnn_in['Wr2'], 'L1_gnn_Wx2': _L1_gnn_in['Wx2'], 'L1_gnn_b2': _L1_gnn_in['b2'], 'L1_gnn_g2': _L1_gnn_in['g2'], 'L1_gnn_be2': _L1_gnn_in['be2'], 'L1_gnn_Wr3': _L1_gnn_in['Wr3'], 'L1_gnn_Wx3': _L1_gnn_in['Wx3'], 'L1_gnn_b3': _L1_gnn_in['b3'], 'L1_gnn_g3': _L1_gnn_in['g3'], 'L1_gnn_be3': _L1_gnn_in['be3'], 'L1_gnn_Wl': _L1_gnn_in['Wl'], 'L1_gnn_bl': _L1_gnn_in['bl'], 'L2_gnn_weight': _L2_gnn_in['weight'], 'L2_gnn_bias': _L2_gnn_in['bias'], 'L3_gnn_U': _L3_gnn_in['U']}

def reference(x, adj, nodemask, L0_gnn_W_w, L0_gnn_W_b, L0_gnn_a_w, L0_gnn_a_b, L1_gnn_Wr1, L1_gnn_Wx1, L1_gnn_b1, L1_gnn_g1, L1_gnn_be1, L1_gnn_Wr2, L1_gnn_Wx2, L1_gnn_b2, L1_gnn_g2, L1_gnn_be2, L1_gnn_Wr3, L1_gnn_Wx3, L1_gnn_b3, L1_gnn_g3, L1_gnn_be3, L1_gnn_Wl, L1_gnn_bl, L2_gnn_weight, L2_gnn_bias, L3_gnn_U):
    import jax
    import jax.numpy as jnp

    def _L0_gnn_ref(h, A, W_w, W_b, a_w, a_b):
        import jax, jax.numpy as jnp
        import numpy as np
        C = 128
        Wh = jnp.einsum('bnc,dc->bnd', h, W_w) + W_b
        si = Wh @ a_w[:C]
        sj = Wh @ a_w[C:]
        s = si[:, :, None] + sj[:, None, :] + a_b
        e = jnp.exp(s) * A
        alpha = e / jnp.sum(e, axis=2, keepdims=True)
        h_prime = jnp.einsum('bij,bjc->bic', alpha, h)
        return h_prime

    def _L1_gnn_ref(x, adj, mask, Wr1, Wx1, b1, g1, be1, Wr2, Wx2, b2, g2, be2, Wr3, Wx3, b3, g3, be3, Wl, bl):
        import jax, jax.numpy as jnp
        import numpy as np
        T_DIL = 10
        K_DIL = 2
        BN_EPS = 1e-05
        NORM_EPS = 1e-12

        def _dilate_pattern(adj_bool, mask_b):
            N = adj_bool.shape[0]

            def step(carry, n):
                row = jnp.take(carry, n, axis=0)
                nbi = row.astype(jnp.int32)
                num = jnp.sum(nbi)
                sf = jnp.where(num > T_DIL, (num + K_DIL - 1) // K_DIL, 1)
                rank = jnp.cumsum(nbi)
                rm = row & (rank % sf == 0)
                valid = (mask_b[n] != 0) & (num > 1)
                rm = jnp.where(valid, rm, False)
                keep = ~rm
                carry = carry.at[n].set(row & keep)
                carry = carry.at[:, n].set(carry[:, n] & keep)
                return (carry, None)
            out, _ = jax.lax.scan(step, adj_bool, jnp.arange(N))
            return out

        def _dilate(adj, mask):
            keep = jax.vmap(_dilate_pattern)(adj > 0, mask)
            return adj * keep.astype(adj.dtype)

        def _sage(x, adj, Wr, Wx, b, mf):
            deg = jnp.clip(jnp.sum(adj, axis=-1, keepdims=True), 1.0, None)
            agg = jnp.einsum('bij,bjd->bid', adj, x) / deg
            out = agg @ Wr + x @ Wx + b
            nrm = jnp.maximum(jnp.linalg.norm(out, axis=-1, keepdims=True), NORM_EPS)
            return out / nrm * mf[..., None]

        def _bn(x, g, b):
            m = jnp.mean(x, axis=(0, 1))
            v = jnp.var(x, axis=(0, 1))
            return (x - m) * jax.lax.rsqrt(v + BN_EPS) * g + b

        def _forward(x, adj, mask, Wr1, Wx1, b1, g1, be1, Wr2, Wx2, b2, g2, be2, Wr3, Wx3, b3, g3, be3, Wl, bl):
            mf = mask.astype(x.dtype)
            adj_d = _dilate(adj, mask)
            h1 = _bn(jax.nn.relu(_sage(x, adj_d, Wr1, Wx1, b1, mf)), g1, be1)
            h2 = _bn(jax.nn.relu(_sage(h1, adj_d, Wr2, Wx2, b2, mf)), g2, be2)
            h3 = _bn(jax.nn.relu(_sage(h2, adj_d, Wr3, Wx3, b3, mf)), g3, be3)
            xc = jnp.concatenate([h1, h2, h3], axis=-1) * mf[..., None]
            return (xc @ Wl + bl) * mf[..., None]
        return _forward(x, adj, mask, Wr1, Wx1, b1, g1, be1, Wr2, Wx2, b2, g2, be2, Wr3, Wx3, b3, g3, be3, Wl, bl)

    def _L2_gnn_ref(x, adj, weight, bias):
        import jax, jax.numpy as jnp
        import numpy as np

        def _normalize_adjacency(adj):
            N = adj.shape[-1]
            adj_self = adj + jnp.eye(N, dtype=adj.dtype)
            rowsum = adj_self.sum(axis=2)
            d_inv_sqrt = rowsum ** (-0.5)
            d_inv_sqrt = jnp.where(jnp.isinf(d_inv_sqrt), 0.0, d_inv_sqrt)
            return adj_self * d_inv_sqrt[:, :, None] * d_inv_sqrt[:, None, :]
        adj_norm = _normalize_adjacency(adj)
        support = jnp.einsum('bni,io->bno', x, weight)
        out = jnp.einsum('bnm,bmo->bno', adj_norm, support) + bias
        return out

    def _L3_gnn_ref(x, adj_mat, U):
        import jax, jax.numpy as jnp
        import numpy as np
        B, N, D = (4, 2048, 128)
        mask = (adj_mat > 0).astype(x.dtype)
        deg = jnp.sum(adj_mat, axis=1)
        agg = jnp.einsum('bji,bjd->bid', mask, x)
        out = jax.nn.relu(jnp.einsum('bid,de->bie', agg, U) / deg[..., None])
        return out
    h = jnp.maximum(_layernorm(x, axis=-1), 0.0)
    x = x + _L0_gnn_ref(h, adj, L0_gnn_W_w, L0_gnn_W_b, L0_gnn_a_w, L0_gnn_a_b)
    h = jnp.maximum(_layernorm(x, axis=-1), 0.0)
    x = x + _L1_gnn_ref(h, adj, nodemask, L1_gnn_Wr1, L1_gnn_Wx1, L1_gnn_b1, L1_gnn_g1, L1_gnn_be1, L1_gnn_Wr2, L1_gnn_Wx2, L1_gnn_b2, L1_gnn_g2, L1_gnn_be2, L1_gnn_Wr3, L1_gnn_Wx3, L1_gnn_b3, L1_gnn_g3, L1_gnn_be3, L1_gnn_Wl, L1_gnn_bl)
    h = jnp.maximum(_layernorm(x, axis=-1), 0.0)
    x = x + _L2_gnn_ref(h, adj, L2_gnn_weight, L2_gnn_bias)
    h = jnp.maximum(_layernorm(x, axis=-1), 0.0)
    x = x + _L3_gnn_ref(h, adj, L3_gnn_U)
    return x

_drawn_inputs = setup_inputs


def setup_inputs(seed=0):
    import zlib

    import numpy as np

    out = dict(_drawn_inputs(seed))
    spreads = {'L1_gnn_b1': (0.0, 0.1),
     'L1_gnn_g1': (1.0, 0.2),
     'L1_gnn_be1': (0.0, 0.1),
     'L1_gnn_b2': (0.0, 0.1),
     'L1_gnn_g2': (1.0, 0.2),
     'L1_gnn_be2': (0.0, 0.1),
     'L1_gnn_b3': (0.0, 0.1),
     'L1_gnn_g3': (1.0, 0.2),
     'L1_gnn_be3': (0.0, 0.1),
     'L1_gnn_bl': (0.0, 0.1),
     'L2_gnn_bias': (0.0, 0.1)}
    factors = {}
    for name, (base, spread) in spreads.items():
        noise = np.random.default_rng([zlib.crc32(name.encode()), seed]).standard_normal(out[name].shape)
        drawn = base * np.exp(spread * noise) if base else spread * noise
        out[name] = jnp.asarray(drawn.astype(out[name].dtype))
    for name, factor in factors.items():
        out[name] = (out[name] * factor).astype(out[name].dtype)
    return out
```

```python
from contextlib import ExitStack

import concourse.bass as bass
from concourse import mybir

ALU = mybir.AluOpType
ACT = mybir.ActivationFunctionType
F32 = mybir.dt.float32
BF16 = mybir.dt.bfloat16
F16 = mybir.dt.float16
I32 = mybir.dt.int32
AX = mybir.AxisListType.X

P = 128
HALF = 512
LN_EPS = 1e-5
BN_EPS = 1e-5
NORM_EPS = 1e-12
DENSE_ROW = 10.0
FAST_ROUNDS = 4
ROUND = float(2 ** 23)

(V_WB, V_B1, V_B2, V_B3, V_BL, V_G1, V_G2, V_G3, V_E1, V_E2, V_E3, V_BIAS2) = range(12)
NVEC = 12


class Shapes:
    def __init__(self, x, adj):
        self.B, self.N, self.D = x.shape
        self.NB = self.N // P
        self.T = self.B * self.NB
        self.NH = self.N // HALF
        self.HB = HALF // P
        assert self.D == P and self.B % 2 == 0 and self.N % HALF == 0


def per_pair(engine, B, body):
    if B > 2:
        with engine.Fori(0, B // 2 - 1) as g:
            for parity in range(2):
                body(g * 2 + parity, parity, False)
    for parity in range(2):
        body(B - 2 + parity, parity, parity == 1)


def at(tensor, b, *rest):
    if isinstance(b, int):
        return tensor[b]
    return tensor[bass.ds(b, 1)].rearrange("o ... -> (o ...)") if not rest else None


def graph(tensor3, b):
    if isinstance(b, int):
        return tensor3[b].rearrange("(t p) n -> p t n", p=P)
    return tensor3[bass.ds(b, 1)].rearrange("o (t p) n -> p (o t) n", p=P)


def tiles(tensor, b, nb):
    return tensor[:, bass.ds(b * nb, nb)] if not isinstance(b, int) else tensor[:, b * nb:(b + 1) * nb]


def along_features(col, d):
    return col.unsqueeze(2).to_broadcast([P, col.shape[1], d])


def along_tiles(row, t):
    return row.unsqueeze(1).to_broadcast([P, t, row.shape[1]])


def norm_relu_vector(nc, dve, x, out, w, b):
    s, v = w["stat"], nc.vector
    D = x.shape[2]
    v.tensor_reduce(s[:, 0, :], x, AX, ALU.add)
    dve.drain()
    v.tensor_scalar(s[:, 1, :], s[:, 0, :], -1.0 / D, None, ALU.mult)
    dve.drain()
    v.tensor_tensor(w["centred"][:], x, along_features(s[:, 1, :], D), ALU.add)
    dve.drain()
    v.tensor_tensor(w["squared"][:], w["centred"][:], w["centred"][:], ALU.mult)
    dve.drain()
    v.tensor_reduce(s[:, 2, :], w["squared"][:], AX, ALU.add)
    dve.drain()
    v.tensor_scalar(s[:, 3, :], s[:, 2, :], 1.0 / D, LN_EPS, ALU.mult, ALU.add).then_inc(w["var_ready"], 1)
    dve.wait_ge(w["std_ready"], b + 1)
    v.reciprocal(s[:, 5, :], s[:, 4, :])
    dve.drain()
    return v.scalar_tensor_tensor(out, w["centred"][:], 0.0, along_features(s[:, 5, :], D), ALU.max, ALU.mult)


def norm_root(nc, act, w, b):
    act.wait_ge(w["var_ready"], b + 1)
    nc.scalar.activation(w["stat"][:, 4, :], w["stat"][:, 3, :], ACT.Sqrt).then_inc(w["std_ready"], 1)


def norm_buffers(sb, sem, tag, NB, D):
    return dict(stat=sb(f"{tag}_stat", [P, 6, NB], F32), centred=sb(f"{tag}_centred", [P, NB, D], F32),
                squared=sb(f"{tag}_squared", [P, NB, D], F32),
                var_ready=sem(f"{tag}_var_ready"), std_ready=sem(f"{tag}_std_ready"))


class Scope:

    def __init__(self, nc, tag):
        self.nc, self.tag, self.stack = nc, tag, ExitStack()
        self.sems = []

    def __enter__(self):
        self.stack.__enter__()
        return self

    def __exit__(self, *e):
        if e[0] is None:
            self.nc.clear_and_free_semaphores(self.sems)
            self.nc.all_engine_barrier(sem_only=True)
        return self.stack.__exit__(*e)

    def sb(self, name, shape, dt):
        return self.stack.enter_context(self.nc.sbuf_tensor(f"{self.tag}_{name}", shape, dt))

    def ps(self, name, shape, dt=F32):
        return self.stack.enter_context(self.nc.psum_tensor(f"{self.tag}_{name}", shape, dt))

    def sem(self, name):
        self.sems.append(self.nc.alloc_semaphore(f"{self.tag}_{name}"))
        return self.sems[-1]


def constants_phase(nc, z, A, K):
    D, T, B = z.D, z.T, z.B
    with Scope(nc, "con") as s:
        rows = s.sb("rows", [1, NVEC, D], F32)
        ab = s.sb("ab", [1, 1], F32)
        ones1 = s.sb("ones1", [1, P], F32)
        onesf = s.sb("onesf", [P, P], F32)
        acol = s.sb("acol", [P, 2], F32)
        abc = s.sb("abc", [P, 2, P], F32)
        wbcol = s.sb("wbcol", [P, 1], F32)
        Ww = s.sb("Ww", [P, D], F32)
        maski = s.sb("maski", [T, P], I32)
        maskf = s.sb("maskf", [T, P], F32)
        pm = s.ps("pm", [P, T])
        pbig = [s.ps(f"pbig{i}", [P, 512]) for i in range(3)]
        pv = s.ps("pv", [P, 2, D])
        pc = s.ps("pc", [P, 4])
        loaded, set0, const_ready = s.sem("loaded"), s.sem("set0"), s.sem("const_ready")
        rows_spread, abc_ready, v_done = s.sem("rows_spread"), s.sem("abc_ready"), s.sem("v_done")
        mask_ready, mask_turned = s.sem("mask_ready"), s.sem("mask_turned")
        vecs = [(A["L0_gnn_W_b"], V_WB), (A["L1_gnn_b1"], V_B1), (A["L1_gnn_b2"], V_B2), (A["L1_gnn_b3"], V_B3),
                (A["L1_gnn_bl"], V_BL), (A["L1_gnn_g1"], V_G1), (A["L1_gnn_g2"], V_G2), (A["L1_gnn_g3"], V_G3),
                (A["L1_gnn_be1"], V_E1), (A["L1_gnn_be2"], V_E2), (A["L1_gnn_be3"], V_E3), (A["L2_gnn_bias"], V_BIAS2)]
        weights = [("Wr0", A["L1_gnn_Wr1"]), ("Wr1", A["L1_gnn_Wr2"]), ("Wr2", A["L1_gnn_Wr3"]),
                   ("Wx0", A["L1_gnn_Wx1"]), ("Wx1", A["L1_gnn_Wx2"]), ("Wx2", A["L1_gnn_Wx3"]),
                   ("W2", A["L2_gnn_weight"]), ("U", A["L3_gnn_U"])]
        n_loads = len(vecs) + len(weights) + 8
        with nc.Block() as block:
            @block.sync
            def _(sp):
                for src, i in vecs:
                    sp.dma_start(rows[:, i, :], src.rearrange("(o d) -> o d", o=1)).then_inc(loaded, 16)
                sp.dma_start(ab[:], A["L0_gnn_a_b"].rearrange("(o d) -> o d", o=1)).then_inc(loaded, 16)
                for i in range(2):
                    sp.dma_start(acol[:, i:i + 1], A["L0_gnn_a_w"][i * P:(i + 1) * P].rearrange("(p o) -> p o", o=1))\
                        .then_inc(loaded, 16)
                sp.dma_start(wbcol[:], A["L0_gnn_W_b"].rearrange("(p o) -> p o", o=1)).then_inc(loaded, 16)
                sp.dma_start(Ww[:], A["L0_gnn_W_w"]).then_inc(loaded, 16)
                for name, src in weights:
                    sp.dma_start(K[name][:], src).then_inc(loaded, 16)
                sp.dma_start(K["Wl"][:], A["L1_gnn_Wl"].rearrange("(t p) e -> p t e", p=P)).then_inc(loaded, 16)
                sp.dma_start(maski[:], A["nodemask"].rearrange("b (t p) -> (b t) p", p=P)).then_inc(loaded, 16)
                sp.dma_start(K["X"][:], A["x"].rearrange("b (t p) d -> p (b t) d", p=P)).then_inc(loaded, 16)

            @block.gpsimd
            def _(pool):
                p = nc.gpsimd
                p.memset(K["ident"][:], 0.0)
                p.memset(K["ident16"][:], 0.0)
                p.memset(K["tri"][:], 1.0)
                p.memset(K["upper"][:], 1.0)
                p.memset(K["ones16"][:], 1.0)
                p.memset(onesf[:], 1.0)
                p.memset(K["onescol"][:], 1.0)
                p.memset(ones1[:], 1.0).then_inc(set0, 1)
                pool.wait_ge(set0, 1)
                for m in (K["ident"], K["ident16"]):
                    p.affine_select(out=m[:], in_=m[:], compare_op=ALU.not_equal, fill=1.0, base=0,
                                    pattern=[[-1, P]], channel_multiplier=1)
                p.affine_select(out=K["tri"][:], in_=K["tri"][:], compare_op=ALU.is_ge, fill=0.0, base=0,
                                pattern=[[1, z.N]], channel_multiplier=-1)
                p.affine_select(out=K["upper"][:], in_=K["upper"][:], compare_op=ALU.is_ge, fill=0.0, base=-1,
                                pattern=[[1, P]], channel_multiplier=-1).then_inc(const_ready, 1)

            @block.tensor
            def _(pe):
                pe.wait_ge(const_ready, 1)
                pe.wait_ge(loaded, 16 * n_loads)
                flat = rows[:].rearrange("o v d -> o (v d)")
                for i in range(3):
                    nc.tensor.matmul(pbig[i][:], ones1[:], flat[:, i * 512:(i + 1) * 512], start=True, stop=True)
                nc.tensor.matmul(pc[:, 2:3], ones1[:], ab[:], start=True, stop=True).then_inc(rows_spread, 1)
                pe.wait_ge(mask_ready, 1)
                nc.tensor.transpose(pm[:], maskf[:], K["ident"][0:T, 0:T]).then_inc(mask_turned, 1)
                pe.wait_ge(abc_ready, 1)
                for h in range(2):
                    nc.tensor.matmul(pv[:, h, :], abc[:, h, :], Ww[:], start=True, stop=True)
                    last = nc.tensor.matmul(pc[:, h:h + 1], abc[:, h, :], wbcol[:], start=True, stop=True)
                last.then_inc(v_done, 1)

            @block.vector
            def _(dve):
                v = nc.vector
                dve.wait_ge(const_ready, 1)
                dve.wait_ge(loaded, 16 * n_loads)
                for h in range(2):
                    last = v.tensor_scalar(abc[:, h, :], onesf[:], acol[:, h:h + 1], None, ALU.mult)
                last.then_inc(abc_ready, 1)
                v.tensor_copy(maskf[:], maski[:]).then_inc(mask_ready, 1)
                dve.wait_ge(mask_turned, 1)
                v.tensor_copy(K["mask"][:], pm[:])
                dve.drain()
                v.tensor_tensor(K["mask2"][:], K["mask"][:], K["mask"][:], ALU.mult)
                v.tensor_scalar(K["maskok"][:], K["mask"][:], 0.0, None, ALU.not_equal)
                dve.wait_ge(rows_spread, 1)
                for i in range(3):
                    v.tensor_copy(K["vec"][:, 4 * i:4 * i + 4, :].rearrange("p v d -> p (v d)"), pbig[i][:])
                dve.wait_ge(v_done, 1)
                v.tensor_copy(K["av"][:], pv[:])
                v.tensor_copy(K["ac"][:], pc[:, 0:3])
                dve.drain()
                v.tensor_tensor(K["ac"][:, 0:1], K["ac"][:, 0:1], K["ac"][:, 2:3], ALU.add)


def attention_phase(nc, z, A, K):
    B, N, NB, D = z.B, z.N, z.NB, z.D
    W = D + 2
    with Scope(nc, "att") as s:
        adjT = [s.sb(f"adjT{i}", [P, NB, N], F32) for i in range(2)]
        rhs = [s.sb(f"rhs{i}", [P, NB, W], F32) for i in range(2)]
        G = [s.sb(f"G{i}", [P, NB], F32) for i in range(2)]
        h = s.sb("h", [P, NB, D], F32)
        t1 = s.sb("t1", [P, NB, D], F32)
        sj = s.sb("sj", [P, 2, NB], F32)
        E = s.sb("E", [P, NB], F32)
        y = s.sb("y", [P, 2, D], F32)
        q = s.sb("q", [P, 4, 2], F32)
        w = norm_buffers(s.sb, s.sem, "n", NB, D)
        acc = [s.ps(f"acc{i}", [P, 2, 256]) for i in range(4)]
        adj_loaded = [s.sem(f"adj_loaded{i}") for i in range(2)]
        issued = s.sem("issued")
        adj_used, score_ready, exp_ready = s.sem("adj_used"), s.sem("score_ready"), s.sem("exp_ready")
        rhs_ready, sums_ready, sums_read = s.sem("rhs_ready"), s.sem("sums_ready"), s.sem("sums_read")
        QB = NB // 2
        with nc.Block() as block:
            @block.sync
            def _(sp):
                def body(b, par, last):
                    sp.wait_ge(adj_used, b + 1)
                    sp.sem_inc(issued, 1)
                    for c in range(2):
                        hb = NB // 2
                        sp.dma_start(adjT[par][:, c * hb:(c + 1) * hb, :],
                                     graph(A["adj_cols"], b)[:, c * hb:(c + 1) * hb, :]).then_inc(adj_loaded[par], 16)
                per_pair(sp, B, body)

            @block.tensor
            def _(pe):
                pe.sem_inc(adj_used, 2)

                def body(b, par, last):
                    g = (b - par) if isinstance(b, int) else b - par
                    pe.wait_ge(rhs_ready, b + 1)
                    pe.wait_ge(adj_loaded[par], g * 16 + 32)
                    for k in range(QB):
                        pe.wait_ge(sums_read, b * QB + k + 1)
                        for e in range(2):
                            ib = 2 * k + e
                            for jb in range(NB):
                                mm = nc.tensor.matmul(acc[k % 4][:, e, 0:W], adjT[par][:, jb, ib * P:(ib + 1) * P],
                                                      rhs[par][:, jb, :], start=(jb == 0), stop=(jb == NB - 1))
                        mm.then_inc(sums_ready, 1)
                    pe.drain().then_inc(adj_used, 1)
                per_pair(pe, B, body)

            @block.scalar
            def _(act):
                def body(b, par, last):
                    norm_root(nc, act, w, b)
                    act.wait_ge(score_ready, b + 1)
                    nc.scalar.activation(G[par][:], sj[:, 0, :], ACT.Exp, bias=K["ac"][:, 0:1])
                    nc.scalar.activation(E[:], sj[:, 1, :], ACT.Exp, bias=K["ac"][:, 1:2]).then_inc(exp_ready, 1)
                per_pair(act, B, body)

            @block.vector
            def _(dve):
                v = nc.vector
                dve.sem_inc(sums_read, 4)
                for r in rhs:
                    v.memset(r[:, :, D + 1:D + 2], 1.0)

                def prepare(b, par):
                    norm_relu_vector(nc, dve, tiles(K["X"], b, NB), h[:], w, b)
                    dve.drain()
                    for k in range(2):
                        v.tensor_tensor(t1[:], h[:], along_tiles(K["av"][:, k, :], NB), ALU.mult)
                        dve.drain()
                        last = v.tensor_reduce(sj[:, k, :], t1[:], AX, ALU.add)
                        if k == 0:
                            dve.drain()
                    last.then_inc(score_ready, 1)
                    dve.wait_ge(exp_ready, b + 1)
                    v.tensor_copy(rhs[par][:, :, D], E[:])
                    v.tensor_tensor(rhs[par][:, :, 0:D], h[:], along_features(E[:], D), ALU.mult).then_inc(rhs_ready, 1)

                def finish(b, par):
                    for k in range(QB):
                        a = acc[k % 4]
                        xs = K["X"][:, bass.ds(b * NB + 2 * k, 2)]
                        dve.wait_ge(sums_ready, b * QB + k + 1)
                        v.tensor_copy(K["rowsum"][:, bass.ds(b * NB + 2 * k, 2)], a[:, :, D + 1])
                        g = G[par][:, 2 * k:2 * k + 2]
                        v.tensor_tensor(q[:, 0, :], a[:, :, D], g, ALU.mult)
                        dve.drain()
                        v.reciprocal(q[:, 1, :], q[:, 0, :])
                        dve.drain()
                        v.tensor_tensor(q[:, 2, :], q[:, 1, :], g, ALU.mult)
                        dve.drain()
                        v.tensor_tensor(y[:], a[:, :, 0:D], along_features(q[:, 2, :], D), ALU.mult).then_inc(sums_read, 1)
                        dve.drain()
                        v.tensor_tensor(xs, xs, y[:], ALU.add)
                        dve.drain()

                prepare(0, 0)

                def body(b, par, last):
                    if not last:
                        prepare(b + 1, 1 - par)
                    finish(b, par)
                per_pair(dve, B, body)


def removal_parameters(nc, dve, k, num0, off, maskok, w, with_rank_shift, out=None):
    v = nc.vector
    scale, bias, dist = out if out else (w[:, 0], w[:, 1], w[:, 2])
    num, a, fh, par, d, m = (w[:, i] for i in range(3, 9))
    v.tensor_tensor(num, num0, k, ALU.subtract)
    dve.drain()
    v.tensor_scalar(a, num, 0.5, -0.25, ALU.mult, ALU.add)
    v.tensor_scalar(scale, num, DENSE_ROW, None, ALU.is_gt)
    dve.drain()
    v.tensor_scalar(fh, a, ROUND, -ROUND, ALU.add, ALU.add)
    dve.drain()
    v.scalar_tensor_tensor(par, fh, -2.0, num, ALU.mult, ALU.add)
    v.tensor_tensor(m, num, fh, ALU.subtract)
    dve.drain()
    v.tensor_scalar(a, par, -0.25, 0.25, ALU.mult, ALU.add)
    dve.drain()
    v.tensor_tensor(d, num, a, ALU.mult)
    dve.drain()
    v.tensor_tensor(m, m, d, ALU.add)
    v.tensor_tensor(a, d, scale, ALU.mult)
    v.scalar_tensor_tensor(par, num, 2.0, maskok, ALU.is_ge, ALU.mult)
    dve.drain()
    if with_rank_shift:
        v.tensor_tensor(fh, off, k, ALU.subtract)
        v.scalar_tensor_tensor(a, a, 1.0, par, ALU.add, ALU.mult)
        dve.drain()
        v.tensor_tensor(m, fh, m, ALU.subtract)
    else:
        v.tensor_scalar(m, m, -1.0, None, ALU.mult)
        v.scalar_tensor_tensor(a, a, 1.0, par, ALU.add, ALU.mult)
    dve.drain()
    v.tensor_scalar(dist, a, -1.0, None, ALU.add)
    return v.tensor_tensor(bias, m, scale, ALU.mult)


def removal_phase(nc, z, A, K, scratch):
    B, N, NB = z.B, z.N, z.NB
    CH = B // 2
    with Scope(nc, "rem") as s:
        an = [s.sb(f"an{i}", [P, 2, N], F32) for i in range(2)]
        ac = [s.sb(f"ac{i}", [P, 2, N], F32) for i in range(2)]
        rowbin = [s.sb(f"rowbin{i}", [P, 2, N], BF16) for i in range(2)]
        curT = [s.sb(f"curT{i}", [P, B, N], BF16) for i in range(2)]
        both = s.sb("both", [P, B, N], BF16)
        rank = s.sb("rank", [P, B, N], F16)
        rem = s.sb("rem", [P, B, N], BF16)
        dist = [s.sb(f"dist{i}", [P, N], F32) for i in range(2)]
        distd = s.sb("distd", [P, B, P], F32)
        junk = s.sb("junk", [P, N], BF16)
        ones = s.sb("ones", [P, N], BF16)
        w = s.sb("w", [P, 9, B], F32)
        num0, rlast, off = s.sb("num0", [P, B], F32), s.sb("rlast", [P, B], F16), s.sb("off", [P, B], F32)
        k, kprev = s.sb("k", [P, B], F32), s.sb("kprev", [P, B], F32)
        moved, movedsum = s.sb("moved", [P, B], F32), s.sb("movedsum", [P, 1], F32)
        flag = s.sb("flag", [1, 1], I32)
        Kc = s.sb("Kc", [P, NB, B], F32)
        pk = s.ps("pk", [P, B])
        pl = s.ps("pl", [P, NB, B])
        pf = s.ps("pf", [1, 1])
        loaded = [s.sem(f"loaded{i}") for i in range(2)]
        chunk_counted, chunk_compared = s.sem("chunk_counted"), s.sem("chunk_compared")
        counted, bins_ready = s.sem("counted"), s.sem("bins_ready")
        bins_stored = [s.sem(f"bins_stored{i}") for i in range(2)]
        par_ready, dist_ready = s.sem("par_ready"), s.sem("dist_ready")
        rem_ready, lost_ready, moved_ready, flag_sum, flag_ready = (s.sem(n) for n in (
            "rem_ready", "lost_ready", "moved_ready", "flag_sum", "flag_ready"))
        spar, sdist, srem, slost, sback = (s.sem(n) for n in ("slow_par", "slow_dist", "slow_rem", "slow_lost", "slow_back"))
        fpar, fdist, ffree, fullrem, lost_far = (s.sem(n) for n in ("full_par", "full_dist", "full_free", "full_rem", "lost_far"))
        cur_ready = s.sem("cur_ready")
        cur_stored = [s.sem(f"cur_stored{i}") for i in range(2)]
        R = FAST_ROUNDS
        SLOW = P
        with nc.Block() as block:
            @block.sync
            def _(sp):
                for nb in range(NB):
                    rows = slice(nb * P, (nb + 1) * P)
                    for c in range(CH):
                        i = nb * CH + c
                        if i >= 2:
                            sp.wait_ge(chunk_counted, i - 1)
                            sp.wait_ge(chunk_compared, i - 1)
                        gs = slice(2 * c, 2 * c + 2)
                        sp.dma_start(an[i % 2][:], A["adj_rows"][gs, rows, :].rearrange("b p n -> p b n")).then_inc(loaded[i % 2], 16)
                        sp.dma_start(ac[i % 2][:], A["adj_cols"][gs, rows, :].rearrange("b p n -> p b n")).then_inc(loaded[i % 2], 16)

            @block.gpsimd
            def _(pool):
                for nb in range(NB):
                    rows = slice(nb * P, (nb + 1) * P)
                    for c in range(CH):
                        i = nb * CH + c
                        pool.wait_ge(bins_ready, i + 1)
                        pool.dma_start(scratch["rowbin"][2 * c:2 * c + 2, rows, :].rearrange("b p n -> p b n"),
                                       rowbin[i % 2][:]).then_inc(bins_stored[i % 2], 16)
                    pool.wait_ge(cur_ready, nb + 1)
                    pool.dma_start(scratch["curT"][:, rows, :].rearrange("b p n -> p b n"), curT[nb % 2][:]).then_inc(cur_stored[nb % 2], 16)
                for i in range(2):
                    pool.wait_ge(bins_stored[i], 16 * len(range(i, NB * CH, 2)))
                    pool.wait_ge(cur_stored[i], 16 * len(range(i, NB, 2)))

            @block.scalar
            def _(act):
                def distances(ready, n, done):
                    act.wait_ge(ready, n)
                    for b in range(B):
                        nc.scalar.activation(distd[:, b, :], rank[:, b, 0:P], ACT.Abs, bias=w[:, 1, b:b + 1],
                                             scale=w[:, 0, b:b + 1]).then_inc(done, 1)

                for nb in range(NB):
                    for c in range(CH):
                        i = nb * CH + c
                        act.wait_ge(bins_ready, i + 1)
                        for e in range(2):
                            b = 2 * c + e
                            nc.scalar.activation(junk[:], rowbin[i % 2][:, e, :], ACT.Copy, accum_out=num0[:, b:b + 1])
                            act.drain()
                            last = nc.scalar.activation(junk[:], ac[i % 2][:, e, :], ACT.Copy,
                                                        accum_out=K["colsum"][:, b * NB + nb:b * NB + nb + 1])
                            if e == 0:
                                act.drain()
                        act.drain().then_inc(chunk_counted, 1)
                    act.drain().then_inc(counted, 1)
                    with act.Fori(0, R) as t:
                        distances(par_ready, t + (nb * R + 1), dist_ready)
                    act.wait_ge(flag_ready, nb + 1)
                    go = act.value_load(flag[0:1, 0:1], min_val=0, max_val=1)
                    with act.If(go > 0):
                        with act.Fori(0, SLOW) as t:
                            distances(spar, t + 1, sdist)
                        act.wait_ge(sback, 1)
                    W = N - nb * P
                    act.wait_ge(fpar, nb + 1)
                    for b in range(B):
                        act.wait_ge(ffree, nb * B + b + 1)
                        nc.scalar.activation(dist[b % 2][:, 0:W], rank[:, b, 0:W], ACT.Abs, bias=w[:, 1, b:b + 1],
                                             scale=w[:, 0, b:b + 1]).then_inc(fdist, 1)

            @block.tensor
            def _(pe):
                def lost(ready, n, done):
                    pe.wait_ge(ready, n)
                    for b in range(B):
                        mm = nc.tensor.matmul(pk[:, b:b + 1], rem[:, b, 0:P], K["ones16"][:, 0:1], start=True, stop=True)
                    mm.then_inc(done, 1)

                for nb in range(NB):
                    with pe.Fori(0, R) as t:
                        lost(rem_ready, t + (nb * R + 1), lost_ready)
                    pe.wait_ge(moved_ready, nb + 1)
                    nc.tensor.matmul(pf[:], movedsum[:], K["onescol"][:, 0:1], start=True, stop=True).then_inc(flag_sum, 1)
                    pe.wait_ge(flag_ready, nb + 1)
                    go = pe.value_load(flag[0:1, 0:1], min_val=0, max_val=1)
                    with pe.If(go > 0):
                        with pe.Fori(0, SLOW) as t:
                            lost(srem, t + 1, slost)
                    if nb < NB - 1:
                        pe.wait_ge(fullrem, nb + 1)
                        for jb in range(nb + 1, NB):
                            for b in range(B):
                                o = (jb - nb) * P
                                mm = nc.tensor.matmul(pl[:, jb, b:b + 1], rem[:, b, o:o + P], K["ones16"][:, 0:1],
                                                      start=True, stop=True)
                        mm.then_inc(lost_far, 1)

            @block.vector
            def _(dve):
                v = nc.vector
                v.memset(ones[:], 1.0)
                v.memset(Kc[:], 0.0)
                dve.sem_inc(ffree, 2)
                dve.drain()

                def one_round(ready, dready, drem, dlost, dn, n, mask, base):
                    removal_parameters(nc, dve, k[:], num0[:], off[:], mask, w, True).then_inc(ready, 1)
                    v.tensor_copy(kprev[:], k[:])
                    for b in range(B):
                        dve.wait_ge(dready, dn + (b + 1))
                        last = v.scalar_tensor_tensor(rem[:, b, 0:P], distd[:, b, :], w[:, 2, b:b + 1], both[:, b, 0:P],
                                                      ALU.is_equal, ALU.mult)
                    last.then_inc(drem, 1)
                    dve.wait_ge(dlost, n)
                    v.tensor_tensor(k[:], base, pk[:], ALU.add)
                    dve.drain()

                for nb in range(NB):
                    n0, W = nb * P, N - nb * P
                    mask = K["maskok"][:].rearrange("p (b t) -> p t b", t=NB)[:, nb, :]
                    base = Kc[:, nb, :]
                    cT = curT[nb % 2]
                    if nb >= 2:
                        dve.wait_ge(cur_stored[nb % 2], 16 * (nb // 2))
                    for c in range(CH):
                        i = nb * CH + c
                        rb = rowbin[i % 2]
                        dve.wait_ge(loaded[i % 2], 32 * (i // 2 + 1))
                        if i >= 2:
                            dve.wait_ge(bins_stored[i % 2], 16 * (i // 2))
                            dve.wait_ge(chunk_counted, i - 1)
                        gs = slice(2 * c, 2 * c + 2)
                        v.tensor_scalar(rb[:], an[i % 2][:], 0.0, None, ALU.is_gt).then_inc(bins_ready, 1)
                        v.tensor_scalar(cT[:, gs, :], ac[i % 2][:], 0.0, None, ALU.is_gt)
                        dve.drain().then_inc(chunk_compared, 1)
                        v.tensor_tensor(both[:, gs, 0:W], rb[:, :, n0:N], cT[:, gs, n0:N], ALU.mult)
                        for e in range(2):
                            v.tensor_tensor_scan(rank[:, 2 * c + e, 0:W], ones[:, 0:W], rb[:, e, n0:N], 0.0, ALU.mult, ALU.add)
                    dve.drain()
                    v.tensor_tensor(both[:, :, 0:P], both[:, :, 0:P],
                                    K["upper"][:].unsqueeze(1).to_broadcast([P, B, P]), ALU.mult)
                    v.tensor_copy(rlast[:], rank[:, :, W - 1])
                    v.tensor_copy(k[:], base)
                    dve.wait_ge(counted, nb + 1)
                    dve.drain()
                    v.tensor_tensor(off[:], num0[:], rlast[:], ALU.subtract)
                    dve.drain()
                    with dve.Fori(0, R) as t:
                        one_round(par_ready, dist_ready, rem_ready, lost_ready, t * B + nb * R * B, t + (nb * R + 1), mask, base)
                    v.tensor_tensor(moved[:], k[:], kprev[:], ALU.not_equal)
                    dve.drain()
                    v.reduce_sum(movedsum[:], moved[:], AX).then_inc(moved_ready, 1)
                    dve.wait_ge(flag_sum, nb + 1)
                    v.tensor_scalar(flag[:], pf[:], 0.0, None, ALU.is_gt).then_inc(flag_ready, 1)
                    dve.wait_ge(flag_ready, nb + 1)
                    go = dve.value_load(flag[0:1, 0:1], min_val=0, max_val=1)
                    with dve.If(go > 0):
                        with dve.Fori(0, SLOW) as t:
                            one_round(spar, sdist, srem, slost, t * B, t + 1, mask, base)
                        for sm in (spar, sdist, srem, slost):
                            dve.sem_clear(sm)
                        dve.sem_inc(sback, 1)
                    params = tuple(K[n][:].rearrange("p (b t) -> p t b", t=NB)[:, nb, :] for n in ("rscale", "rbias", "rdist"))
                    removal_parameters(nc, dve, k[:], num0[:], off[:], mask, w, False, params)
                    dve.drain()
                    removal_parameters(nc, dve, k[:], num0[:], off[:], mask, w, True).then_inc(fpar, 1)
                    dve.drain()
                    for b in range(B):
                        dve.wait_ge(fdist, nb * B + b + 1)
                        last = v.scalar_tensor_tensor(rem[:, b, 0:W], dist[b % 2][:, 0:W], w[:, 2, b:b + 1], both[:, b, 0:W],
                                                      ALU.is_equal, ALU.mult).then_inc(ffree, 1)
                    dve.drain().then_inc(fullrem, 1)
                    v.tensor_tensor(cT[:, :, n0:N], cT[:, :, n0:N], rem[:, :, 0:W], ALU.subtract).then_inc(cur_ready, 1)
                    if nb < NB - 1:
                        dve.wait_ge(lost_far, nb + 1)
                        v.tensor_tensor(Kc[:, nb + 1:NB, :], Kc[:, nb + 1:NB, :], pl[:, nb + 1:NB, :], ALU.add)
                        dve.drain()


def keep_phase(nc, z, A, K, scratch):
    B, N, NB, NH, HB = z.B, z.N, z.NB, z.NH, z.HB
    with Scope(nc, "keep") as s:
        cur = [s.sb(f"cur{i}", [P, NB, N], BF16) for i in range(2)]
        rowbin = [s.sb(f"rowbin{i}", [P, NB, N], BF16) for i in range(2)]
        adjT = [s.sb(f"adjT{i}", [P, NB, N], F32) for i in range(2)]
        rem = s.sb("rem", [P, NB, N], BF16)
        dist = [s.sb(f"dist{i}", [P, N], F32) for i in range(2)]
        prank = [s.ps(f"prank{i}", [P, N]) for i in range(2)]
        pboth = s.ps("pboth", [P, N])
        pdeg = s.ps("pdeg", [P, NB])
        loaded = [s.sem(f"loaded{i}") for i in range(2)]
        issued = s.sem("issued")
        in_free, rank_ready, rank_read, dist_ready, dist_read = (s.sem(n) for n in (
            "in_free", "rank_ready", "rank_read", "dist_ready", "dist_read"))
        rem_ready, rem_used, both_ready, both_read, deg_ready, deg_read = (s.sem(n) for n in (
            "rem_ready", "rem_used", "both_ready", "both_read", "deg_ready", "deg_read"))
        masked, stored, out_free = s.sem("masked"), s.sem("stored"), s.sem("out_free")
        with nc.Block() as block:
            @block.sync
            def _(sp):
                def body(b, par, last):
                    sp.wait_ge(in_free, b + 1)
                    sp.sem_inc(issued, 1)
                    sp.dma_start(cur[par][:], graph(scratch["curT"], b)).then_inc(loaded[par], 16)
                    sp.dma_start(rowbin[par][:], graph(scratch["rowbin"], b)).then_inc(loaded[par], 16)
                    sp.wait_ge(out_free, b + 1)
                    sp.sem_inc(issued, 1)
                    sp.dma_start(adjT[par][:], graph(A["adj_cols"], b)).then_inc(loaded[par], 16)
                per_pair(sp, B, body)

            @block.gpsimd
            def _(pool):
                pool.sem_inc(out_free, 2)

                def body(b, par, last):
                    pool.wait_ge(masked, b * NB + NB)
                    pool.wait_ge(deg_ready, b + 1)
                    pool.dma_start(graph(scratch["keptT"], b), adjT[par][:]).then_inc(stored, 16)
                    pool.wait_ge(stored, b * 16 + 16)
                    pool.sem_inc(out_free, 1)
                per_pair(pool, B, body)

            @block.tensor
            def _(pe):
                t = nc.tensor
                pe.sem_inc(in_free, 2)

                def body(b, par, last):
                    g = b - par
                    pe.wait_ge(loaded[par], g * 24 + 48)
                    for nb in range(NB):
                        pe.wait_ge(rank_read, b * NB + nb + 1)
                        for hf in range(NH):
                            for jb in range(min(NB, (hf + 1) * HB)):
                                lo = max(jb * P, hf * HALF)
                                wd = (hf + 1) * HALF - lo
                                mm = t.matmul(prank[nb % 2][:, lo:lo + wd], cur[par][:, jb, nb * P:(nb + 1) * P],
                                              K["tri"][:, lo - jb * P:lo - jb * P + wd],
                                              start=(jb == 0), stop=(jb == min(NB, (hf + 1) * HB) - 1))
                        mm.then_inc(rank_ready, 1)
                    pe.wait_ge(rem_ready, b * NB + NB)
                    for jb in range(NB):
                        pe.wait_ge(both_read, b * NB + jb + 1)
                        for hf in range(NH):
                            t.matmul(pboth[:, hf * HALF:(hf + 1) * HALF], K["ident16"][:],
                                     rem[:, jb, hf * HALF:(hf + 1) * HALF], start=True, stop=False)
                            for nb in range(hf * HB, (hf + 1) * HB):
                                mm = t.matmul(pboth[:, nb * P:(nb + 1) * P], rem[:, nb, jb * P:(jb + 1) * P],
                                              K["ident16"][:], start=False, stop=(nb == (hf + 1) * HB - 1))
                        mm.then_inc(both_ready, 1)
                    pe.drain().then_inc(rem_used, 1)
                    pe.wait_ge(masked, b * NB + NB)
                    pe.wait_ge(deg_read, b + 1)
                    for ib in range(NB):
                        for jb in range(NB):
                            mm = t.matmul(pdeg[:, ib:ib + 1], adjT[par][:, jb, ib * P:(ib + 1) * P], K["onescol"][:, 0:1],
                                          start=(jb == 0), stop=(jb == NB - 1))
                    mm.then_inc(deg_ready, 1)
                per_pair(pe, B, body)

            @block.scalar
            def _(act):
                act.sem_inc(rank_read, 2)

                def body(b, par, last):
                    for nb in range(NB):
                        act.wait_ge(rank_ready, b * NB + nb + 1)
                        act.wait_ge(dist_read, b * NB + nb + 1)
                        col = bass.ds(b * NB + nb, 1)
                        nc.scalar.activation(dist[nb % 2][:], prank[nb % 2][:], ACT.Abs, bias=K["rbias"][:, col],
                                             scale=K["rscale"][:, col]).then_inc(dist_ready, 1)
                        act.drain().then_inc(rank_read, 1)
                per_pair(act, B, body)

            @block.vector
            def _(dve):
                v = nc.vector
                dve.sem_inc(dist_read, 2)
                dve.sem_inc(rem_used, 1)
                dve.sem_inc(both_read, 1)
                dve.sem_inc(deg_read, 1)

                def body(b, par, last):
                    g = b - par
                    dve.wait_ge(loaded[par], g * 24 + 48)
                    dve.wait_ge(rem_used, b + 1)
                    for nb in range(NB):
                        dve.wait_ge(dist_ready, b * NB + nb + 1)
                        col = bass.ds(b * NB + nb, 1)
                        v.scalar_tensor_tensor(rem[:, nb, :], dist[nb % 2][:], K["rdist"][:, col], rowbin[par][:, nb, :],
                                               ALU.is_equal, ALU.mult).then_inc(rem_ready, 1)
                        dve.drain().then_inc(dist_read, 1)
                    dve.sem_inc(in_free, 1)
                    for jb in range(NB):
                        dve.wait_ge(both_ready, b * NB + jb + 1)
                        v.scalar_tensor_tensor(adjT[par][:, jb, :], pboth[:], 0.5, adjT[par][:, jb, :],
                                               ALU.is_lt, ALU.mult).then_inc(masked, 1)
                        dve.drain().then_inc(both_read, 1)
                    dve.wait_ge(deg_ready, b + 1)
                    cols = bass.ds(b * NB, NB)
                    v.tensor_scalar(K["rdeg"][:, cols], pdeg[:], 1.0, None, ALU.max)
                    dve.drain().then_inc(deg_read, 1)
                    v.reciprocal(K["rdeg"][:, cols], K["rdeg"][:, cols])
                per_pair(dve, B, body)


def sage_phase(nc, z, A, K, scratch, layer):
    B, N, NB, NH, HB, D = z.B, z.N, z.NB, z.NH, z.HB, z.D
    first = layer == 0
    with Scope(nc, f"sage{layer}") as s:
        adjT = [s.sb(f"adjT{i}", [P, NB, N], F32) for i in range(2)]
        h = [s.sb(f"h{i}", [P, NB, D], F32) for i in range(2)]
        hT = s.sb("hT", [P, N], F32)
        aggT = s.sb("aggT", [P, N], F32)
        o = s.sb("o", [P, NB, D], F32)
        t1 = s.sb("t1", [P, NB, D], F32)
        nrm = s.sb("nrm", [P, 5, NB], F32)
        acc = s.sb("acc", [P, 2, NB, D], F32)
        rsq = s.sb("rsq", [P, NB, D], F32)
        tot = s.sb("tot", [P, 2, D], F32)
        mv = s.sb("mv", [P, 4, D], F32)
        onesf = s.sb("onesf", [P, P], F32)
        w = norm_buffers(s.sb, s.sem, "n", NB, D) if first else None
        agg = s.ps("agg", [P, N])
        tp = s.ps("tp", [P, N])
        o1 = s.ps("o1", [P, NB, D])
        o2 = s.ps("o2", [P, NB, D])
        sem = {n: s.sem(n) for n in (
            "adj_used", "issued", "h_ready", "tp_ready", "hT_ready", "agg_half", "aggT_half", "o1_ready", "o2_ready", "y_ready",
            "y_read", "o_read", "ss_ready", "len_ready", "r_ready", "r_summed", "tot_ready", "totals", "bn_var", "bn_std")}
        loaded = [s.sem(f"loaded{i}") for i in range(2)]
        r = K["r"]
        with nc.Block() as block:
            @block.sync
            def _(sp):
                def body(b, par, last):
                    sp.wait_ge(sem["adj_used"], b + 1)
                    sp.sem_inc(sem["issued"], 1)
                    for c in range(2):
                        hb = NB // 2
                        sp.dma_start(adjT[par][:, c * hb:(c + 1) * hb, :],
                                     graph(scratch["keptT"], b)[:, c * hb:(c + 1) * hb, :]).then_inc(loaded[par], 16)
                per_pair(sp, B, body)

            @block.tensor
            def _(pe):
                t = nc.tensor
                pe.sem_inc(sem["adj_used"], 2)

                def body(b, par, last):
                    pe.wait_ge(sem["h_ready"], b + 1)
                    for ib in range(NB):
                        mm = t.transpose(tp[:, ib * P:(ib + 1) * P], h[par][:, ib, :], K["ident"][:])
                    mm.then_inc(sem["tp_ready"], 1)
                    pe.wait_ge(loaded[par], (b - par) * 16 + 32)
                    for hf in range(NH):
                        for jb in range(NB):
                            mm = t.matmul(agg[:, hf * HALF:(hf + 1) * HALF], h[par][:, jb, :],
                                          adjT[par][:, jb, hf * HALF:(hf + 1) * HALF], start=(jb == 0), stop=(jb == NB - 1))
                        mm.then_inc(sem["agg_half"], 1)
                    pe.drain().then_inc(sem["adj_used"], 1)
                    pe.wait_ge(sem["hT_ready"], b + 1)
                    pe.wait_ge(sem["o_read"], b + 1)
                    if not first:
                        for ib in range(NB):
                            mm = t.matmul(o1[:, ib, :], hT[:, ib * P:(ib + 1) * P], K["Wl"][:, layer - 1, :], start=True, stop=True)
                        mm.then_inc(sem["y_ready"], 1)
                    for ib in range(NB):
                        mm = t.matmul(o2[:, ib, :], hT[:, ib * P:(ib + 1) * P], K[f"Wx{layer}"][:], start=True, stop=True)
                    mm.then_inc(sem["o2_ready"], 1)
                    if not first:
                        pe.wait_ge(sem["y_read"], b + 1)
                    for hf in range(NH):
                        pe.wait_ge(sem["aggT_half"], b * NH + hf + 1)
                        for ib in range(hf * HB, (hf + 1) * HB):
                            mm = t.matmul(o1[:, ib, :], aggT[:, ib * P:(ib + 1) * P], K[f"Wr{layer}"][:], start=True, stop=True)
                    mm.then_inc(sem["o1_ready"], 1)
                per_pair(pe, B, body)
                pe.wait_ge(sem["tot_ready"], 1)
                t.matmul(o1[:, 0:2, :], onesf[:], tot[:], start=True, stop=True).then_inc(sem["totals"], 1)

            @block.scalar
            def _(act):
                def body(b, par, last):
                    act.wait_ge(sem["tp_ready"], b + 1)
                    nc.scalar.activation(hT[:], tp[:], ACT.Copy).then_inc(sem["hT_ready"], 1)
                    if first and not last:
                        norm_root(nc, act, w, b + 1)
                    for hf in range(NH):
                        act.wait_ge(sem["agg_half"], b * NH + hf + 1)
                        sl = slice(hf * HALF, (hf + 1) * HALF)
                        nc.scalar.activation(aggT[:, sl], agg[:, sl], ACT.Copy).then_inc(sem["aggT_half"], 1)
                    act.wait_ge(sem["ss_ready"], b + 1)
                    nc.scalar.activation(nrm[:, 1, :], nrm[:, 0, :], ACT.Sqrt).then_inc(sem["len_ready"], 1)
                if first:
                    norm_root(nc, act, w, 0)
                per_pair(act, B, body)
                act.wait_ge(sem["bn_var"], 1)
                nc.scalar.activation(mv[:, 2, :], mv[:, 1, :], ACT.Sqrt).then_inc(sem["bn_std"], 1)

            @block.gpsimd
            def _(pool):
                g = nc.gpsimd
                g.memset(acc[:], 0.0)
                g.memset(onesf[:], 1.0)
                pool.drain()

                def body(b, par, last):
                    pool.wait_ge(sem["r_ready"], b + 1)
                    rb = tiles(r, b, NB)
                    g.tensor_tensor(rsq[:], rb, rb, ALU.mult)
                    g.tensor_tensor(acc[:, 0], acc[:, 0], rb, ALU.add)
                    pool.drain()
                    g.tensor_tensor(acc[:, 1], acc[:, 1], rsq[:], ALU.add)
                    pool.drain()
                per_pair(pool, B, body)
                pool.drain().then_inc(sem["r_summed"], 1)

            @block.vector
            def _(dve):
                v = nc.vector
                dve.sem_inc(sem["o_read"], 1)

                def prepare(b, par):
                    if first:
                        norm_relu_vector(nc, dve, tiles(K["X"], b, NB), h[par][:], w, b).then_inc(sem["h_ready"], 1)
                    else:
                        v.tensor_tensor(t1[:], tiles(r, b, NB), along_tiles(K["bnscale"][:], NB), ALU.mult)
                        dve.drain()
                        v.tensor_tensor(h[par][:], t1[:], along_tiles(K["bnshift"][:], NB), ALU.add).then_inc(sem["h_ready"], 1)
                    dve.drain()

                def finish(b, par):
                    cols = bass.ds(b * NB, NB)
                    if not first:
                        dve.wait_ge(sem["y_ready"], b + 1)
                        v.tensor_tensor(t1[:], o1[:], along_features(K["mask2"][:, cols], D), ALU.mult).then_inc(sem["y_read"], 1)
                        dve.drain()
                        v.tensor_tensor(tiles(K["X"], b, NB), tiles(K["X"], b, NB), t1[:], ALU.add)
                        dve.drain()
                    dve.wait_ge(sem["o2_ready"], b + 1)
                    v.tensor_tensor(o[:], o2[:], along_tiles(K["vec"][:, V_B1 + layer, :], NB), ALU.add)
                    dve.wait_ge(sem["o1_ready"], b + 1)
                    v.tensor_tensor(t1[:], o1[:], along_features(K["rdeg"][:, cols], D), ALU.mult)
                    dve.drain().then_inc(sem["o_read"], 1)
                    v.tensor_tensor(o[:], o[:], t1[:], ALU.add)
                    dve.drain()
                    v.tensor_tensor(t1[:], o[:], o[:], ALU.mult)
                    dve.drain()
                    v.tensor_reduce(nrm[:, 0, :], t1[:], AX, ALU.add).then_inc(sem["ss_ready"], 1)
                    dve.wait_ge(sem["len_ready"], b + 1)
                    v.tensor_scalar(nrm[:, 2, :], nrm[:, 1, :], NORM_EPS, None, ALU.max)
                    dve.drain()
                    v.reciprocal(nrm[:, 3, :], nrm[:, 2, :])
                    dve.drain()
                    v.tensor_tensor(nrm[:, 4, :], nrm[:, 3, :], K["mask"][:, cols], ALU.mult)
                    dve.drain()
                    v.tensor_tensor(t1[:], o[:], along_features(nrm[:, 4, :], D), ALU.mult)
                    dve.drain()
                    v.tensor_scalar(tiles(r, b, NB), t1[:], 0.0, None, ALU.max).then_inc(sem["r_ready"], 1)
                    dve.drain()

                prepare(0, 0)

                def body(b, par, last):
                    if not last:
                        prepare(b + 1, 1 - par)
                    finish(b, par)
                per_pair(dve, B, body)
                dve.wait_ge(sem["r_summed"], 1)
                for i in range(2):
                    last = v.tensor_reduce(tot[:, i, :], acc[:, i].rearrange("p t d -> p d t"), AX, ALU.add)
                last.then_inc(sem["tot_ready"], 1)
                dve.wait_ge(sem["totals"], 1)
                n_all = float(B * N)
                v.tensor_scalar(mv[:, 0, :], o1[:, 0, :], 1.0 / n_all, None, ALU.mult)
                v.tensor_scalar(mv[:, 1, :], o1[:, 1, :], 1.0 / n_all, None, ALU.mult)
                dve.drain()
                v.tensor_tensor(mv[:, 2, :], mv[:, 0, :], mv[:, 0, :], ALU.mult)
                dve.drain()
                v.tensor_tensor(mv[:, 1, :], mv[:, 1, :], mv[:, 2, :], ALU.subtract)
                dve.drain()
                v.tensor_scalar(mv[:, 1, :], mv[:, 1, :], BN_EPS, None, ALU.add).then_inc(sem["bn_var"], 1)
                dve.wait_ge(sem["bn_std"], 1)
                v.reciprocal(mv[:, 3, :], mv[:, 2, :])
                dve.drain()
                v.tensor_tensor(K["bnscale"][:], mv[:, 3, :], K["vec"][:, V_G1 + layer, :], ALU.mult)
                dve.drain()
                v.tensor_tensor(mv[:, 1, :], mv[:, 0, :], K["bnscale"][:], ALU.mult)
                dve.drain()
                v.tensor_tensor(K["bnshift"][:], K["vec"][:, V_E1 + layer, :], mv[:, 1, :], ALU.subtract)


def gcn_phase(nc, z, A, K):
    B, N, NB, NH, HB, D = z.B, z.N, z.NB, z.NH, z.HB, z.D
    with Scope(nc, "gcn") as s:
        adjT = [s.sb(f"adjT{i}", [P, NB, N], F32) for i in range(2)]
        h = s.sb("h", [P, NB, D], F32)
        hT = s.sb("hT", [P, N], F32)
        h3 = s.sb("h3", [P, NB, D], F32)
        t1 = s.sb("t1", [P, NB, D], F32)
        y = s.sb("y", [P, 4, D], F32)
        sup = [s.sb(f"sup{i}", [P, NB, D], F32) for i in range(2)]
        dinv = s.sb("dinv", [P, z.T], F32)
        dw = s.sb("dw", [P, 3, z.T], F32)
        w = norm_buffers(s.sb, s.sem, "n", NB, D)
        tp = s.ps("tp", [P, N])
        pr = s.ps("pr", [P, NB, D])
        acc = [s.ps(f"acc{i}", [P, 4, D]) for i in range(4)]
        sem = {n: s.sem(n) for n in (
            "adj_used", "issued", "h_ready", "tp_ready", "hT_ready", "pr_ready", "sup_ready", "sums_ready", "sums_read",
            "deg_ready", "dinv_ready")}
        loaded = [s.sem(f"loaded{i}") for i in range(2)]
        QB = NB // 4
        with nc.Block() as block:
            @block.sync
            def _(sp):
                def body(b, par, last):
                    sp.wait_ge(sem["adj_used"], b + 1)
                    sp.sem_inc(sem["issued"], 1)
                    for c in range(2):
                        hb = NB // 2
                        sp.dma_start(adjT[par][:, c * hb:(c + 1) * hb, :],
                                     graph(A["adj_cols"], b)[:, c * hb:(c + 1) * hb, :]).then_inc(loaded[par], 16)
                per_pair(sp, B, body)

            @block.tensor
            def _(pe):
                t = nc.tensor
                pe.sem_inc(sem["adj_used"], 2)

                def project(n, src, weight):
                    pe.wait_ge(sem["h_ready"], n + 1)
                    for ib in range(NB):
                        mm = t.transpose(tp[:, ib * P:(ib + 1) * P], src[:, ib, :], K["ident"][:])
                    mm.then_inc(sem["tp_ready"], 1)
                    pe.wait_ge(sem["hT_ready"], n + 1)
                    for ib in range(NB):
                        mm = t.matmul(pr[:, ib, :], hT[:, ib * P:(ib + 1) * P], weight, start=True, stop=True)
                    mm.then_inc(sem["pr_ready"], 1)

                def prepare(b):
                    project(b * 2, h3, K["Wl"][:, 2, :])
                    project(b * 2 + 1, h, K["W2"][:])

                prepare(0)

                def body(b, par, last):
                    pe.wait_ge(sem["sup_ready"], b + 1)
                    pe.wait_ge(loaded[par], (b - par) * 16 + 32)
                    for k in range(QB):
                        a = acc[(par * QB + k) % 4]
                        pe.wait_ge(sem["sums_read"], b * QB + k + 1)
                        for e in range(4):
                            ib = 4 * k + e
                            for jb in range(NB):
                                mm = t.matmul(a[:, e, :], adjT[par][:, jb, ib * P:(ib + 1) * P], sup[par][:, jb, :],
                                              start=(jb == 0), stop=(jb == NB - 1))
                        mm.then_inc(sem["sums_ready"], 1)
                        if k == 0 and not last:
                            prepare(b + 1)
                    pe.drain().then_inc(sem["adj_used"], 1)
                per_pair(pe, B, body)

            @block.scalar
            def _(act):
                act.wait_ge(sem["deg_ready"], 1)
                nc.scalar.activation(dinv[:], dw[:, 1, :], ACT.Sqrt).then_inc(sem["dinv_ready"], 1)

                def body(b, par, last):
                    for k in range(2):
                        act.wait_ge(sem["tp_ready"], b * 2 + k + 1)
                        nc.scalar.activation(hT[:], tp[:], ACT.Copy).then_inc(sem["hT_ready"], 1)
                        if k == 0:
                            norm_root(nc, act, w, b)
                per_pair(act, B, body)

            @block.vector
            def _(dve):
                v = nc.vector
                dve.sem_inc(sem["sums_read"], 4)
                v.tensor_scalar(dw[:, 0, :], K["rowsum"][:], 1.0, None, ALU.add)
                dve.drain()
                v.tensor_scalar(dw[:, 2, :], dw[:, 0, :], 0.0, None, ALU.is_equal)
                dve.drain()
                v.tensor_tensor(dw[:, 0, :], dw[:, 0, :], dw[:, 2, :], ALU.add)
                dve.drain()
                v.reciprocal(dw[:, 1, :], dw[:, 0, :]).then_inc(sem["deg_ready"], 1)
                v.tensor_scalar(dw[:, 2, :], dw[:, 2, :], -1.0, 1.0, ALU.mult, ALU.add)
                dve.wait_ge(sem["dinv_ready"], 1)
                dve.drain()
                v.tensor_tensor(dinv[:], dinv[:], dw[:, 2, :], ALU.mult)
                dve.drain()

                def prepare(b, par):
                    x = tiles(K["X"], b, NB)
                    cols = bass.ds(b * NB, NB)
                    v.tensor_tensor(t1[:], tiles(K["r"], b, NB), along_tiles(K["bnscale"][:], NB), ALU.mult)
                    dve.drain()
                    v.tensor_tensor(h3[:], t1[:], along_tiles(K["bnshift"][:], NB), ALU.add).then_inc(sem["h_ready"], 1)
                    dve.drain()
                    v.tensor_tensor(t1[:], along_tiles(K["vec"][:, V_BL, :], NB), along_features(K["mask"][:, cols], D), ALU.mult)
                    dve.drain()
                    v.tensor_tensor(x, x, t1[:], ALU.add)
                    dve.drain()
                    dve.wait_ge(sem["pr_ready"], b * 2 + 1)
                    v.tensor_tensor(t1[:], pr[:], along_features(K["mask2"][:, cols], D), ALU.mult)
                    dve.drain()
                    v.tensor_tensor(x, x, t1[:], ALU.add)
                    dve.drain()
                    norm_relu_vector(nc, dve, x, h[:], w, b).then_inc(sem["h_ready"], 1)
                    dve.wait_ge(sem["pr_ready"], b * 2 + 2)
                    v.tensor_tensor(sup[par][:], pr[:], along_features(dinv[:, cols], D), ALU.mult)
                    dve.drain().then_inc(sem["sup_ready"], 1)

                def finish(b, par):
                    for k in range(QB):
                        a = acc[(par * QB + k) % 4]
                        dve.wait_ge(sem["sums_ready"], b * QB + k + 1)
                        cols = bass.ds(b * NB + 4 * k, 4)
                        xs = K["X"][:, cols]
                        v.tensor_tensor(y[:], a[:], sup[par][:, 4 * k:4 * k + 4, :], ALU.add)
                        dve.drain().then_inc(sem["sums_read"], 1)
                        v.tensor_tensor(y[:], y[:], along_features(dinv[:, cols], D), ALU.mult)
                        dve.drain()
                        v.tensor_tensor(y[:], y[:], along_tiles(K["vec"][:, V_BIAS2, :], 4), ALU.add)
                        dve.drain()
                        v.tensor_tensor(xs, xs, y[:], ALU.add)
                        dve.drain()

                prepare(0, 0)

                def body(b, par, last):
                    if not last:
                        prepare(b + 1, 1 - par)
                    finish(b, par)
                per_pair(dve, B, body)


def maxdeg_phase(nc, z, A, K, scratch, out):
    B, N, NB, NH, HB, D = z.B, z.N, z.NB, z.NH, z.HB, z.D
    with Scope(nc, "l3") as s:
        rowbin = [s.sb(f"rowbin{i}", [P, NB, N], BF16) for i in range(2)]
        h = s.sb("h", [P, NB, D], F32)
        rest = s.sb("rest", [P, NB, D], F32)
        parts = [s.sb(f"parts{i}", [P, 3, NB, D], BF16) for i in range(2)]
        aggT = s.sb("aggT", [P, N], F32)
        y = s.sb("y", [P, NB, D], F32)
        res = [s.sb(f"res{i}", [P, NB, D], F32) for i in range(2)]
        rcol = s.sb("rcol", [P, z.T], F32)
        w = norm_buffers(s.sb, s.sem, "n", NB, D)
        agg = [s.ps(f"agg{i}", [P, N]) for i in range(2)]
        pr = s.ps("pr", [P, NB, D])
        sem = {n: s.sem(n) for n in (
            "in_used", "issued", "h_ready", "agg_half", "aggT_half", "pr_ready", "pr_read", "res_ready", "res_free", "stored")}
        loaded = [s.sem(f"loaded{i}") for i in range(2)]
        with nc.Block() as block:
            @block.sync
            def _(sp):
                def body(b, par, last):
                    sp.wait_ge(sem["in_used"], b + 1)
                    sp.sem_inc(sem["issued"], 1)
                    sp.dma_start(rowbin[par][:], graph(scratch["rowbin"], b)).then_inc(loaded[par], 16)
                per_pair(sp, B, body)

            @block.gpsimd
            def _(pool):
                pool.sem_inc(sem["res_free"], 2)

                def body(b, par, last):
                    pool.wait_ge(sem["res_ready"], b + 1)
                    pool.dma_start(graph(out, b), res[par][:]).then_inc(sem["stored"], 16)
                    pool.wait_ge(sem["stored"], b * 16 + 16)
                    pool.sem_inc(sem["res_free"], 1)
                per_pair(pool, B, body)

            @block.tensor
            def _(pe):
                t = nc.tensor
                pe.sem_inc(sem["in_used"], 2)

                def body(b, par, last):
                    pe.wait_ge(sem["h_ready"], b + 1)
                    pe.wait_ge(loaded[par], (b - par) * 8 + 16)
                    for hf in range(NH):
                        sl = slice(hf * HALF, (hf + 1) * HALF)
                        for jb in range(NB):
                            for q in range(3):
                                mm = t.matmul(agg[par][:, sl], parts[par][:, q, jb, :], rowbin[par][:, jb, sl],
                                              start=(jb == 0 and q == 0), stop=(jb == NB - 1 and q == 2))
                        mm.then_inc(sem["agg_half"], 1)
                    pe.drain().then_inc(sem["in_used"], 1)
                    pe.wait_ge(sem["pr_read"], b + 1)
                    for hf in range(NH):
                        pe.wait_ge(sem["aggT_half"], b * NH + hf + 1)
                        for ib in range(hf * HB, (hf + 1) * HB):
                            mm = t.matmul(pr[:, ib, :], aggT[:, ib * P:(ib + 1) * P], K["U"][:], start=True, stop=True)
                    mm.then_inc(sem["pr_ready"], 1)
                per_pair(pe, B, body)

            @block.scalar
            def _(act):
                norm_root(nc, act, w, 0)

                def body(b, par, last):
                    if not last:
                        norm_root(nc, act, w, b + 1)
                    for hf in range(NH):
                        act.wait_ge(sem["agg_half"], b * NH + hf + 1)
                        sl = slice(hf * HALF, (hf + 1) * HALF)
                        act.wait_ge(sem["pr_read"], b + 1)
                        nc.scalar.activation(aggT[:, sl], agg[par][:, sl], ACT.Copy).then_inc(sem["aggT_half"], 1)
                per_pair(act, B, body)

            @block.vector
            def _(dve):
                v = nc.vector
                dve.sem_inc(sem["pr_read"], 1)
                v.reciprocal(rcol[:], K["colsum"][:])

                def prepare(b, par):
                    pt = parts[par]
                    norm_relu_vector(nc, dve, tiles(K["X"], b, NB), h[:], w, b)
                    dve.drain()
                    v.tensor_copy(pt[:, 0], h[:])
                    dve.drain()
                    v.tensor_tensor(rest[:], h[:], pt[:, 0], ALU.subtract)
                    dve.drain()
                    v.tensor_copy(pt[:, 1], rest[:])
                    dve.drain()
                    v.tensor_tensor(pt[:, 2], rest[:], pt[:, 1], ALU.subtract).then_inc(sem["h_ready"], 1)
                    dve.drain()

                def finish(b, par):
                    cols = bass.ds(b * NB, NB)
                    dve.wait_ge(sem["pr_ready"], b + 1)
                    v.tensor_tensor(y[:], pr[:], along_features(rcol[:, cols], D), ALU.mult)
                    dve.drain().then_inc(sem["pr_read"], 1)
                    dve.wait_ge(sem["res_free"], b + 1)
                    v.scalar_tensor_tensor(res[par][:], y[:], 0.0, tiles(K["X"], b, NB), ALU.max, ALU.add)\
                        .then_inc(sem["res_ready"], 1)
                    dve.drain()

                prepare(0, 0)

                def body(b, par, last):
                    if not last:
                        prepare(b + 1, 1 - par)
                    finish(b, par)
                per_pair(dve, B, body)


def build_program(nc, A, out):
    z = Shapes(A["x"], A["adj_rows"])
    B, N, D, T = z.B, z.N, z.D, z.T
    scratch = {"rowbin": nc.dram_tensor("rowbin", (B, N, N), BF16, kind="Internal").ap(),
               "curT": nc.dram_tensor("curT", (B, N, N), BF16, kind="Internal").ap(),
               "keptT": nc.dram_tensor("keptT", (B, N, N), F32, kind="Internal").ap()}
    with ExitStack() as ctx:
        K = {}

        def resident(name, shape, dt=F32):
            K[name] = ctx.enter_context(nc.sbuf_tensor(f"k_{name}", shape, dt))
        resident("X", [P, T, D])
        for n in ("Wr0", "Wr1", "Wr2", "Wx0", "Wx1", "Wx2", "W2", "U", "ident"):
            resident(n, [P, P])
        resident("Wl", [P, 3, D])
        resident("vec", [P, NVEC, D])
        resident("av", [P, 2, D])
        resident("ac", [P, 3])
        resident("onescol", [P, 2])
        for n in ("mask", "mask2", "maskok", "rowsum", "colsum", "rdeg", "rscale", "rbias", "rdist"):
            resident(n, [P, T])
        resident("bnscale", [P, D])
        resident("bnshift", [P, D])
        resident("ident16", [P, P], BF16)
        resident("ones16", [P, 2], BF16)
        resident("upper", [P, P], BF16)
        resident("tri", [P, N], BF16)
        constants_phase(nc, z, A, K)
        attention_phase(nc, z, A, K)
        removal_phase(nc, z, A, K, scratch)
        keep_phase(nc, z, A, K, scratch)
        resident("r", [P, T, D])
        for layer in range(3):
            sage_phase(nc, z, A, K, scratch, layer)
        gcn_phase(nc, z, A, K)
        maxdeg_phase(nc, z, A, K, scratch, out)


_VECTORS = ["L0_gnn_W_w", "L0_gnn_W_b", "L0_gnn_a_w", "L0_gnn_a_b", "L1_gnn_Wr1", "L1_gnn_Wx1", "L1_gnn_b1", "L1_gnn_g1",
            "L1_gnn_be1", "L1_gnn_Wr2", "L1_gnn_Wx2", "L1_gnn_b2", "L1_gnn_g2", "L1_gnn_be2", "L1_gnn_Wr3", "L1_gnn_Wx3",
            "L1_gnn_b3", "L1_gnn_g3", "L1_gnn_be3", "L1_gnn_Wl", "L1_gnn_bl", "L2_gnn_weight", "L2_gnn_bias", "L3_gnn_U"]


def kernel(**inputs):
    import numpy as _np
    import concourse.bacc as _bacc
    from concourse import mybir as _mybir
    from concourse.bass_utils import run_bass_kernel_spmd as _run

    nc = _bacc.Bacc("TRN2", target_bir_lowering=False, num_devices=1)
    arrays = {"x": _np.ascontiguousarray(inputs["x"]), "nodemask": _np.ascontiguousarray(inputs["nodemask"]),
              "adj_rows": _np.ascontiguousarray(inputs["adj"]),
              "adj_cols": _np.ascontiguousarray(_np.asarray(inputs["adj"]).transpose(0, 2, 1))}
    for name in _VECTORS:
        arrays[name] = _np.ascontiguousarray(inputs[name])
        if arrays[name].ndim == 0:
            arrays[name] = arrays[name].reshape(1)
    A, feed = {}, {}
    for name, a in arrays.items():
        A[name] = nc.dram_tensor(f"in_{name}", a.shape, _mybir.dt.from_np(a.dtype), kind="ExternalInput").ap()
        feed[f"in_{name}"] = a
    out = nc.dram_tensor("out_x", arrays["x"].shape, F32, kind="ExternalOutput").ap()
    build_program(nc, A, out)
    r = _run(nc, [feed], core_ids=[0])
    return r.results[0]["out_x"]
```

```python
from contextlib import ExitStack

import concourse.bass as bass
from concourse import mybir

ALU = mybir.AluOpType
ACT = mybir.ActivationFunctionType
F32 = mybir.dt.float32
BF16 = mybir.dt.bfloat16
F16 = mybir.dt.float16
I32 = mybir.dt.int32
AX = mybir.AxisListType.X

P = 128
HALF = 512
LN_EPS = 1e-5
BN_EPS = 1e-5
NORM_EPS = 1e-12
DENSE_ROW = 10.0
FAST_ROUNDS = 4
ROUND = float(2 ** 23)

(V_WB, V_B1, V_B2, V_B3, V_BL, V_G1, V_G2, V_G3, V_E1, V_E2, V_E3, V_BIAS2) = range(12)
NVEC = 12


class Shapes:
    def __init__(self, x, adj):
        self.B, self.N, self.D = x.shape
        self.NB = self.N // P
        self.T = self.B * self.NB
        self.NH = self.N // HALF
        self.HB = HALF // P
        assert self.D == P and self.B % 2 == 0 and self.N % HALF == 0


def per_pair(engine, B, body):
    if B > 2:
        with engine.Fori(0, B // 2 - 1) as g:
            for parity in range(2):
                body(g * 2 + parity, parity, False)
    for parity in range(2):
        body(B - 2 + parity, parity, parity == 1)


def block_rows(tensor3, b, nb):
    g = tensor3[b] if isinstance(b, int) else tensor3[bass.ds(b, 1)].rearrange("o m n -> (o m) n")
    return g[nb * P:(nb + 1) * P, :]


def graph(tensor3, b):
    if isinstance(b, int):
        return tensor3[b].rearrange("(t p) n -> p t n", p=P)
    return tensor3[bass.ds(b, 1)].rearrange("o (t p) n -> p (o t) n", p=P)


def tiles(tensor, b, nb):
    return tensor[:, bass.ds(b * nb, nb)] if not isinstance(b, int) else tensor[:, b * nb:(b + 1) * nb]


def along_features(col, d):
    return col.unsqueeze(2).to_broadcast([P, col.shape[1], d])


def along_tiles(row, t):
    return row.unsqueeze(1).to_broadcast([P, t, row.shape[1]])


def norm_relu_vector(nc, dve, x, out, w, b):
    s, v = w["stat"], nc.vector
    D = x.shape[2]
    v.tensor_reduce(s[:, 0, :], x, AX, ALU.add)
    dve.drain()
    v.tensor_scalar(s[:, 1, :], s[:, 0, :], -1.0 / D, None, ALU.mult)
    dve.drain()
    v.tensor_tensor(w["centred"][:], x, along_features(s[:, 1, :], D), ALU.add)
    dve.drain()
    v.tensor_tensor(w["squared"][:], w["centred"][:], w["centred"][:], ALU.mult)
    dve.drain()
    v.tensor_reduce(s[:, 2, :], w["squared"][:], AX, ALU.add)
    dve.drain()
    v.tensor_scalar(s[:, 3, :], s[:, 2, :], 1.0 / D, LN_EPS, ALU.mult, ALU.add).then_inc(w["var_ready"], 1)
    dve.wait_ge(w["std_ready"], b + 1)
    v.reciprocal(s[:, 5, :], s[:, 4, :])
    dve.drain()
    return v.scalar_tensor_tensor(out, w["centred"][:], 0.0, along_features(s[:, 5, :], D), ALU.max, ALU.mult)


def norm_root(nc, act, w, b):
    act.wait_ge(w["var_ready"], b + 1)
    nc.scalar.activation(w["stat"][:, 4, :], w["stat"][:, 3, :], ACT.Sqrt).then_inc(w["std_ready"], 1)


def norm_buffers(sb, sem, tag, NB, D):
    return dict(stat=sb(f"{tag}_stat", [P, 6, NB], F32), centred=sb(f"{tag}_centred", [P, NB, D], F32),
                squared=sb(f"{tag}_squared", [P, NB, D], F32),
                var_ready=sem(f"{tag}_var_ready"), std_ready=sem(f"{tag}_std_ready"))


class Scope:

    def __init__(self, nc, tag):
        self.nc, self.tag, self.stack = nc, tag, ExitStack()
        self.sems = []

    def __enter__(self):
        self.stack.__enter__()
        return self

    def __exit__(self, *e):
        if e[0] is None:
            self.nc.clear_and_free_semaphores(self.sems)
            self.nc.all_engine_barrier(sem_only=True)
        return self.stack.__exit__(*e)

    def sb(self, name, shape, dt):
        return self.stack.enter_context(self.nc.sbuf_tensor(f"{self.tag}_{name}", shape, dt))

    def ps(self, name, shape, dt=F32):
        return self.stack.enter_context(self.nc.psum_tensor(f"{self.tag}_{name}", shape, dt))

    def sem(self, name):
        self.sems.append(self.nc.alloc_semaphore(f"{self.tag}_{name}"))
        return self.sems[-1]


def constants_phase(nc, z, A, K):
    D, T, B = z.D, z.T, z.B
    with Scope(nc, "con") as s:
        rows = s.sb("rows", [1, NVEC, D], F32)
        ab = s.sb("ab", [1, 1], F32)
        ones1 = s.sb("ones1", [1, P], F32)
        onesf = s.sb("onesf", [P, P], F32)
        acol = s.sb("acol", [P, 2], F32)
        abc = s.sb("abc", [P, 2, P], F32)
        wbcol = s.sb("wbcol", [P, 1], F32)
        Ww = s.sb("Ww", [P, D], F32)
        maski = s.sb("maski", [T, P], I32)
        maskf = s.sb("maskf", [T, P], F32)
        pm = s.ps("pm", [P, T])
        pbig = [s.ps(f"pbig{i}", [P, 512]) for i in range(3)]
        pv = s.ps("pv", [P, 2, D])
        pc = s.ps("pc", [P, 4])
        loaded, set0, const_ready = s.sem("loaded"), s.sem("set0"), s.sem("const_ready")
        rows_spread, abc_ready, v_done = s.sem("rows_spread"), s.sem("abc_ready"), s.sem("v_done")
        mask_ready, mask_turned = s.sem("mask_ready"), s.sem("mask_turned")
        vecs = [(A["L0_gnn_W_b"], V_WB), (A["L1_gnn_b1"], V_B1), (A["L1_gnn_b2"], V_B2), (A["L1_gnn_b3"], V_B3),
                (A["L1_gnn_bl"], V_BL), (A["L1_gnn_g1"], V_G1), (A["L1_gnn_g2"], V_G2), (A["L1_gnn_g3"], V_G3),
                (A["L1_gnn_be1"], V_E1), (A["L1_gnn_be2"], V_E2), (A["L1_gnn_be3"], V_E3), (A["L2_gnn_bias"], V_BIAS2)]
        weights = [("Wr0", A["L1_gnn_Wr1"]), ("Wr1", A["L1_gnn_Wr2"]), ("Wr2", A["L1_gnn_Wr3"]),
                   ("Wx0", A["L1_gnn_Wx1"]), ("Wx1", A["L1_gnn_Wx2"]), ("Wx2", A["L1_gnn_Wx3"]),
                   ("W2", A["L2_gnn_weight"]), ("U", A["L3_gnn_U"])]
        n_loads = len(vecs) + len(weights) + 8
        with nc.Block() as block:
            @block.sync
            def _(sp):
                for src, i in vecs:
                    sp.dma_start(rows[:, i, :], src.rearrange("(o d) -> o d", o=1)).then_inc(loaded, 16)
                sp.dma_start(ab[:], A["L0_gnn_a_b"].rearrange("(o d) -> o d", o=1)).then_inc(loaded, 16)
                for i in range(2):
                    sp.dma_start(acol[:, i:i + 1], A["L0_gnn_a_w"][i * P:(i + 1) * P].rearrange("(p o) -> p o", o=1))\
                        .then_inc(loaded, 16)
                sp.dma_start(wbcol[:], A["L0_gnn_W_b"].rearrange("(p o) -> p o", o=1)).then_inc(loaded, 16)
                sp.dma_start(Ww[:], A["L0_gnn_W_w"]).then_inc(loaded, 16)
                for name, src in weights:
                    sp.dma_start(K[name][:], src).then_inc(loaded, 16)
                sp.dma_start(K["Wl"][:], A["L1_gnn_Wl"].rearrange("(t p) e -> p t e", p=P)).then_inc(loaded, 16)
                sp.dma_start(maski[:], A["nodemask"].rearrange("b (t p) -> (b t) p", p=P)).then_inc(loaded, 16)
                sp.dma_start(K["X"][:], A["x"].rearrange("b (t p) d -> p (b t) d", p=P)).then_inc(loaded, 16)

            @block.gpsimd
            def _(pool):
                p = nc.gpsimd
                p.memset(K["ident"][:], 0.0)
                p.memset(K["ident16"][:], 0.0)
                p.memset(K["tri"][:], 1.0)
                p.memset(K["upper"][:], 1.0)
                p.memset(K["ones16"][:], 1.0)
                p.memset(onesf[:], 1.0)
                p.memset(K["onescol"][:], 1.0)
                p.memset(ones1[:], 1.0).then_inc(set0, 1)
                pool.wait_ge(set0, 1)
                for m in (K["ident"], K["ident16"]):
                    p.affine_select(out=m[:], in_=m[:], compare_op=ALU.not_equal, fill=1.0, base=0,
                                    pattern=[[-1, P]], channel_multiplier=1)
                p.affine_select(out=K["tri"][:], in_=K["tri"][:], compare_op=ALU.is_ge, fill=0.0, base=0,
                                pattern=[[1, z.N]], channel_multiplier=-1)
                p.affine_select(out=K["upper"][:], in_=K["upper"][:], compare_op=ALU.is_ge, fill=0.0, base=-1,
                                pattern=[[1, P]], channel_multiplier=-1).then_inc(const_ready, 1)

            @block.tensor
            def _(pe):
                pe.wait_ge(const_ready, 1)
                pe.wait_ge(loaded, 16 * n_loads)
                flat = rows[:].rearrange("o v d -> o (v d)")
                for i in range(3):
                    nc.tensor.matmul(pbig[i][:], ones1[:], flat[:, i * 512:(i + 1) * 512], start=True, stop=True)
                nc.tensor.matmul(pc[:, 2:3], ones1[:], ab[:], start=True, stop=True).then_inc(rows_spread, 1)
                pe.wait_ge(mask_ready, 1)
                nc.tensor.transpose(pm[:], maskf[:], K["ident"][0:T, 0:T]).then_inc(mask_turned, 1)
                pe.wait_ge(abc_ready, 1)
                for h in range(2):
                    nc.tensor.matmul(pv[:, h, :], abc[:, h, :], Ww[:], start=True, stop=True)
                    last = nc.tensor.matmul(pc[:, h:h + 1], abc[:, h, :], wbcol[:], start=True, stop=True)
                last.then_inc(v_done, 1)

            @block.vector
            def _(dve):
                v = nc.vector
                dve.wait_ge(const_ready, 1)
                dve.wait_ge(loaded, 16 * n_loads)
                for h in range(2):
                    last = v.tensor_scalar(abc[:, h, :], onesf[:], acol[:, h:h + 1], None, ALU.mult)
                last.then_inc(abc_ready, 1)
                v.tensor_copy(maskf[:], maski[:]).then_inc(mask_ready, 1)
                dve.wait_ge(mask_turned, 1)
                v.tensor_copy(K["mask"][:], pm[:])
                dve.drain()
                v.tensor_tensor(K["mask2"][:], K["mask"][:], K["mask"][:], ALU.mult)
                v.tensor_scalar(K["maskok"][:], K["mask"][:], 0.0, None, ALU.not_equal)
                dve.wait_ge(rows_spread, 1)
                for i in range(3):
                    v.tensor_copy(K["vec"][:, 4 * i:4 * i + 4, :].rearrange("p v d -> p (v d)"), pbig[i][:])
                dve.wait_ge(v_done, 1)
                v.tensor_copy(K["av"][:], pv[:])
                v.tensor_copy(K["ac"][:], pc[:, 0:3])
                dve.drain()
                v.tensor_tensor(K["ac"][:, 0:1], K["ac"][:, 0:1], K["ac"][:, 2:3], ALU.add)


def attention_phase(nc, z, A, K):
    B, N, NB, D = z.B, z.N, z.NB, z.D
    W = D + 2
    with Scope(nc, "att") as s:
        adjT = [s.sb(f"adjT{i}", [P, NB, N], F32) for i in range(2)]
        rhs = [s.sb(f"rhs{i}", [P, NB, W], F32) for i in range(2)]
        G = [s.sb(f"G{i}", [P, NB], F32) for i in range(2)]
        h = s.sb("h", [P, NB, D], F32)
        t1 = s.sb("t1", [P, NB, D], F32)
        sj = s.sb("sj", [P, 2, NB], F32)
        E = s.sb("E", [P, NB], F32)
        y = s.sb("y", [P, 2, D], F32)
        q = s.sb("q", [P, 4, 2], F32)
        w = norm_buffers(s.sb, s.sem, "n", NB, D)
        acc = [s.ps(f"acc{i}", [P, 2, 256]) for i in range(4)]
        adj_loaded = [s.sem(f"adj_loaded{i}") for i in range(2)]
        issued, adj_summed = s.sem("issued"), s.sem("adj_summed")
        junk = s.sb("junk", [P, N], BF16)
        adj_used, score_ready, exp_ready = s.sem("adj_used"), s.sem("score_ready"), s.sem("exp_ready")
        rhs_ready, sums_ready, sums_read = s.sem("rhs_ready"), s.sem("sums_ready"), s.sem("sums_read")
        QB = NB // 2
        with nc.Block() as block:
            @block.sync
            def _(sp):
                def body(b, par, last):
                    sp.wait_ge(adj_summed, b + 1)
                    sp.sem_inc(issued, 1)
                    sp.wait_ge(adj_used, b + 1)
                    sp.sem_inc(issued, 1)
                    for c in range(2):
                        hb = NB // 2
                        sp.dma_start(adjT[par][:, c * hb:(c + 1) * hb, :],
                                     graph(A["adj_cols"], b)[:, c * hb:(c + 1) * hb, :]).then_inc(adj_loaded[par], 16)
                per_pair(sp, B, body)

            @block.tensor
            def _(pe):
                pe.sem_inc(adj_used, 2)

                def body(b, par, last):
                    g = (b - par) if isinstance(b, int) else b - par
                    pe.wait_ge(rhs_ready, b + 1)
                    pe.wait_ge(adj_loaded[par], g * 16 + 32)
                    for k in range(QB):
                        pe.wait_ge(sums_read, b * QB + k + 1)
                        for e in range(2):
                            ib = 2 * k + e
                            for jb in range(NB):
                                mm = nc.tensor.matmul(acc[k % 4][:, e, 0:W], adjT[par][:, jb, ib * P:(ib + 1) * P],
                                                      rhs[par][:, jb, :], start=(jb == 0), stop=(jb == NB - 1))
                        mm.then_inc(sums_ready, 1)
                    pe.drain().then_inc(adj_used, 1)
                per_pair(pe, B, body)

            @block.scalar
            def _(act):
                def body(b, par, last):
                    act.wait_ge(adj_loaded[par], (b - par) * 16 + 32)
                    for jb in range(NB):
                        nc.scalar.activation(junk[:], adjT[par][:, jb, :], ACT.Copy,
                                             accum_out=K["colsum"][:, bass.ds(b * NB + jb, 1)])
                        act.drain()
                        if not last and jb == NB // 2 - 1:
                            scores(b + 1, 1 - par)
                    act.sem_inc(adj_summed, 1)

                def scores(b, par):
                    norm_root(nc, act, w, b)
                    act.wait_ge(score_ready, b + 1)
                    nc.scalar.activation(G[par][:], sj[:, 0, :], ACT.Exp, bias=K["ac"][:, 0:1])
                    nc.scalar.activation(E[:], sj[:, 1, :], ACT.Exp, bias=K["ac"][:, 1:2]).then_inc(exp_ready, 1)
                act.sem_inc(adj_summed, 2)
                scores(0, 0)
                per_pair(act, B, body)

            @block.vector
            def _(dve):
                v = nc.vector
                dve.sem_inc(sums_read, 4)
                for r in rhs:
                    v.memset(r[:, :, D + 1:D + 2], 1.0)

                def prepare(b, par):
                    norm_relu_vector(nc, dve, tiles(K["X"], b, NB), h[:], w, b)
                    dve.drain()
                    for k in range(2):
                        v.tensor_tensor(t1[:], h[:], along_tiles(K["av"][:, k, :], NB), ALU.mult)
                        dve.drain()
                        last = v.tensor_reduce(sj[:, k, :], t1[:], AX, ALU.add)
                        if k == 0:
                            dve.drain()
                    last.then_inc(score_ready, 1)
                    dve.wait_ge(exp_ready, b + 1)
                    v.tensor_copy(rhs[par][:, :, D], E[:])
                    v.tensor_tensor(rhs[par][:, :, 0:D], h[:], along_features(E[:], D), ALU.mult).then_inc(rhs_ready, 1)

                def finish(b, par):
                    for k in range(QB):
                        a = acc[k % 4]
                        xs = K["X"][:, bass.ds(b * NB + 2 * k, 2)]
                        dve.wait_ge(sums_ready, b * QB + k + 1)
                        v.tensor_copy(K["rowsum"][:, bass.ds(b * NB + 2 * k, 2)], a[:, :, D + 1])
                        g = G[par][:, 2 * k:2 * k + 2]
                        v.tensor_tensor(q[:, 0, :], a[:, :, D], g, ALU.mult)
                        dve.drain()
                        v.reciprocal(q[:, 1, :], q[:, 0, :])
                        dve.drain()
                        v.tensor_tensor(q[:, 2, :], q[:, 1, :], g, ALU.mult)
                        dve.drain()
                        v.tensor_tensor(y[:], a[:, :, 0:D], along_features(q[:, 2, :], D), ALU.mult).then_inc(sums_read, 1)
                        dve.drain()
                        v.tensor_tensor(xs, xs, y[:], ALU.add)
                        dve.drain()

                prepare(0, 0)

                def body(b, par, last):
                    if not last:
                        prepare(b + 1, 1 - par)
                    finish(b, par)
                per_pair(dve, B, body)


def removal_parameters(nc, dve, k, num0, off, maskok, w, with_rank_shift, out=None):
    v = nc.vector
    scale, bias, dist = out if out else (w[:, 0], w[:, 1], w[:, 2])
    num, a, fh, par, d, m = (w[:, i] for i in range(3, 9))
    v.tensor_tensor(num, num0, k, ALU.subtract)
    dve.drain()
    v.tensor_scalar(a, num, 0.5, -0.25, ALU.mult, ALU.add)
    v.tensor_scalar(scale, num, DENSE_ROW, None, ALU.is_gt)
    dve.drain()
    v.tensor_scalar(fh, a, ROUND, -ROUND, ALU.add, ALU.add)
    dve.drain()
    v.scalar_tensor_tensor(par, fh, -2.0, num, ALU.mult, ALU.add)
    v.tensor_tensor(m, num, fh, ALU.subtract)
    dve.drain()
    v.tensor_scalar(a, par, -0.25, 0.25, ALU.mult, ALU.add)
    dve.drain()
    v.tensor_tensor(d, num, a, ALU.mult)
    dve.drain()
    v.tensor_tensor(m, m, d, ALU.add)
    v.tensor_tensor(a, d, scale, ALU.mult)
    v.scalar_tensor_tensor(par, num, 2.0, maskok, ALU.is_ge, ALU.mult)
    dve.drain()
    if with_rank_shift:
        v.tensor_tensor(fh, off, k, ALU.subtract)
        v.scalar_tensor_tensor(a, a, 1.0, par, ALU.add, ALU.mult)
        dve.drain()
        v.tensor_tensor(m, fh, m, ALU.subtract)
    else:
        v.tensor_scalar(m, m, -1.0, None, ALU.mult)
        v.scalar_tensor_tensor(a, a, 1.0, par, ALU.add, ALU.mult)
    dve.drain()
    v.tensor_scalar(dist, a, -1.0, None, ALU.add)
    return v.tensor_tensor(bias, m, scale, ALU.mult)


def removal_phase(nc, z, A, K, scratch):
    B, N, NB = z.B, z.N, z.NB
    CH = B // 2
    R, SLOW = FAST_ROUNDS, P
    width = (N, N - P)
    with Scope(nc, "rem") as s:
        an = [s.sb(f"an{i}", [P, 2, N], F32) for i in range(2)]
        ac = [s.sb(f"ac{i}", [P, 2, N], F32) for i in range(2)]
        rowbin = [s.sb(f"rowbin{i}", [P, B, N], BF16) for i in range(2)]
        curT = [s.sb(f"curT{i}", [P, B, width[i]], BF16) for i in range(2)]
        rank = [s.sb(f"rank{i}", [P, B, width[i]], F16) for i in range(2)]
        both = s.sb("both", [P, B, P], BF16)
        rem = s.sb("rem", [P, B, P], BF16)
        lostto = s.sb("lostto", [P, B, N - P], BF16)
        dist = [s.sb(f"dist{i}", [P, N - P], F32) for i in range(2)]
        distd = s.sb("distd", [P, B, P], F32)
        junk = s.sb("junk", [P, N], BF16)
        w = s.sb("w", [P, 9, B], F32)
        num0 = [s.sb(f"num0{i}", [P, B], F32) for i in range(2)]
        rlast, off = s.sb("rlast", [P, B], F16), s.sb("off", [P, B], F32)
        k, kprev = s.sb("k", [P, B], F32), s.sb("kprev", [P, B], F32)
        moved, movedsum = s.sb("moved", [P, B], F32), s.sb("movedsum", [P, 1], F32)
        flag = s.sb("flag", [1, 1], I32)
        Kc = s.sb("Kc", [P, NB, B], F32)
        pk = s.ps("pk", [P, B])
        pl = s.ps("pl", [P, NB, B])
        pf = s.ps("pf", [1, 1])
        loaded = [s.sem(f"loaded{i}") for i in range(2)]
        compared, counted = s.sem("compared"), s.sem("counted")
        par_ready, dist_ready = s.sem("par_ready"), s.sem("dist_ready")
        rem_ready, lost_ready, moved_ready, flag_sum, flag_ready = (s.sem(n) for n in (
            "rem_ready", "lost_ready", "moved_ready", "flag_sum", "flag_ready"))
        spar, sdist, srem, slost, sback = (s.sem(n) for n in ("slow_par", "slow_dist", "slow_rem", "slow_lost", "slow_back"))
        fpar, fdist, ffree, fullrem, lost_far = (s.sem(n) for n in ("full_par", "full_dist", "full_free", "full_rem", "lost_far"))
        bins_ready, cur_ready = s.sem("bins_ready"), s.sem("cur_ready")
        stored = [s.sem(f"stored{i}") for i in range(2)]
        stores = [3] * (NB - 1) + [2]

        def stored_before(nb):
            return 16 * sum(stores[nb % 2:nb:2])

        with nc.Block() as block:
            @block.sync
            def _(sp):
                for i in range(NB * CH):
                    nb, c = divmod(i, CH)
                    rows, gs = slice(nb * P, (nb + 1) * P), slice(2 * c, 2 * c + 2)
                    if i >= 2:
                        sp.wait_ge(compared, i - 1)
                    sp.dma_start(an[i % 2][:], A["adj_rows"][gs, rows, :].rearrange("b p n -> p b n")).then_inc(loaded[i % 2], 16)
                    sp.dma_start(ac[i % 2][:, :, 0:N - nb * P],
                                 A["adj_cols"][gs, rows, nb * P:N].rearrange("b p n -> p b n")).then_inc(loaded[i % 2], 16)

            @block.gpsimd
            def _(pool):
                for nb in range(NB):
                    rows, n0, W = slice(nb * P, (nb + 1) * P), nb * P, N - nb * P
                    done = stored[nb % 2]
                    pool.wait_ge(bins_ready, CH * (nb + 1))
                    pool.dma_start(scratch["rowbin"][:, rows, :].rearrange("b p n -> p b n"), rowbin[nb % 2][:]).then_inc(done, 16)
                    pool.wait_ge(cur_ready, nb + 1)
                    pool.dma_start(scratch["curT"][:, rows, n0:N].rearrange("b p n -> p b n"),
                                   curT[nb % 2][:, :, 0:W]).then_inc(done, 16)
                    if W > P:
                        pool.dma_start(scratch["rem"][:, rows, n0 + P:N].rearrange("b p n -> p b n"),
                                       rank[nb % 2][:, :, P:W].bitcast(BF16)).then_inc(done, 16)
                for i in range(2):
                    pool.wait_ge(stored[i], 16 * sum(stores[i::2]))

            @block.scalar
            def _(act):
                def count(i):
                    nb, c = divmod(i, CH)
                    act.wait_ge(bins_ready, i + 1)
                    for b in (2 * c, 2 * c + 1):
                        nc.scalar.activation(junk[:], rowbin[nb % 2][:, b, :], ACT.Copy, accum_out=num0[nb % 2][:, b:b + 1])
                        act.drain()
                    if c == CH - 1:
                        act.drain().then_inc(counted, 1)

                def distances(nb, ready, n, done):
                    act.wait_ge(ready, n)
                    for b in range(B):
                        nc.scalar.activation(distd[:, b, :], rank[nb % 2][:, b, 0:P], ACT.Abs, bias=w[:, 1, b:b + 1],
                                             scale=w[:, 0, b:b + 1]).then_inc(done, 1)

                for c in range(CH):
                    count(c)
                for nb in range(NB):
                    todo = list(range((nb + 1) * CH, (nb + 2) * CH)) if nb < NB - 1 else []
                    for t in range(R):
                        distances(nb, par_ready, nb * R + t + 1, dist_ready)
                        if todo:
                            count(todo.pop(0))
                    for i in todo:
                        count(i)
                    act.wait_ge(flag_ready, nb + 1)
                    go = act.value_load(flag[0:1, 0:1], min_val=0, max_val=1)
                    with act.If(go > 0):
                        with act.Fori(0, SLOW) as t:
                            distances(nb, spar, t + 1, sdist)
                    W = N - nb * P
                    if W > P:
                        act.wait_ge(fpar, nb + 1)
                        for b in range(B):
                            act.wait_ge(ffree, nb * B + b + 1)
                            nc.scalar.activation(dist[b % 2][:, 0:W - P], rank[nb % 2][:, b, P:W], ACT.Abs,
                                                 bias=w[:, 1, b:b + 1], scale=w[:, 0, b:b + 1]).then_inc(fdist, 1)

            @block.tensor
            def _(pe):
                def lost(ready, n, done):
                    pe.wait_ge(ready, n)
                    for b in range(B):
                        mm = nc.tensor.matmul(pk[:, b:b + 1], rem[:, b, :], K["ones16"][:, 0:1], start=True, stop=True)
                    mm.then_inc(done, 1)

                for nb in range(NB):
                    for t in range(R):
                        lost(rem_ready, nb * R + t + 1, lost_ready)
                    pe.wait_ge(moved_ready, nb + 1)
                    nc.tensor.matmul(pf[:], movedsum[:], K["onescol"][:, 0:1], start=True, stop=True).then_inc(flag_sum, 1)
                    pe.wait_ge(flag_ready, nb + 1)
                    go = pe.value_load(flag[0:1, 0:1], min_val=0, max_val=1)
                    with pe.If(go > 0):
                        with pe.Fori(0, SLOW) as t:
                            lost(srem, t + 1, slost)
                    if nb < NB - 1:
                        pe.wait_ge(fullrem, nb + 1)
                        for jb in range(nb + 1, NB):
                            for b in range(B):
                                o = (jb - nb - 1) * P
                                mm = nc.tensor.matmul(pl[:, jb, b:b + 1], lostto[:, b, o:o + P], K["ones16"][:, 0:1],
                                                      start=True, stop=True)
                        mm.then_inc(lost_far, 1)

            @block.vector
            def _(dve):
                v = nc.vector
                v.memset(Kc[:], 0.0)
                dve.sem_inc(ffree, 2)
                dve.drain()

                def compare(i):
                    nb, c = divmod(i, CH)
                    n0, W = nb * P, N - nb * P
                    gs = slice(2 * c, 2 * c + 2)
                    if c == 0 and nb >= 2:
                        dve.wait_ge(stored[nb % 2], stored_before(nb))
                    dve.wait_ge(loaded[i % 2], 32 * (i // 2 + 1))
                    v.tensor_scalar(rowbin[nb % 2][:, gs, :], an[i % 2][:], 0.0, None, ALU.is_gt).then_inc(bins_ready, 1)
                    v.tensor_scalar(curT[nb % 2][:, gs, 0:W], ac[i % 2][:, :, 0:W], 0.0, None, ALU.is_gt)
                    dve.drain().then_inc(compared, 1)
                    for b in (2 * c, 2 * c + 1):
                        v.tensor_tensor_scan(rank[nb % 2][:, b, 0:W], K["ones16"][:, 0:1].to_broadcast([P, W]), rowbin[nb % 2][:, b, n0:N], 0.0,
                                             ALU.mult, ALU.add)

                def one_round(ready, dready, drem, dlost, dn, n, nb, chunk=None):
                    mask = K["maskok"][:].rearrange("p (b t) -> p t b", t=NB)[:, nb, :]
                    removal_parameters(nc, dve, k[:], num0[nb % 2][:], off[:], mask, w, True).then_inc(ready, 1)
                    v.tensor_copy(kprev[:], k[:])
                    if chunk is not None:
                        compare(chunk)
                    for b in range(B):
                        dve.wait_ge(dready, dn + (b + 1))
                        last = v.scalar_tensor_tensor(rem[:, b, :], distd[:, b, :], w[:, 2, b:b + 1], both[:, b, :],
                                                      ALU.is_equal, ALU.mult)
                    last.then_inc(drem, 1)
                    dve.wait_ge(dlost, n)
                    v.tensor_tensor(k[:], Kc[:, nb, :], pk[:], ALU.add)
                    dve.drain()

                for c in range(CH):
                    compare(c)
                for nb in range(NB):
                    n0, W = nb * P, N - nb * P
                    mask = K["maskok"][:].rearrange("p (b t) -> p t b", t=NB)[:, nb, :]
                    cT, rk, rb, n0count = curT[nb % 2], rank[nb % 2], rowbin[nb % 2], num0[nb % 2]
                    dve.drain()
                    v.tensor_tensor(both[:], rb[:, :, n0:n0 + P], cT[:, :, 0:P], ALU.mult)
                    v.tensor_copy(rlast[:], rk[:, :, W - 1])
                    v.tensor_copy(k[:], Kc[:, nb, :])
                    dve.drain()
                    dve.wait_ge(counted, nb + 1)
                    v.tensor_tensor(off[:], n0count[:], rlast[:], ALU.subtract)
                    v.tensor_tensor(both[:], both[:], K["upper"][:].unsqueeze(1).to_broadcast([P, B, P]), ALU.mult)
                    dve.drain()
                    todo = list(range((nb + 1) * CH, (nb + 2) * CH)) if nb < NB - 1 else []
                    for t in range(R):
                        one_round(par_ready, dist_ready, rem_ready, lost_ready, (nb * R + t) * B, nb * R + t + 1, nb,
                                  todo.pop(0) if todo else None)
                    for i in todo:
                        compare(i)
                    v.tensor_tensor(moved[:], k[:], kprev[:], ALU.not_equal)
                    dve.drain()
                    v.reduce_sum(movedsum[:], moved[:], AX).then_inc(moved_ready, 1)
                    dve.wait_ge(flag_sum, nb + 1)
                    v.tensor_scalar(flag[:], pf[:], 0.0, None, ALU.is_gt).then_inc(flag_ready, 1)
                    dve.wait_ge(flag_ready, nb + 1)
                    go = dve.value_load(flag[0:1, 0:1], min_val=0, max_val=1)
                    with dve.If(go > 0):
                        with dve.Fori(0, SLOW) as t:
                            one_round(spar, sdist, srem, slost, t * B, t + 1, nb)
                        for sm in (spar, sdist, srem, slost):
                            dve.sem_clear(sm)
                    if W > P:
                        removal_parameters(nc, dve, k[:], n0count[:], off[:], mask, w, True).then_inc(fpar, 1)
                        dve.drain()
                    v.tensor_tensor(cT[:, :, 0:P], cT[:, :, 0:P], rem[:], ALU.subtract)
                    if W > P:
                        rem_far = rk[:, :, P:W].bitcast(BF16)
                        for b in range(B):
                            dve.wait_ge(fdist, nb * B + b + 1)
                            v.scalar_tensor_tensor(rem_far[:, b, :], dist[b % 2][:, 0:W - P], w[:, 2, b:b + 1],
                                                   rb[:, b, n0 + P:N], ALU.is_equal, ALU.mult).then_inc(ffree, 1)
                        dve.drain()
                        v.tensor_tensor(lostto[:, :, 0:W - P], rem_far, cT[:, :, P:W], ALU.mult)
                        dve.drain().then_inc(fullrem, 1)
                        v.tensor_tensor(cT[:, :, P:W], cT[:, :, P:W], lostto[:, :, 0:W - P], ALU.subtract)
                    dve.drain().then_inc(cur_ready, 1)
                    params = tuple(K[n][:].rearrange("p (b t) -> p t b", t=NB)[:, nb, :] for n in ("rscale", "rbias", "rdist"))
                    removal_parameters(nc, dve, k[:], n0count[:], off[:], mask, w, False, params)
                    if nb < NB - 1:
                        dve.wait_ge(lost_far, nb + 1)
                        v.tensor_tensor(Kc[:, nb + 1:NB, :], Kc[:, nb + 1:NB, :], pl[:, nb + 1:NB, :], ALU.add)
                        dve.drain()


def keep_phase(nc, z, A, K, scratch):
    B, N, NB, NH, HB = z.B, z.N, z.NB, z.NH, z.HB
    pieces = [(nb, hf * HALF, min((hf + 1) * HALF, (nb + 1) * P)) for nb in range(NB) for hf in range(NH)
              if hf * HALF < (nb + 1) * P]
    NR, NM = 3, 4
    assert len(pieces) % NR == 0 and (NB * NH) % NM == 0
    with Scope(nc, "keep") as s:
        cur = [s.sb(f"cur{i}", [P, NB, N], BF16) for i in range(2)]
        rowbin = [s.sb(f"rowbin{i}", [P, NB, N], BF16) for i in range(1)] * 2
        adjT = [s.sb(f"adjT{i}", [P, NB, N], F32) for i in range(2)]
        rem = [s.sb(f"rem{i}", [P, NB, N], BF16) for i in range(2)]
        dist = [s.sb(f"dist{i}", [P, HALF], F32) for i in range(NR)]
        keptsum = s.sb("keptsum", [P, N], F32)
        test = s.sb("test", [P, 2, NB], F32)
        prank = [s.ps(f"prank{i}", [P, HALF]) for i in range(NR)]
        pboth = [s.ps(f"pboth{i}", [P, HALF]) for i in range(NM)]
        pdeg = s.ps("pdeg", [P, NB])
        loaded = [s.sem(f"loaded{i}") for i in range(2)]
        bin_loaded = s.sem("bin_loaded")
        adj_loaded = [s.sem(f"adj_loaded{i}") for i in range(2)]
        issued, cur_free, bin_free, rem_free, rank_ready, rank_read, dist_ready, dist_read = (s.sem(n) for n in (
            "issued", "cur_free", "bin_free", "rem_free", "rank_ready", "rank_read", "dist_ready", "dist_read"))
        rem_ready, both_ready, both_read, deg_ready, deg_read = (s.sem(n) for n in (
            "rem_ready", "both_ready", "both_read", "deg_ready", "deg_read"))
        masked, stored, summed = s.sem("masked"), s.sem("stored"), s.sem("summed")
        NP, NW = len(pieces), NB * NH
        n_loads = NB + (NB - 1)
        with nc.Block() as block:
            @block.sync
            def _(sp):
                def body(b, par, last):
                    sp.wait_ge(cur_free, b + 1)
                    sp.sem_inc(issued, 1)
                    for jb in range(NB):
                        sp.dma_start(cur[par][:, jb, jb * P:N], block_rows(scratch["curT"], b, jb)[:, jb * P:N])\
                            .then_inc(loaded[par], 16)
                    sp.wait_ge(rem_free, b + 1)
                    sp.sem_inc(issued, 1)
                    for nb in range(NB - 1):
                        sp.dma_start(rem[par][:, nb, (nb + 1) * P:N], block_rows(scratch["rem"], b, nb)[:, (nb + 1) * P:N])\
                            .then_inc(loaded[par], 16)
                    sp.wait_ge(bin_free, b + 1)
                    sp.sem_inc(issued, 1)
                    for nb in range(NB):
                        sp.dma_start(rowbin[par][:, nb, 0:(nb + 1) * P], block_rows(scratch["rowbin"], b, nb)[:, 0:(nb + 1) * P])\
                            .then_inc(bin_loaded, 16)
                per_pair(sp, B, body)

            @block.gpsimd
            def _(pool):
                g = nc.gpsimd

                def body(b, par, last):
                    pool.wait_ge(deg_read, b + 1)
                    for jb in range(1, NB):
                        pool.wait_ge(masked, b * NW + (jb + 1) * NH)
                        g.tensor_tensor(keptsum[:], adjT[par][:, 0, :] if jb == 1 else keptsum[:], adjT[par][:, jb, :], ALU.add)
                        pool.drain()
                    pool.sem_inc(summed, 1)
                per_pair(pool, B, body)

            @block.tensor
            def _(pe):
                t = nc.tensor
                pe.sem_inc(cur_free, 2)
                pe.sem_inc(rem_free, 2)

                def ranks(b, par):
                    pe.wait_ge(loaded[par], (b - par) * (8 * n_loads) + 16 * n_loads)
                    for q, (nb, lo, hi) in enumerate(pieces):
                        pe.wait_ge(rank_read, b * NP + q + 1)
                        last_jb = min(nb, (hi - 1) // P)
                        for jb in range(last_jb + 1):
                            a = max(jb * P, lo)
                            mm = t.matmul(prank[q % NR][:, a - lo:hi - lo], cur[par][:, jb, nb * P:(nb + 1) * P],
                                          K["tri"][:, a - jb * P:hi - jb * P], start=(jb == 0), stop=(jb == last_jb))
                        mm.then_inc(rank_ready, 1)
                    pe.drain().then_inc(cur_free, 1)

                def body(b, par, last):
                    if not last:
                        ranks(b + 1, 1 - par)
                    pe.wait_ge(rem_ready, b * NP + NP)
                    for jb in range(NB):
                        for hf in range(NH):
                            q = jb * NH + hf
                            pe.wait_ge(both_read, b * NW + q + 1)
                            o = pboth[q % NM]
                            t.matmul(o[:], K["ident16"][:], rem[par][:, jb, hf * HALF:(hf + 1) * HALF], start=True, stop=False)
                            for e in range(HB):
                                nb = hf * HB + e
                                mm = t.matmul(o[:, e * P:(e + 1) * P], rem[par][:, nb, jb * P:(jb + 1) * P],
                                              K["ident16"][:], start=False, stop=(e == HB - 1))
                            mm.then_inc(both_ready, 1)
                    pe.drain().then_inc(rem_free, 1)
                    pe.wait_ge(summed, b + 1)
                    for ib in range(NB):
                        mm = t.matmul(pdeg[:, ib:ib + 1], keptsum[:, ib * P:(ib + 1) * P], K["onescol"][:, 0:1],
                                      start=True, stop=True)
                    mm.then_inc(deg_ready, 1)
                ranks(0, 0)
                per_pair(pe, B, body)

            @block.scalar
            def _(act):
                act.sem_inc(rank_read, NR)
                act.sem_inc(stored, 16)

                def distances(b):
                    cols = bass.ds(b * NB, NB)
                    nc.scalar.activation(test[:, 0, :], K["rscale"][:, cols], ACT.Copy)
                    nc.scalar.activation(test[:, 1, :], K["rbias"][:, cols], ACT.Copy)
                    act.drain()
                    for q, (nb, lo, hi) in enumerate(pieces):
                        act.wait_ge(rank_ready, b * NP + q + 1)
                        act.wait_ge(dist_read, b * NP + q + 1)
                        nc.scalar.activation(dist[q % NR][:, 0:hi - lo], prank[q % NR][:, 0:hi - lo], ACT.Abs,
                                             bias=test[:, 1, nb:nb + 1], scale=test[:, 0, nb:nb + 1]).then_inc(dist_ready, 1)
                        act.drain().then_inc(rank_read, 1)

                def body(b, par, last):
                    if not last:
                        distances(b + 1)
                        act.wait_ge(stored, b * 16 + 16)
                        act.dma_start(adjT[1 - par][:], graph(A["adj_cols"], b + 1)).then_inc(adj_loaded[1 - par], 16)
                    act.wait_ge(masked, b * NW + NW)
                    act.wait_ge(summed, b + 1)
                    act.dma_start(graph(scratch["keptT"], b), adjT[par][:]).then_inc(stored, 16)
                act.dma_start(adjT[0][:], graph(A["adj_cols"], 0)).then_inc(adj_loaded[0], 16)
                distances(0)
                per_pair(act, B, body)
                act.wait_ge(stored, 16 + 16 * B)

            @block.vector
            def _(dve):
                v = nc.vector
                dve.sem_inc(dist_read, NR)
                dve.sem_inc(both_read, NM)
                dve.sem_inc(deg_read, 1)
                dve.sem_inc(bin_free, 1)

                def removals(b, par):
                    dve.wait_ge(loaded[par], (b - par) * (8 * n_loads) + 16 * n_loads)
                    dve.wait_ge(bin_loaded, b * (16 * NB) + 16 * NB)
                    for q, (nb, lo, hi) in enumerate(pieces):
                        dve.wait_ge(dist_ready, b * NP + q + 1)
                        col = bass.ds(b * NB + nb, 1)
                        v.scalar_tensor_tensor(rem[par][:, nb, lo:hi], dist[q % NR][:, 0:hi - lo], K["rdist"][:, col],
                                               rowbin[par][:, nb, lo:hi], ALU.is_equal, ALU.mult).then_inc(rem_ready, 1)
                        dve.drain().then_inc(dist_read, 1)
                    dve.sem_inc(bin_free, 1)

                def body(b, par, last):
                    if not last:
                        removals(b + 1, 1 - par)
                    dve.wait_ge(adj_loaded[par], (b - par) * 8 + 16)
                    for jb in range(NB):
                        for hf in range(NH):
                            q = jb * NH + hf
                            sl = slice(hf * HALF, (hf + 1) * HALF)
                            dve.wait_ge(both_ready, b * NW + q + 1)
                            v.scalar_tensor_tensor(adjT[par][:, jb, sl], pboth[q % NM][:], 0.5, adjT[par][:, jb, sl],
                                                   ALU.is_lt, ALU.mult).then_inc(masked, 1)
                            dve.drain().then_inc(both_read, 1)
                    cols = bass.ds(b * NB, NB)
                    dve.wait_ge(deg_ready, b + 1)
                    v.tensor_scalar(K["rdeg"][:, cols], pdeg[:], 1.0, None, ALU.max)
                    dve.drain().then_inc(deg_read, 1)
                    v.reciprocal(K["rdeg"][:, cols], K["rdeg"][:, cols])
                removals(0, 0)
                per_pair(dve, B, body)


def sage_phase(nc, z, A, K, scratch, layer):
    B, N, NB, NH, HB, D = z.B, z.N, z.NB, z.NH, z.HB, z.D
    first = layer == 0
    with Scope(nc, f"sage{layer}") as s:
        adjT = [s.sb(f"adjT{i}", [P, NB, N], F32) for i in range(2)]
        h = [s.sb(f"h{i}", [P, NB, D], F32) for i in range(2)]
        hT = s.sb("hT", [P, N], F32)
        aggT = s.sb("aggT", [P, N], F32)
        o = s.sb("o", [P, NB, D], F32)
        t1 = s.sb("t1", [P, NB, D], F32)
        nrm = s.sb("nrm", [P, 5, NB], F32)
        acc = s.sb("acc", [P, 2, NB, D], F32)
        rsq = s.sb("rsq", [P, NB, D], F32)
        tot = s.sb("tot", [P, 2, D], F32)
        mv = s.sb("mv", [P, 4, D], F32)
        onesf = s.sb("onesf", [P, P], F32)
        w = norm_buffers(s.sb, s.sem, "n", NB, D) if first else None
        agg = s.ps("agg", [P, N])
        tp = s.ps("tp", [P, N])
        o1 = s.ps("o1", [P, NB, D])
        o2 = s.ps("o2", [P, NB, D])
        sem = {n: s.sem(n) for n in (
            "adj_used", "issued", "h_ready", "tp_ready", "hT_ready", "agg_half", "aggT_half", "o1_ready", "o2_ready", "y_ready",
            "y_read", "o_read", "ss_ready", "len_ready", "r_ready", "r_summed", "tot_ready", "totals", "bn_var", "bn_std")}
        loaded = [s.sem(f"loaded{i}") for i in range(2)]
        r = K["r"]
        with nc.Block() as block:
            @block.sync
            def _(sp):
                def body(b, par, last):
                    sp.wait_ge(sem["adj_used"], b + 1)
                    sp.sem_inc(sem["issued"], 1)
                    for c in range(2):
                        hb = NB // 2
                        sp.dma_start(adjT[par][:, c * hb:(c + 1) * hb, :],
                                     graph(scratch["keptT"], b)[:, c * hb:(c + 1) * hb, :]).then_inc(loaded[par], 16)
                per_pair(sp, B, body)

            @block.tensor
            def _(pe):
                t = nc.tensor
                pe.sem_inc(sem["adj_used"], 2)

                def body(b, par, last):
                    pe.wait_ge(sem["h_ready"], b + 1)
                    for ib in range(NB):
                        mm = t.transpose(tp[:, ib * P:(ib + 1) * P], h[par][:, ib, :], K["ident"][:])
                    mm.then_inc(sem["tp_ready"], 1)
                    pe.wait_ge(loaded[par], (b - par) * 16 + 32)
                    for hf in range(NH):
                        for jb in range(NB):
                            mm = t.matmul(agg[:, hf * HALF:(hf + 1) * HALF], h[par][:, jb, :],
                                          adjT[par][:, jb, hf * HALF:(hf + 1) * HALF], start=(jb == 0), stop=(jb == NB - 1))
                        mm.then_inc(sem["agg_half"], 1)
                    pe.drain().then_inc(sem["adj_used"], 1)
                    pe.wait_ge(sem["hT_ready"], b + 1)
                    pe.wait_ge(sem["o_read"], b + 1)
                    if not first:
                        for ib in range(NB):
                            mm = t.matmul(o1[:, ib, :], hT[:, ib * P:(ib + 1) * P], K["Wl"][:, layer - 1, :], start=True, stop=True)
                        mm.then_inc(sem["y_ready"], 1)
                    for ib in range(NB):
                        mm = t.matmul(o2[:, ib, :], hT[:, ib * P:(ib + 1) * P], K[f"Wx{layer}"][:], start=True, stop=True)
                    mm.then_inc(sem["o2_ready"], 1)
                    if not first:
                        pe.wait_ge(sem["y_read"], b + 1)
                    for hf in range(NH):
                        pe.wait_ge(sem["aggT_half"], b * NH + hf + 1)
                        for ib in range(hf * HB, (hf + 1) * HB):
                            mm = t.matmul(o1[:, ib, :], aggT[:, ib * P:(ib + 1) * P], K[f"Wr{layer}"][:], start=True, stop=True)
                    mm.then_inc(sem["o1_ready"], 1)
                per_pair(pe, B, body)
                pe.wait_ge(sem["tot_ready"], 1)
                t.matmul(o1[:, 0:2, :], onesf[:], tot[:], start=True, stop=True).then_inc(sem["totals"], 1)

            @block.scalar
            def _(act):
                def body(b, par, last):
                    act.wait_ge(sem["tp_ready"], b + 1)
                    nc.scalar.activation(hT[:], tp[:], ACT.Copy).then_inc(sem["hT_ready"], 1)
                    if first and not last:
                        norm_root(nc, act, w, b + 1)
                    for hf in range(NH):
                        act.wait_ge(sem["agg_half"], b * NH + hf + 1)
                        sl = slice(hf * HALF, (hf + 1) * HALF)
                        nc.scalar.activation(aggT[:, sl], agg[:, sl], ACT.Copy).then_inc(sem["aggT_half"], 1)
                    act.wait_ge(sem["ss_ready"], b + 1)
                    nc.scalar.activation(nrm[:, 1, :], nrm[:, 0, :], ACT.Sqrt).then_inc(sem["len_ready"], 1)
                if first:
                    norm_root(nc, act, w, 0)
                per_pair(act, B, body)
                act.wait_ge(sem["bn_var"], 1)
                nc.scalar.activation(mv[:, 2, :], mv[:, 1, :], ACT.Sqrt).then_inc(sem["bn_std"], 1)

            @block.gpsimd
            def _(pool):
                g = nc.gpsimd
                g.memset(acc[:], 0.0)
                g.memset(onesf[:], 1.0)
                pool.drain()

                def body(b, par, last):
                    pool.wait_ge(sem["r_ready"], b + 1)
                    rb = tiles(r, b, NB)
                    g.tensor_tensor(rsq[:], rb, rb, ALU.mult)
                    g.tensor_tensor(acc[:, 0], acc[:, 0], rb, ALU.add)
                    pool.drain()
                    g.tensor_tensor(acc[:, 1], acc[:, 1], rsq[:], ALU.add)
                    pool.drain()
                per_pair(pool, B, body)
                pool.drain().then_inc(sem["r_summed"], 1)

            @block.vector
            def _(dve):
                v = nc.vector
                dve.sem_inc(sem["o_read"], 1)

                def prepare(b, par):
                    if first:
                        norm_relu_vector(nc, dve, tiles(K["X"], b, NB), h[par][:], w, b).then_inc(sem["h_ready"], 1)
                    else:
                        v.tensor_tensor(t1[:], tiles(r, b, NB), along_tiles(K["bnscale"][:], NB), ALU.mult)
                        dve.drain()
                        v.tensor_tensor(h[par][:], t1[:], along_tiles(K["bnshift"][:], NB), ALU.add).then_inc(sem["h_ready"], 1)
                    dve.drain()

                def finish(b, par):
                    cols = bass.ds(b * NB, NB)
                    if not first:
                        dve.wait_ge(sem["y_ready"], b + 1)
                        v.tensor_tensor(t1[:], o1[:], along_features(K["mask2"][:, cols], D), ALU.mult).then_inc(sem["y_read"], 1)
                        dve.drain()
                        v.tensor_tensor(tiles(K["X"], b, NB), tiles(K["X"], b, NB), t1[:], ALU.add)
                        dve.drain()
                    dve.wait_ge(sem["o2_ready"], b + 1)
                    v.tensor_tensor(o[:], o2[:], along_tiles(K["vec"][:, V_B1 + layer, :], NB), ALU.add)
                    dve.wait_ge(sem["o1_ready"], b + 1)
                    v.tensor_tensor(t1[:], o1[:], along_features(K["rdeg"][:, cols], D), ALU.mult)
                    dve.drain().then_inc(sem["o_read"], 1)
                    v.tensor_tensor(o[:], o[:], t1[:], ALU.add)
                    dve.drain()
                    v.tensor_tensor(t1[:], o[:], o[:], ALU.mult)
                    dve.drain()
                    v.tensor_reduce(nrm[:, 0, :], t1[:], AX, ALU.add).then_inc(sem["ss_ready"], 1)
                    dve.wait_ge(sem["len_ready"], b + 1)
                    v.tensor_scalar(nrm[:, 2, :], nrm[:, 1, :], NORM_EPS, None, ALU.max)
                    dve.drain()
                    v.reciprocal(nrm[:, 3, :], nrm[:, 2, :])
                    dve.drain()
                    v.tensor_tensor(nrm[:, 4, :], nrm[:, 3, :], K["mask"][:, cols], ALU.mult)
                    dve.drain()
                    v.tensor_tensor(t1[:], o[:], along_features(nrm[:, 4, :], D), ALU.mult)
                    dve.drain()
                    v.tensor_scalar(tiles(r, b, NB), t1[:], 0.0, None, ALU.max).then_inc(sem["r_ready"], 1)
                    dve.drain()

                prepare(0, 0)

                def body(b, par, last):
                    if not last:
                        prepare(b + 1, 1 - par)
                    finish(b, par)
                per_pair(dve, B, body)
                dve.wait_ge(sem["r_summed"], 1)
                for i in range(2):
                    last = v.tensor_reduce(tot[:, i, :], acc[:, i].rearrange("p t d -> p d t"), AX, ALU.add)
                last.then_inc(sem["tot_ready"], 1)
                dve.wait_ge(sem["totals"], 1)
                n_all = float(B * N)
                v.tensor_scalar(mv[:, 0, :], o1[:, 0, :], 1.0 / n_all, None, ALU.mult)
                v.tensor_scalar(mv[:, 1, :], o1[:, 1, :], 1.0 / n_all, None, ALU.mult)
                dve.drain()
                v.tensor_tensor(mv[:, 2, :], mv[:, 0, :], mv[:, 0, :], ALU.mult)
                dve.drain()
                v.tensor_tensor(mv[:, 1, :], mv[:, 1, :], mv[:, 2, :], ALU.subtract)
                dve.drain()
                v.tensor_scalar(mv[:, 1, :], mv[:, 1, :], BN_EPS, None, ALU.add).then_inc(sem["bn_var"], 1)
                dve.wait_ge(sem["bn_std"], 1)
                v.reciprocal(mv[:, 3, :], mv[:, 2, :])
                dve.drain()
                v.tensor_tensor(K["bnscale"][:], mv[:, 3, :], K["vec"][:, V_G1 + layer, :], ALU.mult)
                dve.drain()
                v.tensor_tensor(mv[:, 1, :], mv[:, 0, :], K["bnscale"][:], ALU.mult)
                dve.drain()
                v.tensor_tensor(K["bnshift"][:], K["vec"][:, V_E1 + layer, :], mv[:, 1, :], ALU.subtract)


def gcn_phase(nc, z, A, K):
    B, N, NB, NH, HB, D = z.B, z.N, z.NB, z.NH, z.HB, z.D
    with Scope(nc, "gcn") as s:
        adjT = [s.sb(f"adjT{i}", [P, NB, N], F32) for i in range(2)]
        h = s.sb("h", [P, NB, D], F32)
        hT = s.sb("hT", [P, N], F32)
        h3 = s.sb("h3", [P, NB, D], F32)
        t1 = s.sb("t1", [P, NB, D], F32)
        y = s.sb("y", [P, 4, D], F32)
        sup = [s.sb(f"sup{i}", [P, NB, D], F32) for i in range(2)]
        dinv = s.sb("dinv", [P, z.T], F32)
        dw = s.sb("dw", [P, 3, z.T], F32)
        w = norm_buffers(s.sb, s.sem, "n", NB, D)
        tp = s.ps("tp", [P, N])
        pr = s.ps("pr", [P, NB, D])
        acc = [s.ps(f"acc{i}", [P, 4, D]) for i in range(4)]
        sem = {n: s.sem(n) for n in (
            "adj_used", "issued", "h_ready", "tp_ready", "hT_ready", "pr_ready", "sup_ready", "sums_ready", "sums_read",
            "deg_ready", "dinv_ready")}
        loaded = [s.sem(f"loaded{i}") for i in range(2)]
        QB = NB // 4
        with nc.Block() as block:
            @block.sync
            def _(sp):
                def body(b, par, last):
                    sp.wait_ge(sem["adj_used"], b + 1)
                    sp.sem_inc(sem["issued"], 1)
                    for c in range(2):
                        hb = NB // 2
                        sp.dma_start(adjT[par][:, c * hb:(c + 1) * hb, :],
                                     graph(A["adj_cols"], b)[:, c * hb:(c + 1) * hb, :]).then_inc(loaded[par], 16)
                per_pair(sp, B, body)

            @block.tensor
            def _(pe):
                t = nc.tensor
                pe.sem_inc(sem["adj_used"], 2)

                def project(n, src, weight):
                    pe.wait_ge(sem["h_ready"], n + 1)
                    for ib in range(NB):
                        mm = t.transpose(tp[:, ib * P:(ib + 1) * P], src[:, ib, :], K["ident"][:])
                    mm.then_inc(sem["tp_ready"], 1)
                    pe.wait_ge(sem["hT_ready"], n + 1)
                    for ib in range(NB):
                        mm = t.matmul(pr[:, ib, :], hT[:, ib * P:(ib + 1) * P], weight, start=True, stop=True)
                    mm.then_inc(sem["pr_ready"], 1)

                def prepare(b):
                    project(b * 2, h3, K["Wl"][:, 2, :])
                    project(b * 2 + 1, h, K["W2"][:])

                prepare(0)

                def body(b, par, last):
                    pe.wait_ge(sem["sup_ready"], b + 1)
                    pe.wait_ge(loaded[par], (b - par) * 16 + 32)
                    for k in range(QB):
                        a = acc[(par * QB + k) % 4]
                        pe.wait_ge(sem["sums_read"], b * QB + k + 1)
                        for e in range(4):
                            ib = 4 * k + e
                            for jb in range(NB):
                                mm = t.matmul(a[:, e, :], adjT[par][:, jb, ib * P:(ib + 1) * P], sup[par][:, jb, :],
                                              start=(jb == 0), stop=(jb == NB - 1))
                        mm.then_inc(sem["sums_ready"], 1)
                        if k == 0 and not last:
                            prepare(b + 1)
                    pe.drain().then_inc(sem["adj_used"], 1)
                per_pair(pe, B, body)

            @block.scalar
            def _(act):
                act.wait_ge(sem["deg_ready"], 1)
                nc.scalar.activation(dinv[:], dw[:, 1, :], ACT.Sqrt).then_inc(sem["dinv_ready"], 1)

                def body(b, par, last):
                    for k in range(2):
                        act.wait_ge(sem["tp_ready"], b * 2 + k + 1)
                        nc.scalar.activation(hT[:], tp[:], ACT.Copy).then_inc(sem["hT_ready"], 1)
                        if k == 0:
                            norm_root(nc, act, w, b)
                per_pair(act, B, body)

            @block.vector
            def _(dve):
                v = nc.vector
                dve.sem_inc(sem["sums_read"], 4)
                v.tensor_scalar(dw[:, 0, :], K["rowsum"][:], 1.0, None, ALU.add)
                dve.drain()
                v.tensor_scalar(dw[:, 2, :], dw[:, 0, :], 0.0, None, ALU.is_equal)
                dve.drain()
                v.tensor_tensor(dw[:, 0, :], dw[:, 0, :], dw[:, 2, :], ALU.add)
                dve.drain()
                v.reciprocal(dw[:, 1, :], dw[:, 0, :]).then_inc(sem["deg_ready"], 1)
                v.tensor_scalar(dw[:, 2, :], dw[:, 2, :], -1.0, 1.0, ALU.mult, ALU.add)
                dve.wait_ge(sem["dinv_ready"], 1)
                dve.drain()
                v.tensor_tensor(dinv[:], dinv[:], dw[:, 2, :], ALU.mult)
                dve.drain()

                def prepare(b, par):
                    x = tiles(K["X"], b, NB)
                    cols = bass.ds(b * NB, NB)
                    v.tensor_tensor(t1[:], tiles(K["r"], b, NB), along_tiles(K["bnscale"][:], NB), ALU.mult)
                    dve.drain()
                    v.tensor_tensor(h3[:], t1[:], along_tiles(K["bnshift"][:], NB), ALU.add).then_inc(sem["h_ready"], 1)
                    dve.drain()
                    v.tensor_tensor(t1[:], along_tiles(K["vec"][:, V_BL, :], NB), along_features(K["mask"][:, cols], D), ALU.mult)
                    dve.drain()
                    v.tensor_tensor(x, x, t1[:], ALU.add)
                    dve.drain()
                    dve.wait_ge(sem["pr_ready"], b * 2 + 1)
                    v.tensor_tensor(t1[:], pr[:], along_features(K["mask2"][:, cols], D), ALU.mult)
                    dve.drain()
                    v.tensor_tensor(x, x, t1[:], ALU.add)
                    dve.drain()
                    norm_relu_vector(nc, dve, x, h[:], w, b).then_inc(sem["h_ready"], 1)
                    dve.wait_ge(sem["pr_ready"], b * 2 + 2)
                    v.tensor_tensor(sup[par][:], pr[:], along_features(dinv[:, cols], D), ALU.mult)
                    dve.drain().then_inc(sem["sup_ready"], 1)

                def finish(b, par):
                    for k in range(QB):
                        a = acc[(par * QB + k) % 4]
                        dve.wait_ge(sem["sums_ready"], b * QB + k + 1)
                        cols = bass.ds(b * NB + 4 * k, 4)
                        xs = K["X"][:, cols]
                        v.tensor_tensor(y[:], a[:], sup[par][:, 4 * k:4 * k + 4, :], ALU.add)
                        dve.drain().then_inc(sem["sums_read"], 1)
                        v.tensor_tensor(y[:], y[:], along_features(dinv[:, cols], D), ALU.mult)
                        dve.drain()
                        v.tensor_tensor(y[:], y[:], along_tiles(K["vec"][:, V_BIAS2, :], 4), ALU.add)
                        dve.drain()
                        v.tensor_tensor(xs, xs, y[:], ALU.add)
                        dve.drain()

                prepare(0, 0)

                def body(b, par, last):
                    if not last:
                        prepare(b + 1, 1 - par)
                    finish(b, par)
                per_pair(dve, B, body)


def maxdeg_phase(nc, z, A, K, scratch, out):
    B, N, NB, NH, HB, D = z.B, z.N, z.NB, z.NH, z.HB, z.D
    with Scope(nc, "l3") as s:
        rowbin = [s.sb(f"rowbin{i}", [P, NB, N], BF16) for i in range(2)]
        h = s.sb("h", [P, NB, D], F32)
        rest = s.sb("rest", [P, NB, D], F32)
        parts = [s.sb(f"parts{i}", [P, 3, NB, D], BF16) for i in range(2)]
        aggT = s.sb("aggT", [P, N], F32)
        y = s.sb("y", [P, NB, D], F32)
        res = [s.sb(f"res{i}", [P, NB, D], F32) for i in range(2)]
        rcol = s.sb("rcol", [P, z.T], F32)
        w = norm_buffers(s.sb, s.sem, "n", NB, D)
        agg = [s.ps(f"agg{i}", [P, N]) for i in range(2)]
        pr = s.ps("pr", [P, NB, D])
        sem = {n: s.sem(n) for n in (
            "in_used", "issued", "h_ready", "agg_half", "aggT_half", "pr_ready", "pr_read", "res_ready", "res_free", "stored")}
        loaded = [s.sem(f"loaded{i}") for i in range(2)]
        with nc.Block() as block:
            @block.sync
            def _(sp):
                def body(b, par, last):
                    sp.wait_ge(sem["in_used"], b + 1)
                    sp.sem_inc(sem["issued"], 1)
                    sp.dma_start(rowbin[par][:], graph(scratch["rowbin"], b)).then_inc(loaded[par], 16)
                per_pair(sp, B, body)

            @block.gpsimd
            def _(pool):
                pool.sem_inc(sem["res_free"], 2)

                def body(b, par, last):
                    pool.wait_ge(sem["res_ready"], b + 1)
                    pool.dma_start(graph(out, b), res[par][:]).then_inc(sem["stored"], 16)
                    pool.wait_ge(sem["stored"], b * 16 + 16)
                    pool.sem_inc(sem["res_free"], 1)
                per_pair(pool, B, body)

            @block.tensor
            def _(pe):
                t = nc.tensor
                pe.sem_inc(sem["in_used"], 2)

                def body(b, par, last):
                    pe.wait_ge(sem["h_ready"], b + 1)
                    pe.wait_ge(loaded[par], (b - par) * 8 + 16)
                    for hf in range(NH):
                        sl = slice(hf * HALF, (hf + 1) * HALF)
                        for jb in range(NB):
                            for q in range(3):
                                mm = t.matmul(agg[par][:, sl], parts[par][:, q, jb, :], rowbin[par][:, jb, sl],
                                              start=(jb == 0 and q == 0), stop=(jb == NB - 1 and q == 2))
                        mm.then_inc(sem["agg_half"], 1)
                    pe.drain().then_inc(sem["in_used"], 1)
                    pe.wait_ge(sem["pr_read"], b + 1)
                    for hf in range(NH):
                        pe.wait_ge(sem["aggT_half"], b * NH + hf + 1)
                        for ib in range(hf * HB, (hf + 1) * HB):
                            mm = t.matmul(pr[:, ib, :], aggT[:, ib * P:(ib + 1) * P], K["U"][:], start=True, stop=True)
                    mm.then_inc(sem["pr_ready"], 1)
                per_pair(pe, B, body)

            @block.scalar
            def _(act):
                norm_root(nc, act, w, 0)

                def body(b, par, last):
                    if not last:
                        norm_root(nc, act, w, b + 1)
                    for hf in range(NH):
                        act.wait_ge(sem["agg_half"], b * NH + hf + 1)
                        sl = slice(hf * HALF, (hf + 1) * HALF)
                        act.wait_ge(sem["pr_read"], b + 1)
                        nc.scalar.activation(aggT[:, sl], agg[par][:, sl], ACT.Copy).then_inc(sem["aggT_half"], 1)
                per_pair(act, B, body)

            @block.vector
            def _(dve):
                v = nc.vector
                dve.sem_inc(sem["pr_read"], 1)
                v.reciprocal(rcol[:], K["colsum"][:])

                def prepare(b, par):
                    pt = parts[par]
                    norm_relu_vector(nc, dve, tiles(K["X"], b, NB), h[:], w, b)
                    dve.drain()
                    v.tensor_copy(pt[:, 0], h[:])
                    dve.drain()
                    v.tensor_tensor(rest[:], h[:], pt[:, 0], ALU.subtract)
                    dve.drain()
                    v.tensor_copy(pt[:, 1], rest[:])
                    dve.drain()
                    v.tensor_tensor(pt[:, 2], rest[:], pt[:, 1], ALU.subtract).then_inc(sem["h_ready"], 1)
                    dve.drain()

                def finish(b, par):
                    cols = bass.ds(b * NB, NB)
                    dve.wait_ge(sem["pr_ready"], b + 1)
                    v.tensor_tensor(y[:], pr[:], along_features(rcol[:, cols], D), ALU.mult)
                    dve.drain().then_inc(sem["pr_read"], 1)
                    dve.wait_ge(sem["res_free"], b + 1)
                    v.scalar_tensor_tensor(res[par][:], y[:], 0.0, tiles(K["X"], b, NB), ALU.max, ALU.add)\
                        .then_inc(sem["res_ready"], 1)
                    dve.drain()

                prepare(0, 0)

                def body(b, par, last):
                    if not last:
                        prepare(b + 1, 1 - par)
                    finish(b, par)
                per_pair(dve, B, body)


def build_program(nc, A, out):
    z = Shapes(A["x"], A["adj_rows"])
    B, N, D, T = z.B, z.N, z.D, z.T
    scratch = {"rowbin": nc.dram_tensor("rowbin", (B, N, N), BF16, kind="Internal").ap(),
               "rem": nc.dram_tensor("rem", (B, N, N), BF16, kind="Internal").ap(),
               "curT": nc.dram_tensor("curT", (B, N, N), BF16, kind="Internal").ap(),
               "keptT": nc.dram_tensor("keptT", (B, N, N), F32, kind="Internal").ap()}
    with ExitStack() as ctx:
        K = {}

        def resident(name, shape, dt=F32):
            K[name] = ctx.enter_context(nc.sbuf_tensor(f"k_{name}", shape, dt))
        resident("X", [P, T, D])
        for n in ("Wr0", "Wr1", "Wr2", "Wx0", "Wx1", "Wx2", "W2", "U", "ident"):
            resident(n, [P, P])
        resident("Wl", [P, 3, D])
        resident("vec", [P, NVEC, D])
        resident("av", [P, 2, D])
        resident("ac", [P, 3])
        resident("onescol", [P, 2])
        for n in ("mask", "mask2", "maskok", "rowsum", "colsum", "rdeg", "rscale", "rbias", "rdist"):
            resident(n, [P, T])
        resident("bnscale", [P, D])
        resident("bnshift", [P, D])
        resident("ident16", [P, P], BF16)
        resident("ones16", [P, 2], BF16)
        resident("upper", [P, P], BF16)
        resident("tri", [P, N], BF16)
        constants_phase(nc, z, A, K)
        attention_phase(nc, z, A, K)
        removal_phase(nc, z, A, K, scratch)
        keep_phase(nc, z, A, K, scratch)
        resident("r", [P, T, D])
        for layer in range(3):
            sage_phase(nc, z, A, K, scratch, layer)
        gcn_phase(nc, z, A, K)
        maxdeg_phase(nc, z, A, K, scratch, out)


_VECTORS = ["L0_gnn_W_w", "L0_gnn_W_b", "L0_gnn_a_w", "L0_gnn_a_b", "L1_gnn_Wr1", "L1_gnn_Wx1", "L1_gnn_b1", "L1_gnn_g1",
            "L1_gnn_be1", "L1_gnn_Wr2", "L1_gnn_Wx2", "L1_gnn_b2", "L1_gnn_g2", "L1_gnn_be2", "L1_gnn_Wr3", "L1_gnn_Wx3",
            "L1_gnn_b3", "L1_gnn_g3", "L1_gnn_be3", "L1_gnn_Wl", "L1_gnn_bl", "L2_gnn_weight", "L2_gnn_bias", "L3_gnn_U"]


def kernel(**inputs):
    import numpy as _np
    import concourse.bacc as _bacc
    from concourse import mybir as _mybir
    from concourse.bass_utils import run_bass_kernel_spmd as _run

    nc = _bacc.Bacc("TRN2", target_bir_lowering=False, num_devices=1)
    arrays = {"x": _np.ascontiguousarray(inputs["x"]), "nodemask": _np.ascontiguousarray(inputs["nodemask"]),
              "adj_rows": _np.ascontiguousarray(inputs["adj"]),
              "adj_cols": _np.ascontiguousarray(_np.asarray(inputs["adj"]).transpose(0, 2, 1))}
    for name in _VECTORS:
        arrays[name] = _np.ascontiguousarray(inputs[name])
        if arrays[name].ndim == 0:
            arrays[name] = arrays[name].reshape(1)
    A, feed = {}, {}
    for name, a in arrays.items():
        A[name] = nc.dram_tensor(f"in_{name}", a.shape, _mybir.dt.from_np(a.dtype), kind="ExternalInput").ap()
        feed[f"in_{name}"] = a
    out = nc.dram_tensor("out_x", arrays["x"].shape, F32, kind="ExternalOutput").ap()
    build_program(nc, A, out)
    r = _run(nc, [feed], core_ids=[0])
    return r.results[0]["out_x"]
```

```python
from contextlib import ExitStack

import concourse.bass as bass
from concourse import mybir

ALU = mybir.AluOpType
ACT = mybir.ActivationFunctionType
F32 = mybir.dt.float32
BF16 = mybir.dt.bfloat16
F16 = mybir.dt.float16
I32 = mybir.dt.int32
AX = mybir.AxisListType.X

P = 128
HALF = 512
LN_EPS = 1e-5
BN_EPS = 1e-5
NORM_EPS = 1e-12
DENSE_ROW = 10.0
FAST_ROUNDS = 4
ROUND = float(2 ** 23)

(V_WB, V_B1, V_B2, V_B3, V_BL, V_G1, V_G2, V_G3, V_E1, V_E2, V_E3, V_BIAS2) = range(12)
NVEC = 12
W_COLS = 13


class Shapes:
    def __init__(self, x, adj):
        self.B, self.N, self.D = x.shape
        self.NB = self.N // P
        self.T = self.B * self.NB
        self.NH = self.N // HALF
        self.HB = HALF // P
        assert self.D == P and self.B % 2 == 0 and self.N % HALF == 0


def per_pair(engine, B, body):
    if B > 2:
        with engine.Fori(0, B // 2 - 1) as g:
            for parity in range(2):
                body(g * 2 + parity, parity, False)
    for parity in range(2):
        body(B - 2 + parity, parity, parity == 1)


def block_rows(tensor3, b, nb):
    g = tensor3[b] if isinstance(b, int) else tensor3[bass.ds(b, 1)].rearrange("o m n -> (o m) n")
    return g[nb * P:(nb + 1) * P, :]


def graph(tensor3, b):
    if isinstance(b, int):
        return tensor3[b].rearrange("(t p) n -> p t n", p=P)
    return tensor3[bass.ds(b, 1)].rearrange("o (t p) n -> p (o t) n", p=P)


def tiles(tensor, b, nb):
    return tensor[:, bass.ds(b * nb, nb)] if not isinstance(b, int) else tensor[:, b * nb:(b + 1) * nb]


def along_features(col, d):
    return col.unsqueeze(2).to_broadcast([P, col.shape[1], d])


def along_tiles(row, t):
    return row.unsqueeze(1).to_broadcast([P, t, row.shape[1]])


def norm_buffers(sb, sem, tag, NB, D):
    return dict(stat=sb(f"{tag}_stat", [P, 6, NB], F32), junk=sb(f"{tag}_junk", [P, NB, D], F32),
                mean_ready=sem(f"{tag}_mean_ready"), std_ready=sem(f"{tag}_std_ready"), scale_ready=sem(f"{tag}_scale_ready"),
                passed=sem(f"{tag}_passed"))


def norm_mean(nc, dve, x, w):
    s, v = w["stat"], nc.vector
    v.tensor_reduce(s[:, 0, :], x, AX, ALU.add)
    dve.drain()
    v.tensor_scalar(s[:, 1, :], s[:, 0, :], -1.0 / x.shape[2], None, ALU.mult).then_inc(w["mean_ready"], 1)


def norm_scale(nc, dve, w, b):
    s, v = w["stat"], nc.vector
    dve.wait_ge(w["std_ready"], b + 1)
    v.reciprocal(s[:, 4, :], s[:, 3, :])
    dve.drain()
    v.tensor_tensor(s[:, 5, :], s[:, 4, :], s[:, 1, :], ALU.mult).then_inc(w["scale_ready"], 1)


def norm_root(nc, act, K, x, w, b, D):
    s, a = w["stat"], nc.scalar
    act.drain()
    act.wait_ge(w["mean_ready"], b + 1)
    act.sem_inc(w["passed"], 1)
    for t in range(s.shape[2]):
        a.activation(w["junk"][:, t, :], x(t), ACT.Square, bias=s[:, 1, t:t + 1], accum_out=s[:, 2, t:t + 1])
    act.drain()
    a.activation(s[:, 3, :], s[:, 2, :], ACT.Sqrt, bias=K["eps"][:, 0:1], scale=1.0 / D).then_inc(w["std_ready"], 1)


def norm_apply(nc, act, x, out, w, b, done):
    s = w["stat"]
    act.wait_ge(w["scale_ready"], b + 1)
    act.sem_inc(w["passed"], 1)
    for t in range(s.shape[2]):
        last = nc.scalar.activation(out[:, t, :], x(t), ACT.Relu, bias=s[:, 5, t:t + 1], scale=s[:, 4, t:t + 1])
    last.then_inc(done, 1)


class GraphStream:

    def __init__(self, z, sb, sem, sources):
        self.B, self.NB, self.sources, self.stage = z.B, z.NB, sources, 0
        self.buffers = [sb(f"adjT{i}", [P, z.NB, z.N], F32) for i in range(2)]
        self.loaded = [sem(f"loaded{i}") for i in range(2)]

    def load(self, sp, source, b, par):
        hb = self.NB // 2
        for c in range(2):
            sp.dma_start(self.buffers[par][:, c * hb:(c + 1) * hb, :],
                         graph(source, b)[:, c * hb:(c + 1) * hb, :]).then_inc(self.loaded[par], 16)

    def wait_loaded(self, engine, b, par):
        engine.wait_ge(self.loaded[par], (b - par) * 16 + (32 + self.stage * self.B * 16))

    def sync_program(self, sp, used, issued):
        if self.stage == 0:
            for b in range(2):
                self.load(sp, self.sources[0], b, b)

        def body(b, par, last):
            more = not (isinstance(b, int) and b >= self.B - 2)
            if more or self.stage + 1 < len(self.sources):
                sp.wait_ge(used, b + 1)
                sp.sem_inc(issued, 1)
                self.load(sp, self.sources[self.stage + (0 if more else 1)], b + 2 if more else par, par)
        per_pair(sp, self.B, body)


class Scope:

    def __init__(self, nc, tag):
        self.nc, self.tag, self.stack = nc, tag, ExitStack()
        self.sems = []

    def __enter__(self):
        self.stack.__enter__()
        return self

    def __exit__(self, *e):
        if e[0] is None:
            self.nc.clear_and_free_semaphores(self.sems)
            self.nc.all_engine_barrier(sem_only=True)
        return self.stack.__exit__(*e)

    def sb(self, name, shape, dt):
        return self.stack.enter_context(self.nc.sbuf_tensor(f"{self.tag}_{name}", shape, dt))

    def ps(self, name, shape, dt=F32):
        return self.stack.enter_context(self.nc.psum_tensor(f"{self.tag}_{name}", shape, dt))

    def sem(self, name):
        self.sems.append(self.nc.alloc_semaphore(f"{self.tag}_{name}"))
        return self.sems[-1]


def constants_phase(nc, z, A, K):
    D, T, B = z.D, z.T, z.B
    with Scope(nc, "con") as s:
        rows = s.sb("rows", [1, NVEC, D], F32)
        ab = s.sb("ab", [1, 1], F32)
        ones1 = s.sb("ones1", [1, P], F32)
        onesf = s.sb("onesf", [P, P], F32)
        acol = s.sb("acol", [P, 2], F32)
        abc = s.sb("abc", [P, 2, P], F32)
        wbcol = s.sb("wbcol", [P, 1], F32)
        Ww = s.sb("Ww", [P, D], F32)
        maski = s.sb("maski", [T, P], I32)
        maskf = s.sb("maskf", [T, P], F32)
        pm = s.ps("pm", [P, T])
        pbig = [s.ps(f"pbig{i}", [P, 512]) for i in range(3)]
        pv = s.ps("pv", [P, 2, D])
        pc = s.ps("pc", [P, 4])
        loaded, set0, const_ready = s.sem("loaded"), s.sem("set0"), s.sem("const_ready")
        rows_spread, abc_ready, v_done = s.sem("rows_spread"), s.sem("abc_ready"), s.sem("v_done")
        mask_ready, mask_turned = s.sem("mask_ready"), s.sem("mask_turned")
        vecs = [(A["L0_gnn_W_b"], V_WB), (A["L1_gnn_b1"], V_B1), (A["L1_gnn_b2"], V_B2), (A["L1_gnn_b3"], V_B3),
                (A["L1_gnn_bl"], V_BL), (A["L1_gnn_g1"], V_G1), (A["L1_gnn_g2"], V_G2), (A["L1_gnn_g3"], V_G3),
                (A["L1_gnn_be1"], V_E1), (A["L1_gnn_be2"], V_E2), (A["L1_gnn_be3"], V_E3), (A["L2_gnn_bias"], V_BIAS2)]
        weights = [("Wr0", A["L1_gnn_Wr1"]), ("Wr1", A["L1_gnn_Wr2"]), ("Wr2", A["L1_gnn_Wr3"]),
                   ("Wx0", A["L1_gnn_Wx1"]), ("Wx1", A["L1_gnn_Wx2"]), ("Wx2", A["L1_gnn_Wx3"]),
                   ("W2", A["L2_gnn_weight"]), ("U", A["L3_gnn_U"])]
        n_loads = len(vecs) + len(weights) + 8
        with nc.Block() as block:
            @block.sync
            def _(sp):
                for src, i in vecs:
                    sp.dma_start(rows[:, i, :], src.rearrange("(o d) -> o d", o=1)).then_inc(loaded, 16)
                sp.dma_start(ab[:], A["L0_gnn_a_b"].rearrange("(o d) -> o d", o=1)).then_inc(loaded, 16)
                for i in range(2):
                    sp.dma_start(acol[:, i:i + 1], A["L0_gnn_a_w"][i * P:(i + 1) * P].rearrange("(p o) -> p o", o=1))\
                        .then_inc(loaded, 16)
                sp.dma_start(wbcol[:], A["L0_gnn_W_b"].rearrange("(p o) -> p o", o=1)).then_inc(loaded, 16)
                sp.dma_start(Ww[:], A["L0_gnn_W_w"]).then_inc(loaded, 16)
                for name, src in weights:
                    sp.dma_start(K[name][:], src).then_inc(loaded, 16)
                sp.dma_start(K["Wl"][:], A["L1_gnn_Wl"].rearrange("(t p) e -> p t e", p=P)).then_inc(loaded, 16)
                sp.dma_start(maski[:], A["nodemask"].rearrange("b (t p) -> (b t) p", p=P)).then_inc(loaded, 16)
                sp.dma_start(K["X"][:], A["x"].rearrange("b (t p) d -> p (b t) d", p=P)).then_inc(loaded, 16)

            @block.gpsimd
            def _(pool):
                p = nc.gpsimd
                p.memset(K["ident"][:], 0.0)
                p.memset(K["ident16"][:], 0.0)
                p.memset(K["tri"][:], 1.0)
                p.memset(K["upper"][:], 1.0)
                p.memset(K["ones16"][:], 1.0)
                p.memset(onesf[:], 1.0)
                p.memset(K["onescol"][:], 1.0)
                p.memset(K["eps"][:], LN_EPS)
                p.memset(ones1[:], 1.0).then_inc(set0, 1)
                pool.wait_ge(set0, 1)
                for m in (K["ident"], K["ident16"]):
                    p.affine_select(out=m[:], in_=m[:], compare_op=ALU.not_equal, fill=1.0, base=0,
                                    pattern=[[-1, P]], channel_multiplier=1)
                p.affine_select(out=K["tri"][:], in_=K["tri"][:], compare_op=ALU.is_ge, fill=0.0, base=0,
                                pattern=[[1, z.N]], channel_multiplier=-1)
                p.affine_select(out=K["upper"][:], in_=K["upper"][:], compare_op=ALU.is_ge, fill=0.0, base=-1,
                                pattern=[[1, P]], channel_multiplier=-1).then_inc(const_ready, 1)

            @block.tensor
            def _(pe):
                pe.wait_ge(const_ready, 1)
                pe.wait_ge(loaded, 16 * n_loads)
                flat = rows[:].rearrange("o v d -> o (v d)")
                for i in range(3):
                    nc.tensor.matmul(pbig[i][:], ones1[:], flat[:, i * 512:(i + 1) * 512], start=True, stop=True)
                nc.tensor.matmul(pc[:, 2:3], ones1[:], ab[:], start=True, stop=True).then_inc(rows_spread, 1)
                pe.wait_ge(mask_ready, 1)
                nc.tensor.transpose(pm[:], maskf[:], K["ident"][0:T, 0:T]).then_inc(mask_turned, 1)
                pe.wait_ge(abc_ready, 1)
                for h in range(2):
                    nc.tensor.matmul(pv[:, h, :], abc[:, h, :], Ww[:], start=True, stop=True)
                    last = nc.tensor.matmul(pc[:, h:h + 1], abc[:, h, :], wbcol[:], start=True, stop=True)
                last.then_inc(v_done, 1)

            @block.vector
            def _(dve):
                v = nc.vector
                dve.wait_ge(const_ready, 1)
                dve.wait_ge(loaded, 16 * n_loads)
                for h in range(2):
                    last = v.tensor_scalar(abc[:, h, :], onesf[:], acol[:, h:h + 1], None, ALU.mult)
                last.then_inc(abc_ready, 1)
                v.tensor_copy(maskf[:], maski[:]).then_inc(mask_ready, 1)
                dve.wait_ge(mask_turned, 1)
                v.tensor_copy(K["mask"][:], pm[:])
                dve.drain()
                v.tensor_tensor(K["mask2"][:], K["mask"][:], K["mask"][:], ALU.mult)
                v.tensor_scalar(K["maskok"][:], K["mask"][:], 0.0, None, ALU.not_equal)
                dve.wait_ge(rows_spread, 1)
                for i in range(3):
                    v.tensor_copy(K["vec"][:, 4 * i:4 * i + 4, :].rearrange("p v d -> p (v d)"), pbig[i][:])
                dve.wait_ge(v_done, 1)
                v.tensor_copy(K["av"][:], pv[:])
                v.tensor_copy(K["ac"][:], pc[:, 0:3])
                dve.drain()
                v.tensor_tensor(K["ac"][:, 0:1], K["ac"][:, 0:1], K["ac"][:, 2:3], ALU.add)


def removal_parameters(nc, dve, k, base, w):
    v = nc.vector
    num0, half0, shift, masked = (base[:, i] for i in range(4))
    scale, bias, dist, num, y, fh, s2, inv, par, t, g, b, d1 = (w[:, i] for i in range(W_COLS))
    v.scalar_tensor_tensor(y, k, -0.5, half0, ALU.mult, ALU.add)
    v.tensor_tensor(num, num0, k, ALU.subtract)
    dve.drain()
    v.tensor_scalar(fh, y, ROUND, -ROUND, ALU.add, ALU.add)
    v.tensor_scalar(s2, num, DENSE_ROW, 2.0, ALU.is_gt, ALU.mult)
    v.tensor_scalar(scale, num, DENSE_ROW, 4.0, ALU.is_gt, ALU.mult)
    v.scalar_tensor_tensor(inv, num, 2.0, masked, ALU.is_lt, ALU.max)
    dve.drain()
    v.scalar_tensor_tensor(par, fh, -2.0, num, ALU.mult, ALU.add)
    v.scalar_tensor_tensor(t, fh, 2.0, shift, ALU.mult, ALU.add)
    dve.drain()
    v.scalar_tensor_tensor(g, par, 0.5, fh, ALU.is_lt, ALU.mult)
    dve.drain()
    v.tensor_tensor(b, t, g, ALU.subtract)
    v.tensor_tensor(d1, g, s2, ALU.mult)
    dve.drain()
    v.scalar_tensor_tensor(dist, inv, -4096.0, d1, ALU.mult, ALU.add)
    return v.tensor_tensor(bias, b, s2, ALU.mult)


def removal_phase(nc, z, A, K, scratch):
    B, N, NB = z.B, z.N, z.NB
    CH = B // 2
    R, SLOW = FAST_ROUNDS, P
    width = (N, N - P)
    with Scope(nc, "rem") as s:
        an = [s.sb(f"an{i}", [P, 2, N], F32) for i in range(2)]
        ac = [s.sb(f"ac{i}", [P, 2, N], F32) for i in range(2)]
        rowbin = [s.sb(f"rowbin{i}", [P, B, N], BF16) for i in range(2)]
        curT = [s.sb(f"curT{i}", [P, B, width[i]], BF16) for i in range(2)]
        rank = [s.sb(f"rank{i}", [P, B, width[i]], F16) for i in range(2)]
        both = s.sb("both", [P, B, P], BF16)
        rem = s.sb("rem", [P, B, P], BF16)
        lostto = s.sb("lostto", [P, B, N - P], BF16)
        dist = [s.sb(f"dist{i}", [P, N - P], F32) for i in range(2)]
        distd = s.sb("distd", [P, B, P], F32)
        junk = s.sb("junk", [P, N], BF16)
        w = s.sb("w", [P, W_COLS, B], F32)
        base = s.sb("base", [P, 4, B], F32)
        unshift = s.sb("unshift", [P, B], F32)
        num0 = [s.sb(f"num0{i}", [P, B], F32) for i in range(2)]
        rlast = s.sb("rlast", [P, B], F16)
        k, kprev = s.sb("k", [P, B], F32), s.sb("kprev", [P, B], F32)
        moved, movedsum = s.sb("moved", [P, B], F32), s.sb("movedsum", [P, 1], F32)
        flag = s.sb("flag", [1, 1], I32)
        Kc = s.sb("Kc", [P, NB, B], F32)
        pk = s.ps("pk", [P, B])
        pl = s.ps("pl", [P, NB, B])
        pf = s.ps("pf", [1, 1])
        loaded = [s.sem(f"loaded{i}") for i in range(2)]
        compared, counted = s.sem("compared"), s.sem("counted")
        par_ready, dist_ready = s.sem("par_ready"), s.sem("dist_ready")
        rem_ready, lost_ready, moved_ready, flag_sum, flag_ready = (s.sem(n) for n in (
            "rem_ready", "lost_ready", "moved_ready", "flag_sum", "flag_ready"))
        spar, sdist, srem, slost, sback = (s.sem(n) for n in ("slow_par", "slow_dist", "slow_rem", "slow_lost", "slow_back"))
        fpar, fdist, ffree, fullrem, lost_far = (s.sem(n) for n in ("full_par", "full_dist", "full_free", "full_rem", "lost_far"))
        bins_ready, cur_ready = s.sem("bins_ready"), s.sem("cur_ready")
        stored = [s.sem(f"stored{i}") for i in range(2)]
        stores = [3] * (NB - 1) + [2]

        def stored_before(nb):
            return 16 * sum(stores[nb % 2:nb:2])

        with nc.Block() as block:
            @block.sync
            def _(sp):
                for i in range(NB * CH):
                    nb, c = divmod(i, CH)
                    rows, gs = slice(nb * P, (nb + 1) * P), slice(2 * c, 2 * c + 2)
                    if i >= 2:
                        sp.wait_ge(compared, i - 1)
                    sp.dma_start(an[i % 2][:], A["adj_rows"][gs, rows, :].rearrange("b p n -> p b n")).then_inc(loaded[i % 2], 16)
                    sp.dma_start(ac[i % 2][:, :, 0:N - nb * P],
                                 A["adj_cols"][gs, rows, nb * P:N].rearrange("b p n -> p b n")).then_inc(loaded[i % 2], 16)

            @block.gpsimd
            def _(pool):
                for nb in range(NB):
                    rows, n0, W = slice(nb * P, (nb + 1) * P), nb * P, N - nb * P
                    done = stored[nb % 2]
                    pool.wait_ge(bins_ready, CH * (nb + 1))
                    pool.dma_start(scratch["rowbin"][:, rows, :].rearrange("b p n -> p b n"), rowbin[nb % 2][:]).then_inc(done, 16)
                    pool.wait_ge(cur_ready, nb + 1)
                    pool.dma_start(scratch["curT"][:, rows, n0:N].rearrange("b p n -> p b n"),
                                   curT[nb % 2][:, :, 0:W]).then_inc(done, 16)
                    if W > P:
                        pool.dma_start(scratch["rem"][:, rows, n0 + P:N].rearrange("b p n -> p b n"),
                                       rank[nb % 2][:, :, P:W].bitcast(BF16)).then_inc(done, 16)
                for i in range(2):
                    pool.wait_ge(stored[i], 16 * sum(stores[i::2]))

            @block.scalar
            def _(act):
                def count(i):
                    nb, c = divmod(i, CH)
                    act.wait_ge(bins_ready, i + 1)
                    for b in (2 * c, 2 * c + 1):
                        nc.scalar.activation(junk[:], rowbin[nb % 2][:, b, :], ACT.Copy, accum_out=num0[nb % 2][:, b:b + 1])
                        act.drain()
                    if c == CH - 1:
                        act.drain().then_inc(counted, 1)

                def distances(nb, ready, n, done):
                    act.wait_ge(ready, n)
                    for b in range(B):
                        nc.scalar.activation(distd[:, b, :], rank[nb % 2][:, b, 0:P], ACT.Abs, bias=w[:, 1, b:b + 1],
                                             scale=w[:, 0, b:b + 1]).then_inc(done, 1)

                for c in range(CH):
                    count(c)
                for nb in range(NB):
                    todo = list(range((nb + 1) * CH, (nb + 2) * CH)) if nb < NB - 1 else []
                    for t in range(R):
                        distances(nb, par_ready, nb * R + t + 1, dist_ready)
                        if todo:
                            count(todo.pop(0))
                    for i in todo:
                        count(i)
                    act.wait_ge(flag_ready, nb + 1)
                    go = act.value_load(flag[0:1, 0:1], min_val=0, max_val=1)
                    with act.If(go > 0):
                        with act.Fori(0, SLOW) as t:
                            distances(nb, spar, t + 1, sdist)
                    W = N - nb * P
                    if W > P:
                        act.wait_ge(fpar, nb + 1)
                        for b in range(B):
                            act.wait_ge(ffree, nb * B + b + 1)
                            nc.scalar.activation(dist[b % 2][:, 0:W - P], rank[nb % 2][:, b, P:W], ACT.Abs,
                                                 bias=w[:, 1, b:b + 1], scale=w[:, 0, b:b + 1]).then_inc(fdist, 1)

            @block.tensor
            def _(pe):
                def lost(ready, n, done):
                    pe.wait_ge(ready, n)
                    for b in range(B):
                        mm = nc.tensor.matmul(pk[:, b:b + 1], rem[:, b, :], K["ones16"][:, 0:1], start=True, stop=True)
                    mm.then_inc(done, 1)

                for nb in range(NB):
                    for t in range(R):
                        lost(rem_ready, nb * R + t + 1, lost_ready)
                    pe.wait_ge(moved_ready, nb + 1)
                    nc.tensor.matmul(pf[:], movedsum[:], K["onescol"][:, 0:1], start=True, stop=True).then_inc(flag_sum, 1)
                    pe.wait_ge(flag_ready, nb + 1)
                    go = pe.value_load(flag[0:1, 0:1], min_val=0, max_val=1)
                    with pe.If(go > 0):
                        with pe.Fori(0, SLOW) as t:
                            lost(srem, t + 1, slost)
                    if nb < NB - 1:
                        pe.wait_ge(fullrem, nb + 1)
                        for jb in range(nb + 1, NB):
                            for b in range(B):
                                o = (jb - nb - 1) * P
                                mm = nc.tensor.matmul(pl[:, jb, b:b + 1], lostto[:, b, o:o + P], K["ones16"][:, 0:1],
                                                      start=True, stop=True)
                        mm.then_inc(lost_far, 1)

            @block.vector
            def _(dve):
                v = nc.vector
                v.memset(Kc[:], 0.0)
                dve.sem_inc(ffree, 2)
                dve.drain()

                def compare(i):
                    nb, c = divmod(i, CH)
                    n0, W = nb * P, N - nb * P
                    gs = slice(2 * c, 2 * c + 2)
                    if c == 0 and nb >= 2:
                        dve.wait_ge(stored[nb % 2], stored_before(nb))
                    dve.wait_ge(loaded[i % 2], 32 * (i // 2 + 1))
                    v.tensor_scalar(rowbin[nb % 2][:, gs, :], an[i % 2][:], 0.0, None, ALU.is_gt).then_inc(bins_ready, 1)
                    v.tensor_scalar(curT[nb % 2][:, gs, 0:W], ac[i % 2][:, :, 0:W], 0.0, None, ALU.is_gt)
                    dve.drain().then_inc(compared, 1)
                    for b in (2 * c, 2 * c + 1):
                        v.tensor_tensor_scan(rank[nb % 2][:, b, 0:W], K["ones16"][:, 0:1].to_broadcast([P, W]), rowbin[nb % 2][:, b, n0:N], 0.0,
                                             ALU.mult, ALU.add)

                def one_round(ready, dready, drem, dlost, dn, n, nb, chunk=None):
                    removal_parameters(nc, dve, k[:], base, w).then_inc(ready, 1)
                    v.tensor_copy(kprev[:], k[:])
                    if chunk is not None:
                        compare(chunk)
                    for b in range(B):
                        dve.wait_ge(dready, dn + (b + 1))
                        last = v.scalar_tensor_tensor(rem[:, b, :], distd[:, b, :], w[:, 2, b:b + 1], both[:, b, :],
                                                      ALU.is_equal, ALU.mult)
                    last.then_inc(drem, 1)
                    dve.wait_ge(dlost, n)
                    v.tensor_tensor(k[:], Kc[:, nb, :], pk[:], ALU.add)
                    dve.drain()

                for c in range(CH):
                    compare(c)
                for nb in range(NB):
                    n0, W = nb * P, N - nb * P
                    mask = K["maskok"][:].rearrange("p (b t) -> p t b", t=NB)[:, nb, :]
                    cT, rk, rb, n0count = curT[nb % 2], rank[nb % 2], rowbin[nb % 2], num0[nb % 2]
                    dve.drain()
                    v.tensor_tensor(both[:], rb[:, :, n0:n0 + P], cT[:, :, 0:P], ALU.mult)
                    v.tensor_copy(rlast[:], rk[:, :, W - 1])
                    v.tensor_copy(k[:], Kc[:, nb, :])
                    dve.drain()
                    dve.wait_ge(counted, nb + 1)
                    v.tensor_copy(base[:, 0], n0count[:])
                    v.tensor_scalar(base[:, 1], n0count[:], 0.5, -0.25, ALU.mult, ALU.add)
                    v.tensor_scalar(base[:, 2], rlast[:], -2.0, None, ALU.mult)
                    v.tensor_scalar(base[:, 3], mask, 0.0, None, ALU.is_equal)
                    v.tensor_tensor(both[:], both[:], K["upper"][:].unsqueeze(1).to_broadcast([P, B, P]), ALU.mult)
                    dve.drain()
                    todo = list(range((nb + 1) * CH, (nb + 2) * CH)) if nb < NB - 1 else []
                    for t in range(R):
                        one_round(par_ready, dist_ready, rem_ready, lost_ready, (nb * R + t) * B, nb * R + t + 1, nb,
                                  todo.pop(0) if todo else None)
                    for i in todo:
                        compare(i)
                    v.tensor_tensor(moved[:], k[:], kprev[:], ALU.not_equal)
                    dve.drain()
                    v.reduce_sum(movedsum[:], moved[:], AX).then_inc(moved_ready, 1)
                    dve.wait_ge(flag_sum, nb + 1)
                    v.tensor_scalar(flag[:], pf[:], 0.0, None, ALU.is_gt).then_inc(flag_ready, 1)
                    dve.wait_ge(flag_ready, nb + 1)
                    go = dve.value_load(flag[0:1, 0:1], min_val=0, max_val=1)
                    with dve.If(go > 0):
                        with dve.Fori(0, SLOW) as t:
                            one_round(spar, sdist, srem, slost, t * B, t + 1, nb)
                        for sm in (spar, sdist, srem, slost):
                            dve.sem_clear(sm)
                    removal_parameters(nc, dve, k[:], base, w).then_inc(fpar, 1)
                    dve.drain()
                    v.tensor_tensor(cT[:, :, 0:P], cT[:, :, 0:P], rem[:], ALU.subtract)
                    if W > P:
                        rem_far = rk[:, :, P:W].bitcast(BF16)
                        for b in range(B):
                            dve.wait_ge(fdist, nb * B + b + 1)
                            v.scalar_tensor_tensor(rem_far[:, b, :], dist[b % 2][:, 0:W - P], w[:, 2, b:b + 1],
                                                   rb[:, b, n0 + P:N], ALU.is_equal, ALU.mult).then_inc(ffree, 1)
                        dve.drain()
                        v.tensor_tensor(lostto[:, :, 0:W - P], rem_far, cT[:, :, P:W], ALU.mult)
                        dve.drain().then_inc(fullrem, 1)
                        v.tensor_tensor(cT[:, :, P:W], cT[:, :, P:W], lostto[:, :, 0:W - P], ALU.subtract)
                    dve.drain().then_inc(cur_ready, 1)
                    rscale, rbias, rdist = (K[n][:].rearrange("p (b t) -> p t b", t=NB)[:, nb, :]
                                            for n in ("rscale", "rbias", "rdist"))
                    v.scalar_tensor_tensor(unshift[:], w[:, 3], -2.0, base[:, 2], ALU.mult, ALU.subtract)
                    v.tensor_copy(rscale, w[:, 0])
                    v.tensor_copy(rdist, w[:, 2])
                    dve.drain()
                    v.tensor_tensor(unshift[:], unshift[:], w[:, 6], ALU.mult)
                    dve.drain()
                    v.tensor_tensor(rbias, w[:, 1], unshift[:], ALU.add)
                    if nb < NB - 1:
                        dve.wait_ge(lost_far, nb + 1)
                        v.tensor_tensor(Kc[:, nb + 1:NB, :], Kc[:, nb + 1:NB, :], pl[:, nb + 1:NB, :], ALU.add)
                        dve.drain()


def keep_attention_phase(nc, z, A, K, scratch):
    B, N, NB, NH, HB, D = z.B, z.N, z.NB, z.NH, z.HB, z.D
    W = D + 2
    QB = NB // 2
    pieces = [(nb, hf * HALF, min((hf + 1) * HALF, (nb + 1) * P)) for nb in range(NB) for hf in range(NH)
              if hf * HALF < (nb + 1) * P]
    NR, NM, NA = 3, 2, 2
    NC, CB = NB // 2, 2
    cur0 = [sum((NB - i) * P for i in range(j)) for j in range(NB + 1)]
    bin0 = [sum((i + 1) * P for i in range(j)) for j in range(NB + 1)]
    assert len(pieces) % NR == 0 and (NB * NH) % NM == 0 and QB % NA == 0
    with Scope(nc, "keep") as s:
        cur = [s.sb(f"cur{i}", [P, cur0[NB]], BF16) for i in range(2)]
        rowbin = s.sb("rowbin", [P, bin0[NB]], BF16)
        adjT = [s.sb(f"adjT{i}", [P, NB, N], F32) for i in range(2)]
        rem = [s.sb(f"rem{i}", [P, NB, N], BF16) for i in range(2)]
        dist = [s.sb(f"dist{i}", [P, HALF], F32) for i in range(NR)]
        keptsum = s.sb("keptsum", [P, N], F32)
        rhs = [s.sb(f"rhs{i}", [P, NB, W], F32) for i in range(2)]
        G = [s.sb(f"G{i}", [P, NB], F32) for i in range(2)]
        h = s.sb("h", [P, NB, D], F32)
        w = norm_buffers(s.sb, s.sem, "n", NB, D)
        t1 = w["junk"]
        colsink = s.sb("colsink", [P, N], BF16)
        sj = s.sb("sj", [P, 2, NB], F32)
        E = s.sb("E", [P, NB], F32)
        y = s.sb("y", [P, 2, D], F32)
        q4 = s.sb("q4", [P, 3, 2], F32)
        test = s.sb("test", [P, 2, NB], F32)
        prank = [s.ps(f"prank{i}", [P, HALF]) for i in range(NR)]
        pboth = [s.ps(f"pboth{i}", [P, HALF]) for i in range(NM)]
        acc = [s.ps(f"acc{i}", [P, 2, 256]) for i in range(NA)]
        pdeg = s.ps("pdeg", [P, NB])
        loaded = [s.sem(f"loaded{i}") for i in range(2)]
        bin_loaded = s.sem("bin_loaded")
        adj_loaded = [s.sem(f"adj_loaded{i}") for i in range(2)]
        issued, cur_free, bin_free, rem_free, rank_ready, rank_read, dist_ready, dist_read = (s.sem(n) for n in (
            "issued", "cur_free", "bin_free", "rem_free", "rank_ready", "rank_read", "dist_ready", "dist_read"))
        rem_ready, both_ready, both_read, deg_ready, deg_read = (s.sem(n) for n in (
            "rem_ready", "both_ready", "both_read", "deg_ready", "deg_read"))
        h_ready, score_ready, exp_ready, rhs_ready, sums_ready, sums_read, col_summed = (s.sem(n) for n in (
            "h_ready", "score_ready", "exp_ready", "rhs_ready", "sums_ready", "sums_read", "col_summed"))
        masked, summed = s.sem("masked"), s.sem("summed")
        stored = [s.sem(f"stored{c}") for c in range(NC)]
        NP, NW = len(pieces), NB * NH
        n_loads = NB + (NB - 1)
        SHARE = NA * 2 * NB // NW
        assert SHARE * NW == NA * 2 * NB
        with nc.Block() as block:
            @block.sync
            def _(sp):
                def load_current(b, par):
                    sp.wait_ge(cur_free, b + 1)
                    sp.sem_inc(issued, 1)
                    for jb in range(NB):
                        sp.dma_start(cur[par][:, cur0[jb]:cur0[jb + 1]], block_rows(scratch["curT"], b, jb)[:, jb * P:N])\
                            .then_inc(loaded[par], 16)
                    sp.wait_ge(bin_free, b + 1)
                    sp.sem_inc(issued, 1)
                    for nb in range(NB):
                        sp.dma_start(rowbin[:, bin0[nb]:bin0[nb + 1]], block_rows(scratch["rowbin"], b, nb)[:, 0:(nb + 1) * P])\
                            .then_inc(bin_loaded, 16)

                def load_removals(b, par):
                    sp.wait_ge(rem_free, b + 1)
                    sp.sem_inc(issued, 1)
                    for nb in range(NB - 1):
                        sp.dma_start(rem[par][:, nb, (nb + 1) * P:N], block_rows(scratch["rem"], b, nb)[:, (nb + 1) * P:N])\
                            .then_inc(loaded[par], 16)

                def load_adjacency(b, par, c):
                    sl = slice(c * CB, (c + 1) * CB)
                    sp.dma_start(adjT[par][:, sl, :], graph(A["adj_cols"], b)[:, sl, :]).then_inc(adj_loaded[par], 16)

                for b in range(2):
                    for c in range(NC):
                        load_adjacency(b, b, c)
                    load_current(b, b)
                    load_removals(b, b)

                def body(b, par, last):
                    two_ahead = not (isinstance(b, int) and b + 2 >= B)
                    if two_ahead:
                        load_current(b + 2, par)
                    for c in range(NC):
                        sl = slice(c * CB, (c + 1) * CB)
                        sp.wait_ge(masked, b * NW + (c + 1) * CB * NH)
                        sp.sem_inc(issued, 1)
                        sp.dma_start(graph(scratch["keptT"], b)[:, sl, :], adjT[par][:, sl, :]).then_inc(stored[c], 16)
                    if two_ahead:
                        load_removals(b + 2, par)
                        for c in range(NC):
                            sp.wait_ge(stored[c], b * 16 + 16)
                            sp.sem_inc(issued, 1)
                            sp.wait_ge(summed, b * (NB - 1) + (c + 1) * CB - 1)
                            sp.sem_inc(issued, 1)
                            load_adjacency(b + 2, par, c)
                per_pair(sp, B, body)
                for c in range(NC):
                    sp.wait_ge(stored[c], 16 * B)

            @block.gpsimd
            def _(pool):
                g = nc.gpsimd

                def body(b, par, last):
                    pool.wait_ge(deg_read, b + 1)
                    for jb in range(1, NB):
                        pool.wait_ge(masked, b * NW + (jb + 1) * NH)
                        g.tensor_tensor(keptsum[:], adjT[par][:, 0, :] if jb == 1 else keptsum[:], adjT[par][:, jb, :], ALU.add)
                        pool.drain().then_inc(summed, 1)
                per_pair(pool, B, body)

            @block.tensor
            def _(pe):
                t = nc.tensor
                pe.sem_inc(cur_free, 2)
                pe.sem_inc(rem_free, 2)

                def ranks(b, par):
                    pe.wait_ge(loaded[par], (b - par) * (8 * n_loads) + 16 * n_loads)
                    for q, (nb, lo, hi) in enumerate(pieces):
                        pe.wait_ge(rank_read, b * NP + q + 1)
                        last_jb = min(nb, (hi - 1) // P)
                        for jb in range(last_jb + 1):
                            a = max(jb * P, lo)
                            mm = t.matmul(prank[q % NR][:, a - lo:hi - lo], cur[par][:, cur0[jb] + (nb - jb) * P:cur0[jb] + (nb - jb + 1) * P],
                                          K["tri"][:, a - jb * P:hi - jb * P], start=(jb == 0), stop=(jb == last_jb))
                        mm.then_inc(rank_ready, 1)
                    pe.drain().then_inc(cur_free, 1)

                def attention_inputs(b, par):
                    pe.wait_ge(rhs_ready, b + 1)
                    pe.wait_ge(adj_loaded[par], (b - par) * (8 * NC) + 16 * NC)

                def attention(b, par, first, last):
                    for m in range(first, last):
                        k, (e, jb) = m // (2 * NB), divmod(m % (2 * NB), NB)
                        if e == 0 and jb == 0:
                            pe.wait_ge(sums_read, b * QB + k + 1)
                        ib = 2 * k + e
                        mm = t.matmul(acc[k % NA][:, e, 0:W], adjT[par][:, jb, ib * P:(ib + 1) * P],
                                      rhs[par][:, jb, :], start=(jb == 0), stop=(jb == NB - 1))
                        if e == 1 and jb == NB - 1:
                            mm.then_inc(sums_ready, 1)

                def body(b, par, last):
                    if not last:
                        ranks(b + 1, 1 - par)
                        attention_inputs(b + 1, 1 - par)
                    pe.wait_ge(rem_ready, b * NP + NP)
                    for jb in range(NB):
                        for hf in range(NH):
                            q = jb * NH + hf
                            pe.wait_ge(both_read, b * NW + q + 1)
                            o = pboth[q % NM]
                            t.matmul(o[:], K["ident16"][:], rem[par][:, jb, hf * HALF:(hf + 1) * HALF], start=True, stop=False)
                            for e in range(HB):
                                nb = hf * HB + e
                                mm = t.matmul(o[:, e * P:(e + 1) * P], rem[par][:, nb, jb * P:(jb + 1) * P],
                                              K["ident16"][:], start=False, stop=(e == HB - 1))
                            mm.then_inc(both_ready, 1)
                            if not last:
                                attention(b + 1, 1 - par, q * SHARE, (q + 1) * SHARE)
                    pe.drain().then_inc(rem_free, 1)
                    if not last:
                        attention(b + 1, 1 - par, NW * SHARE, QB * 2 * NB)
                    pe.wait_ge(summed, b * (NB - 1) + (NB - 1))
                    for ib in range(NB):
                        mm = t.matmul(pdeg[:, ib:ib + 1], keptsum[:, ib * P:(ib + 1) * P], K["onescol"][:, 0:1],
                                      start=True, stop=True)
                    mm.then_inc(deg_ready, 1)
                ranks(0, 0)
                attention_inputs(0, 0)
                attention(0, 0, 0, QB * 2 * NB)
                per_pair(pe, B, body)

            @block.scalar
            def _(act):
                act.sem_inc(rank_read, NR)

                def distances(b):
                    cols = bass.ds(b * NB, NB)
                    nc.scalar.activation(test[:, 0, :], K["rscale"][:, cols], ACT.Copy)
                    nc.scalar.activation(test[:, 1, :], K["rbias"][:, cols], ACT.Copy)
                    act.drain()
                    for q, (nb, lo, hi) in enumerate(pieces):
                        act.wait_ge(rank_ready, b * NP + q + 1)
                        act.wait_ge(dist_read, b * NP + q + 1)
                        nc.scalar.activation(dist[q % NR][:, 0:hi - lo], prank[q % NR][:, 0:hi - lo], ACT.Abs,
                                             bias=test[:, 1, nb:nb + 1], scale=test[:, 0, nb:nb + 1]).then_inc(dist_ready, 1)
                        act.drain().then_inc(rank_read, 1)

                def x_tile(b):
                    return lambda t: K["X"][:, bass.ds(b * NB + t, 1)].rearrange("p o d -> p (o d)")

                def scores(b, par):
                    act.wait_ge(score_ready, b + 1)
                    nc.scalar.activation(G[par][:], sj[:, 0, :], ACT.Exp, bias=K["ac"][:, 0:1])
                    nc.scalar.activation(E[:], sj[:, 1, :], ACT.Exp, bias=K["ac"][:, 1:2]).then_inc(exp_ready, 1)

                def column_sums(b, par):
                    act.wait_ge(adj_loaded[par], (b - par) * (8 * NC) + 16 * NC)
                    for jb in range(NB):
                        nc.scalar.activation(colsink[:], adjT[par][:, jb, :], ACT.Copy,
                                             accum_out=K["colsum"][:, bass.ds(b * NB + jb, 1)])
                        act.drain()
                    act.sem_inc(col_summed, 1)

                def body(b, par, last):
                    two_ahead = not (isinstance(b, int) and b + 2 >= B)
                    if not last:
                        distances(b + 1)
                    if two_ahead:
                        norm_root(nc, act, K, x_tile(b + 2), w, b + 2, D)
                        norm_apply(nc, act, x_tile(b + 2), h[:], w, b + 2, h_ready)
                    if not last:
                        column_sums(b + 1, 1 - par)
                    if two_ahead:
                        scores(b + 2, par)
                for b in range(2):
                    norm_root(nc, act, K, x_tile(b), w, b, D)
                    norm_apply(nc, act, x_tile(b), h[:], w, b, h_ready)
                    scores(b, b)
                distances(0)
                column_sums(0, 0)
                per_pair(act, B, body)

            @block.vector
            def _(dve):
                v = nc.vector
                dve.sem_inc(dist_read, NR)
                dve.sem_inc(both_read, NM)
                dve.sem_inc(deg_read, 1)
                dve.sem_inc(bin_free, 1)
                dve.sem_inc(sums_read, NA)
                for buffer in rhs:
                    v.memset(buffer[:, :, D + 1:D + 2], 1.0)

                def score_sums(b):
                    dve.wait_ge(h_ready, b + 1)
                    for k in range(2):
                        v.tensor_tensor(t1[:], h[:], along_tiles(K["av"][:, k, :], NB), ALU.mult)
                        dve.drain()
                        last = v.tensor_reduce(sj[:, k, :], t1[:], AX, ALU.add)
                        if k == 0:
                            dve.drain()
                    last.then_inc(score_ready, 1)

                def right_hand_side(b, par):
                    dve.wait_ge(exp_ready, b + 1)
                    v.tensor_copy(rhs[par][:, :, D], E[:])
                    v.tensor_tensor(rhs[par][:, :, 0:D], h[:], along_features(E[:], D), ALU.mult).then_inc(rhs_ready, 1)

                def finish_attention(b, par, half):
                    for k in range(half * QB // 2, (half + 1) * QB // 2):
                        a = acc[k % NA]
                        xs = K["X"][:, bass.ds(b * NB + 2 * k, 2)]
                        dve.wait_ge(sums_ready, b * QB + k + 1)
                        v.tensor_copy(K["rowsum"][:, bass.ds(b * NB + 2 * k, 2)], a[:, :, D + 1])
                        gk = G[par][:, 2 * k:2 * k + 2]
                        v.tensor_tensor(q4[:, 0, :], a[:, :, D], gk, ALU.mult)
                        dve.drain()
                        v.reciprocal(q4[:, 1, :], q4[:, 0, :])
                        dve.drain()
                        v.tensor_tensor(q4[:, 2, :], q4[:, 1, :], gk, ALU.mult)
                        dve.drain()
                        v.tensor_tensor(y[:], a[:, :, 0:D], along_features(q4[:, 2, :], D), ALU.mult).then_inc(sums_read, 1)
                        dve.drain()
                        v.tensor_tensor(xs, xs, y[:], ALU.add)
                        dve.drain()

                def removals(b, par):
                    dve.wait_ge(loaded[par], (b - par) * (8 * n_loads) + 16 * n_loads)
                    dve.wait_ge(bin_loaded, b * (16 * NB) + 16 * NB)
                    for q, (nb, lo, hi) in enumerate(pieces):
                        dve.wait_ge(dist_ready, b * NP + q + 1)
                        col = bass.ds(b * NB + nb, 1)
                        v.scalar_tensor_tensor(rem[par][:, nb, lo:hi], dist[q % NR][:, 0:hi - lo], K["rdist"][:, col],
                                               rowbin[:, bin0[nb] + lo:bin0[nb] + hi], ALU.is_equal, ALU.mult).then_inc(rem_ready, 1)
                        dve.drain().then_inc(dist_read, 1)
                    dve.sem_inc(bin_free, 1)

                def body(b, par, last):
                    two_ahead = not (isinstance(b, int) and b + 2 >= B)
                    if two_ahead:
                        norm_mean(nc, dve, tiles(K["X"], b + 2, NB), w)
                    if not last:
                        removals(b + 1, 1 - par)
                    dve.wait_ge(col_summed, b + 1)
                    dve.wait_ge(adj_loaded[par], (b - par) * (8 * NC) + 16 * NC)
                    for jb in range(NB):
                        if two_ahead and jb == NB // 4:
                            norm_scale(nc, dve, w, b + 2)
                        for hf in range(NH):
                            q = jb * NH + hf
                            sl = slice(hf * HALF, (hf + 1) * HALF)
                            dve.wait_ge(both_ready, b * NW + q + 1)
                            v.scalar_tensor_tensor(adjT[par][:, jb, sl], pboth[q % NM][:], 0.5, adjT[par][:, jb, sl],
                                                   ALU.is_lt, ALU.mult).then_inc(masked, 1)
                            dve.drain().then_inc(both_read, 1)
                    if not last:
                        finish_attention(b + 1, 1 - par, 0)
                    if two_ahead:
                        score_sums(b + 2)
                    if not last:
                        finish_attention(b + 1, 1 - par, 1)
                    if two_ahead:
                        right_hand_side(b + 2, par)
                    cols = bass.ds(b * NB, NB)
                    dve.wait_ge(deg_ready, b + 1)
                    v.tensor_scalar(K["rdeg"][:, cols], pdeg[:], 1.0, None, ALU.max)
                    dve.drain().then_inc(deg_read, 1)
                    v.reciprocal(K["rdeg"][:, cols], K["rdeg"][:, cols])
                for b in range(2):
                    norm_mean(nc, dve, tiles(K["X"], b, NB), w)
                    norm_scale(nc, dve, w, b)
                    score_sums(b)
                    right_hand_side(b, b)
                    dve.drain()
                removals(0, 0)
                for half in range(2):
                    finish_attention(0, 0, half)
                per_pair(dve, B, body)


def sage_phase(nc, z, A, K, stream, layer):
    B, N, NB, NH, HB, D = z.B, z.N, z.NB, z.NH, z.HB, z.D
    first = layer == 0
    with Scope(nc, f"sage{layer}") as s:
        adjT = stream.buffers
        h = [s.sb(f"h{i}", [P, NB, D], F32) for i in range(2)]
        hT = s.sb("hT", [P, N], F32)
        aggT = s.sb("aggT", [P, N], F32)
        o = s.sb("o", [P, NB, D], F32)
        junk = s.sb("junk", [P, NB, D], F32)
        t1 = s.sb("t1", [P, NB, D], F32)
        nrm = s.sb("nrm", [P, 5, NB], F32)
        acc = s.sb("acc", [P, 2, NB, D], F32)
        rsq = s.sb("rsq", [P, NB, D], F32)
        tot = s.sb("tot", [P, 2, D], F32)
        mv = s.sb("mv", [P, 4, D], F32)
        onesf = s.sb("onesf", [P, P], F32)
        w = norm_buffers(s.sb, s.sem, "n", NB, D) if first else None
        agg = s.ps("agg", [P, N])
        tp = s.ps("tp", [P, N])
        o1 = s.ps("o1", [P, NB, D])
        o2 = s.ps("o2", [P, NB, D])
        sem = {n: s.sem(n) for n in (
            "adj_used", "issued", "h_ready", "tp_ready", "hT_ready", "agg_half", "aggT_half", "o1_ready", "o2_ready", "y_ready",
            "ones_ready", "passed", "y_read", "o_read", "out_ready", "w_ready", "len_ready", "r_ready", "tot_ready", "totals", "bn_var", "bn_std")}
        r = K["r"]
        with nc.Block() as block:
            @block.sync
            def _(sp):
                stream.sync_program(sp, sem["adj_used"], sem["issued"])

            @block.tensor
            def _(pe):
                t = nc.tensor

                def body(b, par, last):
                    pe.wait_ge(sem["h_ready"], b + 1)
                    for ib in range(NB):
                        mm = t.transpose(tp[:, ib * P:(ib + 1) * P], h[par][:, ib, :], K["ident"][:])
                    mm.then_inc(sem["tp_ready"], 1)
                    stream.wait_loaded(pe, b, par)
                    for hf in range(NH):
                        for jb in range(NB):
                            mm = t.matmul(agg[:, hf * HALF:(hf + 1) * HALF], h[par][:, jb, :],
                                          adjT[par][:, jb, hf * HALF:(hf + 1) * HALF], start=(jb == 0), stop=(jb == NB - 1))
                        mm.then_inc(sem["agg_half"], 1)
                    pe.drain().then_inc(sem["adj_used"], 1)
                    pe.wait_ge(sem["hT_ready"], b + 1)
                    pe.wait_ge(sem["o_read"], b + 1)
                    if not first:
                        for ib in range(NB):
                            mm = t.matmul(o1[:, ib, :], hT[:, ib * P:(ib + 1) * P], K["Wl"][:, layer - 1, :], start=True, stop=True)
                        mm.then_inc(sem["y_ready"], 1)
                    for ib in range(NB):
                        mm = t.matmul(o2[:, ib, :], hT[:, ib * P:(ib + 1) * P], K[f"Wx{layer}"][:], start=True, stop=True)
                    mm.then_inc(sem["o2_ready"], 1)
                    if not first:
                        pe.wait_ge(sem["y_read"], b + 1)
                    for hf in range(NH):
                        pe.wait_ge(sem["aggT_half"], b * NH + hf + 1)
                        for ib in range(hf * HB, (hf + 1) * HB):
                            mm = t.matmul(o1[:, ib, :], aggT[:, ib * P:(ib + 1) * P], K[f"Wr{layer}"][:], start=True, stop=True)
                    mm.then_inc(sem["o1_ready"], 1)
                per_pair(pe, B, body)
                pe.wait_ge(sem["ones_ready"], 1)
                pe.wait_ge(sem["tot_ready"], 1)
                t.matmul(o1[:, 0:2, :], onesf[:], tot[:], start=True, stop=True).then_inc(sem["totals"], 1)

            @block.scalar
            def _(act):
                def x_tile(b):
                    return lambda t: K["X"][:, bass.ds(b * NB + t, 1)].rearrange("p o d -> p (o d)")

                def body(b, par, last):
                    act.wait_ge(sem["tp_ready"], b + 1)
                    nc.scalar.activation(hT[:], tp[:], ACT.Copy).then_inc(sem["hT_ready"], 1)
                    if first and not last:
                        norm_apply(nc, act, x_tile(b + 1), h[1 - par][:], w, b + 1, sem["h_ready"])
                        if not (isinstance(b, int) and b + 2 >= B):
                            norm_root(nc, act, K, x_tile(b + 2), w, b + 2, D)
                    for hf in range(NH):
                        act.wait_ge(sem["agg_half"], b * NH + hf + 1)
                        sl = slice(hf * HALF, (hf + 1) * HALF)
                        nc.scalar.activation(aggT[:, sl], agg[:, sl], ACT.Copy).then_inc(sem["aggT_half"], 1)
                    act.drain()
                    act.wait_ge(sem["out_ready"], b + 1)
                    for ib in range(NB):
                        nc.scalar.activation(junk[:, ib, :], o[:, ib, :], ACT.Square, accum_out=nrm[:, 0, ib:ib + 1])
                    act.drain()
                    nc.scalar.activation(nrm[:, 1, :], nrm[:, 0, :], ACT.Sqrt).then_inc(sem["len_ready"], 1)
                    act.wait_ge(sem["w_ready"], b + 1)
                    act.sem_inc(sem["passed"], 1)
                    for ib in range(NB):
                        last_r = nc.scalar.activation(r[:, bass.ds(b * NB + ib, 1)].rearrange("p o d -> p (o d)"), o[:, ib, :],
                                                      ACT.Relu, scale=nrm[:, 4, ib:ib + 1])
                    last_r.then_inc(sem["r_ready"], 1)
                if first:
                    norm_root(nc, act, K, x_tile(0), w, 0, D)
                    norm_apply(nc, act, x_tile(0), h[0][:], w, 0, sem["h_ready"])
                    norm_root(nc, act, K, x_tile(1), w, 1, D)
                per_pair(act, B, body)
                act.wait_ge(sem["bn_var"], 1)
                nc.scalar.activation(mv[:, 2, :], mv[:, 1, :], ACT.Sqrt).then_inc(sem["bn_std"], 1)

            @block.gpsimd
            def _(pool):
                nc.gpsimd.memset(onesf[:], 1.0).then_inc(sem["ones_ready"], 1)

            @block.vector
            def _(dve):
                v = nc.vector
                dve.sem_inc(sem["o_read"], 1)
                v.memset(acc[:], 0.0)

                def prepare(b, par):
                    if first:
                        norm_mean(nc, dve, tiles(K["X"], b, NB), w)
                        norm_scale(nc, dve, w, b)
                    else:
                        v.tensor_tensor(t1[:], tiles(r, b, NB), along_tiles(K["bnscale"][:], NB), ALU.mult)
                        dve.drain()
                        v.tensor_tensor(h[par][:], t1[:], along_tiles(K["bnshift"][:], NB), ALU.add).then_inc(sem["h_ready"], 1)
                        dve.drain()

                def finish(b, par):
                    cols = bass.ds(b * NB, NB)
                    if not first:
                        dve.wait_ge(sem["y_ready"], b + 1)
                        v.tensor_tensor(t1[:], o1[:], along_features(K["mask2"][:, cols], D), ALU.mult).then_inc(sem["y_read"], 1)
                        dve.drain()
                        v.tensor_tensor(tiles(K["X"], b, NB), tiles(K["X"], b, NB), t1[:], ALU.add)
                        dve.drain()
                    dve.wait_ge(sem["o2_ready"], b + 1)
                    v.tensor_tensor(o[:], o2[:], along_tiles(K["vec"][:, V_B1 + layer, :], NB), ALU.add)
                    dve.wait_ge(sem["o1_ready"], b + 1)
                    v.tensor_tensor(t1[:], o1[:], along_features(K["rdeg"][:, cols], D), ALU.mult)
                    dve.drain().then_inc(sem["o_read"], 1)
                    v.tensor_tensor(o[:], o[:], t1[:], ALU.add).then_inc(sem["out_ready"], 1)
                    dve.wait_ge(sem["len_ready"], b + 1)
                    v.tensor_scalar(nrm[:, 2, :], nrm[:, 1, :], NORM_EPS, None, ALU.max)
                    dve.drain()
                    v.reciprocal(nrm[:, 3, :], nrm[:, 2, :])
                    dve.drain()
                    v.tensor_tensor(nrm[:, 4, :], nrm[:, 3, :], K["mask"][:, cols], ALU.mult).then_inc(sem["w_ready"], 1)

                def batch_sums(b):
                    rb = tiles(r, b, NB)
                    dve.wait_ge(sem["r_ready"], b + 1)
                    v.tensor_tensor(rsq[:], rb, rb, ALU.mult)
                    v.tensor_tensor(acc[:, 0], acc[:, 0], rb, ALU.add)
                    dve.drain()
                    v.tensor_tensor(acc[:, 1], acc[:, 1], rsq[:], ALU.add)
                    dve.drain()

                prepare(0, 0)
                if first:
                    prepare(1, 1)

                def body(b, par, last):
                    if first:
                        if not (isinstance(b, int) and b + 2 >= B):
                            prepare(b + 2, par)
                    elif not last:
                        prepare(b + 1, 1 - par)
                    finish(b, par)
                    batch_sums(b)
                per_pair(dve, B, body)
                for i in range(2):
                    last = v.tensor_reduce(tot[:, i, :], acc[:, i].rearrange("p t d -> p d t"), AX, ALU.add)
                last.then_inc(sem["tot_ready"], 1)
                dve.wait_ge(sem["totals"], 1)
                n_all = float(B * N)
                v.tensor_scalar(mv[:, 0, :], o1[:, 0, :], 1.0 / n_all, None, ALU.mult)
                v.tensor_scalar(mv[:, 1, :], o1[:, 1, :], 1.0 / n_all, None, ALU.mult)
                dve.drain()
                v.tensor_tensor(mv[:, 2, :], mv[:, 0, :], mv[:, 0, :], ALU.mult)
                dve.drain()
                v.tensor_tensor(mv[:, 1, :], mv[:, 1, :], mv[:, 2, :], ALU.subtract)
                dve.drain()
                v.tensor_scalar(mv[:, 1, :], mv[:, 1, :], BN_EPS, None, ALU.add).then_inc(sem["bn_var"], 1)
                dve.wait_ge(sem["bn_std"], 1)
                v.reciprocal(mv[:, 3, :], mv[:, 2, :])
                dve.drain()
                v.tensor_tensor(K["bnscale"][:], mv[:, 3, :], K["vec"][:, V_G1 + layer, :], ALU.mult)
                dve.drain()
                v.tensor_tensor(mv[:, 1, :], mv[:, 0, :], K["bnscale"][:], ALU.mult)
                dve.drain()
                v.tensor_tensor(K["bnshift"][:], K["vec"][:, V_E1 + layer, :], mv[:, 1, :], ALU.subtract)


def gcn_phase(nc, z, A, K, stream):
    B, N, NB, NH, HB, D = z.B, z.N, z.NB, z.NH, z.HB, z.D
    with Scope(nc, "gcn") as s:
        adjT = stream.buffers
        h = s.sb("h", [P, NB, D], F32)
        hT = s.sb("hT", [P, N], F32)
        h3 = s.sb("h3", [P, NB, D], F32)
        t1 = s.sb("t1", [P, NB, D], F32)
        t3 = s.sb("t3", [P, NB, D], F32)
        y = s.sb("y", [P, 4, D], F32)
        sup = [s.sb(f"sup{i}", [P, NB, D], F32) for i in range(2)]
        dinv = s.sb("dinv", [P, z.T], F32)
        dw = s.sb("dw", [P, 3, z.T], F32)
        w = norm_buffers(s.sb, s.sem, "n", NB, D)
        tp = s.ps("tp", [P, N])
        pr = [s.ps(f"pr{i}", [P, NB, D]) for i in range(2)]
        acc = [s.ps(f"acc{i}", [P, 4, D]) for i in range(2)]
        sem = {n: s.sem(n) for n in (
            "adj_used", "issued", "h3_ready", "h_ready", "tp_ready", "hT_ready", "pr_ready", "sup_ready", "sums_ready",
            "sums_read", "deg_ready", "dinv_ready", "bl_added", "bias_added", "passed")}
        QB = NB // 4
        assert QB == 2
        with nc.Block() as block:
            @block.sync
            def _(sp):
                stream.sync_program(sp, sem["adj_used"], sem["issued"])

            @block.tensor
            def _(pe):
                t = nc.tensor

                def turn(b, k):
                    pe.wait_ge(sem["h_ready" if k else "h3_ready"], b + 1)
                    for ib in range(NB):
                        mm = t.transpose(tp[:, ib * P:(ib + 1) * P], (h if k else h3)[:, ib, :], K["ident"][:])
                    mm.then_inc(sem["tp_ready"], 1)

                def project(b, k):
                    pe.wait_ge(sem["hT_ready"], b * 2 + k + 1)
                    for ib in range(NB):
                        mm = t.matmul(pr[k][:, ib, :], hT[:, ib * P:(ib + 1) * P], K["W2"][:] if k else K["Wl"][:, 2, :],
                                      start=True, stop=True)
                    mm.then_inc(sem["pr_ready"], 1)

                def sums(par, ibs):
                    for ib in ibs:
                        for jb in range(NB):
                            mm = t.matmul(acc[ib // 4][:, ib % 4, :], adjT[par][:, jb, ib * P:(ib + 1) * P],
                                          sup[par][:, jb, :], start=(jb == 0), stop=(jb == NB - 1))
                    return mm

                for k in range(2):
                    turn(0, k)
                    project(0, k)
                turn(1, 0)

                def body(b, par, last):
                    if not last:
                        project(b + 1, 0)
                    pe.wait_ge(sem["sup_ready"], b + 1)
                    stream.wait_loaded(pe, b, par)
                    pe.wait_ge(sem["sums_read"], b * QB + 1)
                    sums(par, range(0, 4)).then_inc(sem["sums_ready"], 1)
                    pe.wait_ge(sem["sums_read"], b * QB + 2)
                    sums(par, range(4, 6))
                    if not last:
                        turn(b + 1, 1)
                    sums(par, range(6, 8)).then_inc(sem["sums_ready"], 1)
                    pe.drain().then_inc(sem["adj_used"], 1)
                    if not last:
                        project(b + 1, 1)
                        if not (isinstance(b, int) and b + 2 >= B):
                            turn(b + 2, 0)
                per_pair(pe, B, body)

            @block.scalar
            def _(act):
                act.wait_ge(sem["deg_ready"], 1)
                nc.scalar.activation(dinv[:], dw[:, 1, :], ACT.Sqrt).then_inc(sem["dinv_ready"], 1)

                def prepare(b):
                    act.wait_ge(sem["tp_ready"], b * 2 + 1)
                    nc.scalar.activation(hT[:], tp[:], ACT.Copy).then_inc(sem["hT_ready"], 1)
                    def x(t):
                        return K["X"][:, bass.ds(b * NB + t, 1)].rearrange("p o d -> p (o d)")
                    norm_root(nc, act, K, x, w, b, D)
                    norm_apply(nc, act, x, h[:], w, b, sem["h_ready"])
                    act.wait_ge(sem["tp_ready"], b * 2 + 2)
                    nc.scalar.activation(hT[:], tp[:], ACT.Copy).then_inc(sem["hT_ready"], 1)

                def body(b, par, last):
                    if not last:
                        prepare(b + 1)
                prepare(0)
                per_pair(act, B, body)

            @block.gpsimd
            def _(pool):
                g = nc.gpsimd

                def prepare(b):
                    x = tiles(K["X"], b, NB)
                    cols = bass.ds(b * NB, NB)
                    g.tensor_tensor(t3[:], tiles(K["r"], b, NB), along_tiles(K["bnscale"][:], NB), ALU.mult)
                    pool.drain()
                    g.tensor_tensor(h3[:], t3[:], along_tiles(K["bnshift"][:], NB), ALU.add)
                    pool.drain().then_inc(sem["h3_ready"], 1)
                    g.tensor_tensor(t3[:], along_tiles(K["vec"][:, V_BL, :], NB), along_features(K["mask"][:, cols], D), ALU.mult)
                    pool.drain()
                    g.tensor_tensor(x, x, t3[:], ALU.add)
                    pool.drain().then_inc(sem["bl_added"], 1)

                prepare(0)

                def body(b, par, last):
                    if not last:
                        pool.wait_ge(sem["tp_ready"], b * 2 + 1)
                        pool.sem_inc(sem["passed"], 1)
                        prepare(b + 1)
                    pool.wait_ge(sem["h_ready"], b + 1)
                    pool.sem_inc(sem["passed"], 1)
                    x = tiles(K["X"], b, NB)
                    g.tensor_tensor(x, x, along_tiles(K["vec"][:, V_BIAS2, :], NB), ALU.add)
                    pool.drain().then_inc(sem["bias_added"], 1)
                per_pair(pool, B, body)

            @block.vector
            def _(dve):
                v = nc.vector
                dve.sem_inc(sem["sums_read"], 2)
                v.tensor_scalar(dw[:, 0, :], K["rowsum"][:], 1.0, None, ALU.add)
                dve.drain()
                v.tensor_scalar(dw[:, 2, :], dw[:, 0, :], 0.0, None, ALU.is_equal)
                dve.drain()
                v.tensor_tensor(dw[:, 0, :], dw[:, 0, :], dw[:, 2, :], ALU.add)
                dve.drain()
                v.reciprocal(dw[:, 1, :], dw[:, 0, :]).then_inc(sem["deg_ready"], 1)
                v.tensor_scalar(dw[:, 2, :], dw[:, 2, :], -1.0, 1.0, ALU.mult, ALU.add)
                dve.wait_ge(sem["dinv_ready"], 1)
                dve.drain()
                v.tensor_tensor(dinv[:], dinv[:], dw[:, 2, :], ALU.mult)
                dve.drain()

                def normalise(b):
                    x = tiles(K["X"], b, NB)
                    cols = bass.ds(b * NB, NB)
                    dve.wait_ge(sem["pr_ready"], b * 2 + 1)
                    v.tensor_tensor(t1[:], pr[0][:], along_features(K["mask2"][:, cols], D), ALU.mult)
                    dve.drain()
                    dve.wait_ge(sem["bl_added"], b + 1)
                    v.tensor_tensor(x, x, t1[:], ALU.add)
                    dve.drain()
                    norm_mean(nc, dve, x, w)
                    norm_scale(nc, dve, w, b)

                def support(b, par):
                    dve.wait_ge(sem["pr_ready"], b * 2 + 2)
                    v.tensor_tensor(sup[par][:], pr[1][:], along_features(dinv[:, bass.ds(b * NB, NB)], D), ALU.mult)
                    dve.drain().then_inc(sem["sup_ready"], 1)

                def finish(b, par):
                    for k in range(QB):
                        dve.wait_ge(sem["sums_ready"], b * QB + k + 1)
                        cols = bass.ds(b * NB + 4 * k, 4)
                        xs = K["X"][:, cols]
                        v.tensor_tensor(y[:], acc[k][:], sup[par][:, 4 * k:4 * k + 4, :], ALU.add)
                        dve.drain().then_inc(sem["sums_read"], 1)
                        v.tensor_tensor(y[:], y[:], along_features(dinv[:, cols], D), ALU.mult)
                        dve.drain()
                        if k == 0:
                            dve.wait_ge(sem["bias_added"], b + 1)
                        v.tensor_tensor(xs, xs, y[:], ALU.add)
                        dve.drain()

                normalise(0)
                support(0, 0)

                def body(b, par, last):
                    if not last:
                        normalise(b + 1)
                    finish(b, par)
                    if not last:
                        support(b + 1, 1 - par)
                per_pair(dve, B, body)


def maxdeg_phase(nc, z, A, K, scratch, out):
    B, N, NB, NH, HB, D = z.B, z.N, z.NB, z.NH, z.HB, z.D
    with Scope(nc, "l3") as s:
        rowbin = [s.sb(f"rowbin{i}", [P, NB, N], BF16) for i in range(2)]
        h = s.sb("h", [P, NB, D], F32)
        rest = s.sb("rest", [P, NB, D], F32)
        parts = [s.sb(f"parts{i}", [P, 3, NB, D], BF16) for i in range(2)]
        aggT = s.sb("aggT", [P, N], F32)
        y = s.sb("y", [P, NB, D], F32)
        res = [s.sb(f"res{i}", [P, NB, D], F32) for i in range(2)]
        rcol = s.sb("rcol", [P, z.T], F32)
        w = norm_buffers(s.sb, s.sem, "n", NB, D)
        agg = [s.ps(f"agg{i}", [P, N]) for i in range(2)]
        pr = s.ps("pr", [P, NB, D])
        sem = {n: s.sem(n) for n in (
            "in_used", "issued", "normalised", "h_ready", "agg_half", "aggT_half", "pr_ready", "pr_read", "res_ready", "res_free", "stored")}
        loaded = [s.sem(f"loaded{i}") for i in range(2)]
        with nc.Block() as block:
            @block.sync
            def _(sp):
                def body(b, par, last):
                    sp.wait_ge(sem["in_used"], b + 1)
                    sp.sem_inc(sem["issued"], 1)
                    sp.dma_start(rowbin[par][:], graph(scratch["rowbin"], b)).then_inc(loaded[par], 16)
                per_pair(sp, B, body)

            @block.gpsimd
            def _(pool):
                pool.sem_inc(sem["res_free"], 2)

                def body(b, par, last):
                    pool.wait_ge(sem["res_ready"], b + 1)
                    pool.dma_start(graph(out, b), res[par][:]).then_inc(sem["stored"], 16)
                    pool.wait_ge(sem["stored"], b * 16 + 16)
                    pool.sem_inc(sem["res_free"], 1)
                per_pair(pool, B, body)

            @block.tensor
            def _(pe):
                t = nc.tensor
                pe.sem_inc(sem["in_used"], 2)

                def body(b, par, last):
                    pe.wait_ge(sem["h_ready"], b + 1)
                    pe.wait_ge(loaded[par], (b - par) * 8 + 16)
                    for hf in range(NH):
                        sl = slice(hf * HALF, (hf + 1) * HALF)
                        for jb in range(NB):
                            for q in range(3):
                                mm = t.matmul(agg[par][:, sl], parts[par][:, q, jb, :], rowbin[par][:, jb, sl],
                                              start=(jb == 0 and q == 0), stop=(jb == NB - 1 and q == 2))
                        mm.then_inc(sem["agg_half"], 1)
                    pe.drain().then_inc(sem["in_used"], 1)
                    pe.wait_ge(sem["pr_read"], b + 1)
                    for hf in range(NH):
                        pe.wait_ge(sem["aggT_half"], b * NH + hf + 1)
                        for ib in range(hf * HB, (hf + 1) * HB):
                            mm = t.matmul(pr[:, ib, :], aggT[:, ib * P:(ib + 1) * P], K["U"][:], start=True, stop=True)
                    mm.then_inc(sem["pr_ready"], 1)
                per_pair(pe, B, body)

            @block.scalar
            def _(act):
                def x_tile(b):
                    return lambda t: K["X"][:, bass.ds(b * NB + t, 1)].rearrange("p o d -> p (o d)")

                for b in range(2):
                    norm_root(nc, act, K, x_tile(b), w, b, D)
                    norm_apply(nc, act, x_tile(b), h[:], w, b, sem["normalised"])

                def body(b, par, last):
                    for hf in range(NH):
                        act.wait_ge(sem["agg_half"], b * NH + hf + 1)
                        sl = slice(hf * HALF, (hf + 1) * HALF)
                        act.wait_ge(sem["pr_read"], b + 1)
                        nc.scalar.activation(aggT[:, sl], agg[par][:, sl], ACT.Copy).then_inc(sem["aggT_half"], 1)
                    if not (isinstance(b, int) and b + 2 >= B):
                        norm_root(nc, act, K, x_tile(b + 2), w, b + 2, D)
                        norm_apply(nc, act, x_tile(b + 2), h[:], w, b + 2, sem["normalised"])
                per_pair(act, B, body)

            @block.vector
            def _(dve):
                v = nc.vector
                dve.sem_inc(sem["pr_read"], 1)
                v.reciprocal(rcol[:], K["colsum"][:])

                def split(b, par):
                    pt = parts[par]
                    dve.wait_ge(sem["normalised"], b + 1)
                    v.tensor_copy(pt[:, 0], h[:])
                    dve.drain()
                    v.tensor_tensor(rest[:], h[:], pt[:, 0], ALU.subtract)
                    dve.drain()
                    v.tensor_copy(pt[:, 1], rest[:])
                    dve.drain()
                    v.tensor_tensor(pt[:, 2], rest[:], pt[:, 1], ALU.subtract).then_inc(sem["h_ready"], 1)
                    dve.drain()

                def finish(b, par):
                    cols = bass.ds(b * NB, NB)
                    dve.wait_ge(sem["pr_ready"], b + 1)
                    v.tensor_tensor(y[:], pr[:], along_features(rcol[:, cols], D), ALU.mult)
                    dve.drain().then_inc(sem["pr_read"], 1)
                    dve.wait_ge(sem["res_free"], b + 1)
                    v.scalar_tensor_tensor(res[par][:], y[:], 0.0, tiles(K["X"], b, NB), ALU.max, ALU.add)\
                        .then_inc(sem["res_ready"], 1)
                    dve.drain()

                norm_mean(nc, dve, tiles(K["X"], 0, NB), w)
                norm_scale(nc, dve, w, 0)
                split(0, 0)
                norm_mean(nc, dve, tiles(K["X"], 1, NB), w)
                norm_scale(nc, dve, w, 1)

                def body(b, par, last):
                    if not last:
                        split(b + 1, 1 - par)
                    two_ahead = not (isinstance(b, int) and b + 2 >= B)
                    if two_ahead:
                        norm_mean(nc, dve, tiles(K["X"], b + 2, NB), w)
                    finish(b, par)
                    if two_ahead:
                        norm_scale(nc, dve, w, b + 2)
                per_pair(dve, B, body)


def build_program(nc, A, out):
    z = Shapes(A["x"], A["adj_rows"])
    B, N, D, T = z.B, z.N, z.D, z.T
    scratch = {"rowbin": nc.dram_tensor("rowbin", (B, N, N), BF16, kind="Internal").ap(),
               "rem": nc.dram_tensor("rem", (B, N, N), BF16, kind="Internal").ap(),
               "curT": nc.dram_tensor("curT", (B, N, N), BF16, kind="Internal").ap(),
               "keptT": nc.dram_tensor("keptT", (B, N, N), F32, kind="Internal").ap()}
    with ExitStack() as ctx:
        K = {}

        def resident(name, shape, dt=F32):
            K[name] = ctx.enter_context(nc.sbuf_tensor(f"k_{name}", shape, dt))
        resident("X", [P, T, D])
        for n in ("Wr0", "Wr1", "Wr2", "Wx0", "Wx1", "Wx2", "W2", "U", "ident"):
            resident(n, [P, P])
        resident("Wl", [P, 3, D])
        resident("vec", [P, NVEC, D])
        resident("av", [P, 2, D])
        resident("ac", [P, 3])
        resident("onescol", [P, 2])
        resident("eps", [P, 1])
        for n in ("mask", "mask2", "maskok", "rowsum", "colsum", "rdeg", "rscale", "rbias", "rdist"):
            resident(n, [P, T])
        resident("bnscale", [P, D])
        resident("bnshift", [P, D])
        resident("ident16", [P, P], BF16)
        resident("ones16", [P, 2], BF16)
        resident("upper", [P, P], BF16)
        resident("tri", [P, N], BF16)
        constants_phase(nc, z, A, K)
        removal_phase(nc, z, A, K, scratch)
        keep_attention_phase(nc, z, A, K, scratch)
        resident("r", [P, T, D])
        with Scope(nc, "stream") as s:
            stream = GraphStream(z, s.sb, s.sem, [scratch["keptT"]] * 3 + [A["adj_cols"]])
            for layer in range(3):
                sage_phase(nc, z, A, K, stream, layer)
                stream.stage += 1
            gcn_phase(nc, z, A, K, stream)
        maxdeg_phase(nc, z, A, K, scratch, out)


_VECTORS = ["L0_gnn_W_w", "L0_gnn_W_b", "L0_gnn_a_w", "L0_gnn_a_b", "L1_gnn_Wr1", "L1_gnn_Wx1", "L1_gnn_b1", "L1_gnn_g1",
            "L1_gnn_be1", "L1_gnn_Wr2", "L1_gnn_Wx2", "L1_gnn_b2", "L1_gnn_g2", "L1_gnn_be2", "L1_gnn_Wr3", "L1_gnn_Wx3",
            "L1_gnn_b3", "L1_gnn_g3", "L1_gnn_be3", "L1_gnn_Wl", "L1_gnn_bl", "L2_gnn_weight", "L2_gnn_bias", "L3_gnn_U"]


def kernel(**inputs):
    import numpy as _np
    import concourse.bacc as _bacc
    from concourse import mybir as _mybir
    from concourse.bass_utils import run_bass_kernel_spmd as _run

    nc = _bacc.Bacc("TRN2", target_bir_lowering=False, num_devices=1)
    arrays = {"x": _np.ascontiguousarray(inputs["x"]), "nodemask": _np.ascontiguousarray(inputs["nodemask"]),
              "adj_rows": _np.ascontiguousarray(inputs["adj"]),
              "adj_cols": _np.ascontiguousarray(_np.asarray(inputs["adj"]).transpose(0, 2, 1))}
    for name in _VECTORS:
        arrays[name] = _np.ascontiguousarray(inputs[name])
        if arrays[name].ndim == 0:
            arrays[name] = arrays[name].reshape(1)
    A, feed = {}, {}
    for name, a in arrays.items():
        A[name] = nc.dram_tensor(f"in_{name}", a.shape, _mybir.dt.from_np(a.dtype), kind="ExternalInput").ap()
        feed[f"in_{name}"] = a
    out = nc.dram_tensor("out_x", arrays["x"].shape, F32, kind="ExternalOutput").ap()
    build_program(nc, A, out)
    r = _run(nc, [feed], core_ids=[0])
    return r.results[0]["out_x"]
```
